# Optimizing a Trainium2 kernel written in Bass

```python
import numpy as np
import jax
import jax.numpy as jnp

def _softmax(x, axis=-1):
    return jax.nn.softmax(x, axis=axis)

def _gelu(x):
    return jax.nn.gelu(x, approximate=True)

def _silu(x):
    return jax.nn.silu(x)

def _sigmoid(x):
    return jax.nn.sigmoid(x)

def _layernorm(x, axis=-1, eps=1e-05):
    m = jnp.mean(x, axis=axis, keepdims=True)
    v = jnp.var(x, axis=axis, keepdims=True)
    return (x - m) / jnp.sqrt(v + eps)

def _scatter_add(tgt, idx, src, axis=0):
    return tgt.at[idx].add(src)

def _segment_sum(src, seg, n):
    return jax.ops.segment_sum(src, seg, n)
kernel_name = 'mk_decoder_postln_d2_seqx_r8_857a95'

def setup_inputs(seed: int=0):
    np.random.seed(seed)
    _w = jnp.asarray

    def _rec_inputs():
        import jax
        import jax.numpy as jnp
        _rk = jax.random.key(seed)
        x = -0.0005207 + 1.001 * jax.random.normal(jax.random.fold_in(_rk, 1), (32, 128, 128), jnp.float32)
        _lenS = 128 - jax.random.randint(jax.random.fold_in(_rk, 7), (32,), 0, max(1, 128 // 4) + 1, jnp.int32)
        _lenS2 = 77 - jax.random.randint(jax.random.fold_in(_rk, 8), (32,), 0, max(1, 77 // 4) + 1, jnp.int32)
        _ctx_1024P = jax.random.normal(jax.random.fold_in(_rk, 11), (32, 16, 128), jnp.float32)
        _ctx_1024c = jax.random.dirichlet(jax.random.fold_in(_rk, 511), 0.3 * jnp.ones((16,), jnp.float32), (32, 77))
        _ctx_1024t = jnp.einsum('bsk,bkd->bsd', _ctx_1024c, _ctx_1024P)
        _ctx_1024t = _ctx_1024t * jax.lax.rsqrt(jnp.mean(jnp.square(_ctx_1024t)) + 1e-12) * 0.953939
        ctx_1024 = -0.000514642 + 1.00011 * (_ctx_1024t + 0.3 * jax.random.normal(jax.random.fold_in(_rk, 611), (32, 77, 128), jnp.float32))
        return (x, ctx_1024)
    x, ctx_1024 = _rec_inputs()

    def _L0_attn_setup():
        import jax, jax.numpy as jnp
        import numpy as np
        DIM = 128
        HID = 256
        L = 4
        DI = int(HID * 1.5)
        B, T = (4, 256)

        def rmsnorm(x, gamma, dim):
            n = jnp.sqrt(jnp.sum(x * x, axis=-1, keepdims=True))
            return x / jnp.maximum(n, 1e-12) * dim ** 0.5 * (gamma + 1.0)

        def log_g(x):
            return jnp.where(x >= 0, jnp.log(jax.nn.relu(x) + 0.5), -jax.nn.softplus(-x))

        def heinsen_scan_log(log_coeffs, log_values):
            a_star = jnp.cumsum(log_coeffs, axis=1)
            log_h = a_star + jax.lax.cumlogsumexp(log_values - a_star, axis=1)
            return jnp.exp(log_h)
        key = jax.random.key(seed)
        ks = jax.random.split(key, 9)
        s = 0.02
        return {'x': jax.random.normal(ks[0], (B, T, DIM), jnp.float32), 'Wp': jax.random.normal(ks[1], (DIM, HID), jnp.float32) * s, 'bp': jnp.zeros((HID,), jnp.float32), 'g1': jax.random.normal(ks[2], (L, HID), jnp.float32) * s, 'Whg': jax.random.normal(ks[3], (L, HID, 2 * DI), jnp.float32) * s, 'bhg': jnp.zeros((L, 2 * DI), jnp.float32), 'Wo': jax.random.normal(ks[4], (L, DI, HID), jnp.float32) * s, 'bo': jnp.zeros((L, HID), jnp.float32), 'g2': jax.random.normal(ks[5], (L, HID), jnp.float32) * s, 'gf': jax.random.normal(ks[6], (HID,), jnp.float32) * s, 'Wf': jax.random.normal(ks[7], (HID, DIM), jnp.float32) * s, 'bf': jnp.zeros((DIM,), jnp.float32)}
    _L0_attn_all = _L0_attn_setup()
    _L0_attn_in = {k: v for k, v in _L0_attn_all.items() if k in ('Wp', 'bp', 'g1', 'Whg', 'bhg', 'Wo', 'bo', 'g2', 'gf', 'Wf', 'bf')}
    del _L0_attn_all

    def _L0_xattn_setup():
        import jax, jax.numpy as jnp
        import numpy as np
        import math
        B, S, D, H = (1, 256, 128, 16)
        DK = D // H
        DH = 64
        LOG_T_MIN = math.log(0.1)
        LOG_T_MAX = math.log(10.0)

        def _linear(x, W, b):
            return x @ W.T + b
        key = jax.random.key(seed)
        ks = jax.random.split(key, 20)
        p = 0.02
        return {'query': jax.random.normal(ks[0], (B, S, D), jnp.float32), 'key': jax.random.normal(ks[1], (B, S, D), jnp.float32), 'value': jax.random.normal(ks[2], (B, S, D), jnp.float32), 'Wq': jax.random.normal(ks[3], (D, D), jnp.float32) * p, 'bq': jax.random.normal(ks[4], (D,), jnp.float32) * p, 'Wk': jax.random.normal(ks[5], (D, D), jnp.float32) * p, 'bk': jax.random.normal(ks[6], (D,), jnp.float32) * p, 'Wv': jax.random.normal(ks[7], (D, D), jnp.float32) * p, 'bv': jax.random.normal(ks[8], (D,), jnp.float32) * p, 'Wo': jax.random.normal(ks[9], (D, D), jnp.float32) * p, 'bo': jax.random.normal(ks[10], (D,), jnp.float32) * p, 'w1': jax.random.normal(ks[11], (DH, 3), jnp.float32) * 0.3, 'b1': jax.random.normal(ks[12], (DH,), jnp.float32) * 0.1, 'w2': jax.random.normal(ks[13], (DH, DH), jnp.float32) * 0.1, 'b2': jax.random.normal(ks[14], (DH,), jnp.float32) * 0.1, 'w3': jax.random.normal(ks[15], (1, DH), jnp.float32) * 0.1, 'b3': jnp.full((1,), (LOG_T_MIN + LOG_T_MAX) / 2, jnp.float32)}
    _L0_xattn_all = _L0_xattn_setup()
    _L0_xattn_in = {k: v for k, v in _L0_xattn_all.items() if k in ('Wq', 'bq', 'Wk', 'bk', 'Wv', 'bv', 'Wo', 'bo', 'w1', 'b1', 'w2', 'b2', 'w3', 'b3')}
    del _L0_xattn_all

    def _L0_ffn_setup():
        import jax, jax.numpy as jnp
        import numpy as np
        D_MODEL = 128
        NUM_TILES = 64
        TPC = 8
        NUM_CLUSTERS = NUM_TILES // TPC
        GRID = 16
        COMP_H = 32
        NUM_KNOTS = 8
        EPS_LN = 1e-05

        def _calibrate(scores, knots, temperature):
            K = knots.shape[0]
            normalized = jax.nn.sigmoid(scores / (temperature[0] + 1e-06))
            idx_float = normalized * (K - 1)
            idx_low = jnp.clip(idx_float.astype(jnp.int32), 0, K - 2)
            idx_high = idx_low + 1
            t = idx_float - idx_low.astype(scores.dtype)
            val_low = knots[idx_low]
            val_high = knots[idx_high]
            return val_low + t * (val_high - val_low)

        def _forward(x, signatures_raw, knot_values, temperature, compress_w1, compress_b1, compress_w2, compress_b2, spline_w1, spline_b1, spline_w2, spline_b2, directions, norm_gamma, norm_beta, output_scale):
            B, T, D = x.shape
            xf = x.reshape(-1, D)
            q = jnp.where(signatures_raw > 0.3, 1.0, jnp.where(signatures_raw < -0.3, -1.0, 0.0)).astype(signatures_raw.dtype)
            sigs = signatures_raw + jax.lax.stop_gradient(q - signatures_raw)
            cluster_sigs = jnp.sign(sigs.reshape(NUM_CLUSTERS, TPC, D).mean(axis=1))
            cluster_scores = xf @ cluster_sigs.T
            cluster_gates = _calibrate(cluster_scores, knot_values, temperature)
            cluster_idx = jnp.argmax(cluster_gates, axis=-1)
            tile_scores = xf @ sigs.T
            tile_gates = _calibrate(tile_scores, knot_values, temperature)
            gates_by_cluster = tile_gates.reshape(-1, NUM_CLUSTERS, TPC)
            sel_gates = jnp.take_along_axis(gates_by_cluster, cluster_idx[:, None, None], axis=1)[:, 0, :]
            local_idx = jnp.argmax(sel_gates, axis=-1)
            tile_idx = cluster_idx * TPC + local_idx
            h = jax.nn.gelu(xf @ compress_w1 + compress_b1, approximate=False)
            comp = jnp.tanh(h @ compress_w2 + compress_b2)
            w1 = spline_w1[tile_idx]
            b1 = spline_b1[tile_idx]
            hh = jax.nn.relu(jnp.einsum('ni,nig->ng', comp, w1) + b1)
            w2 = spline_w2[tile_idx]
            b2 = spline_b2[tile_idx]
            mag = jnp.einsum('ng,ngo->no', hh, w2) + b2
            ffn_out = mag * directions[tile_idx] * output_scale[0]
            y = xf + ffn_out
            mu = y.mean(axis=-1, keepdims=True)
            var = ((y - mu) ** 2).mean(axis=-1, keepdims=True)
            y = (y - mu) / jnp.sqrt(var + EPS_LN) * norm_gamma + norm_beta
            return y.reshape(B, T, D)
        key = jax.random.key(seed)
        ks = jax.random.split(key, 12)
        B, T = (4, 512)
        x = jax.random.normal(ks[0], (B, T, D_MODEL), dtype=jnp.float32)
        signatures_raw = jax.random.normal(ks[1], (NUM_TILES, D_MODEL), dtype=jnp.float32) * 0.5
        knot_values = jax.nn.sigmoid(jnp.linspace(-3.0, 3.0, NUM_KNOTS).astype(jnp.float32))
        temperature = jnp.ones((1,), dtype=jnp.float32)
        compress_w1 = jax.random.normal(ks[2], (D_MODEL, COMP_H), dtype=jnp.float32) * (1.0 / np.sqrt(D_MODEL))
        compress_b1 = jnp.zeros((COMP_H,), dtype=jnp.float32)
        compress_w2 = jax.random.normal(ks[3], (COMP_H, 2), dtype=jnp.float32) * (1.0 / np.sqrt(COMP_H))
        compress_b2 = jnp.zeros((2,), dtype=jnp.float32)
        spline_w1 = jax.random.normal(ks[4], (NUM_TILES, 2, GRID), dtype=jnp.float32) * (1.0 / np.sqrt(2.0))
        spline_b1 = jnp.zeros((NUM_TILES, GRID), dtype=jnp.float32)
        spline_w2 = jax.random.normal(ks[5], (NUM_TILES, GRID, 1), dtype=jnp.float32) * (1.0 / np.sqrt(GRID))
        spline_b2 = jnp.zeros((NUM_TILES, 1), dtype=jnp.float32)
        directions = jax.random.normal(ks[6], (NUM_TILES, D_MODEL), dtype=jnp.float32) * 0.02
        norm_gamma = jnp.ones((D_MODEL,), dtype=jnp.float32)
        norm_beta = jnp.zeros((D_MODEL,), dtype=jnp.float32)
        output_scale = jnp.ones((1,), dtype=jnp.float32) * 0.1
        return dict(x=x, signatures_raw=signatures_raw, knot_values=knot_values, temperature=temperature, compress_w1=compress_w1, compress_b1=compress_b1, compress_w2=compress_w2, compress_b2=compress_b2, spline_w1=spline_w1, spline_b1=spline_b1, spline_w2=spline_w2, spline_b2=spline_b2, directions=directions, norm_gamma=norm_gamma, norm_beta=norm_beta, output_scale=output_scale)
    _L0_ffn_all = _L0_ffn_setup()
    _L0_ffn_in = {k: v for k, v in _L0_ffn_all.items() if k in ('signatures_raw', 'knot_values', 'temperature', 'compress_w1', 'compress_b1', 'compress_w2', 'compress_b2', 'spline_w1', 'spline_b1', 'spline_w2', 'spline_b2', 'directions', 'norm_gamma', 'norm_beta', 'output_scale')}
    del _L0_ffn_all

    def _L1_attn_setup():
        import jax, jax.numpy as jnp
        import numpy as np
        H, HD, D = (16, 64, 128)
        SCALE = HD ** (-0.5)
        TEMP = 1.0
        EPS = 1e-05
        key = jax.random.key(seed)
        ks = jax.random.split(key, 10)
        B, N = (2, 256)
        lim = 1.0 / np.sqrt(D)

        def lin(k, out_d, in_d):
            k1, k2 = jax.random.split(k)
            W = jax.random.uniform(k1, (out_d, in_d), jnp.float32, -lim, lim)
            b = jax.random.uniform(k2, (out_d,), jnp.float32, -lim, lim)
            return (W, b)
        Wq, bq = lin(ks[0], H * HD, D)
        Wk, bk = lin(ks[1], H * HD, D)
        Wv, bv = lin(ks[2], H * HD, D)
        Wo, bo = lin(ks[3], D, H * HD)
        return {'x': jax.random.normal(ks[4], (B, N, D), jnp.float32), 'adaptive_scale': jnp.ones((H,), jnp.float32), 'Wq': Wq, 'bq': bq, 'Wk': Wk, 'bk': bk, 'Wv': Wv, 'bv': bv, 'Wo': Wo, 'bo': bo, 'gamma': jnp.ones((D,), jnp.float32), 'beta': jnp.zeros((D,), jnp.float32)}
    _L1_attn_all = _L1_attn_setup()
    _L1_attn_in = {k: v for k, v in _L1_attn_all.items() if k in ('adaptive_scale', 'Wq', 'bq', 'Wk', 'bk', 'Wv', 'bv', 'Wo', 'bo', 'gamma', 'beta')}
    del _L1_attn_all

    def _L1_xattn_setup():
        import jax, jax.numpy as jnp
        import numpy as np
        NUM_HEADS = 16
        D_MODEL = 128
        D_K = D_MODEL // NUM_HEADS

        def _split_heads(x):
            B, S, _ = x.shape
            return x.reshape(B, S, NUM_HEADS, D_K).transpose(0, 2, 1, 3)
        key = jax.random.key(seed)
        ks = jax.random.split(key, 11)
        B, S, D = (1, 512, D_MODEL)
        scale = 1.0 / np.sqrt(D)
        return {'Q': jax.random.normal(ks[0], (B, S, D), jnp.float32), 'K': jax.random.normal(ks[1], (B, S, D), jnp.float32), 'V': jax.random.normal(ks[2], (B, S, D), jnp.float32), 'W_Q': jax.random.normal(ks[3], (D, D), jnp.float32) * scale, 'b_Q': jax.random.normal(ks[4], (D,), jnp.float32) * 0.02, 'W_K': jax.random.normal(ks[5], (D, D), jnp.float32) * scale, 'b_K': jax.random.normal(ks[6], (D,), jnp.float32) * 0.02, 'W_V': jax.random.normal(ks[7], (D, D), jnp.float32) * scale, 'b_V': jax.random.normal(ks[8], (D,), jnp.float32) * 0.02, 'W_O': jax.random.normal(ks[9], (D, D), jnp.float32) * scale, 'b_O': jax.random.normal(ks[10], (D,), jnp.float32) * 0.02}
    _L1_xattn_all = _L1_xattn_setup()
    _L1_xattn_in = {k: v for k, v in _L1_xattn_all.items() if k in ('W_Q', 'b_Q', 'W_K', 'b_K', 'W_V', 'b_V', 'W_O', 'b_O')}
    del _L1_xattn_all

    def _L1_ffn_setup():
        import jax, jax.numpy as jnp
        import numpy as np
        EXPERT_NUM = 8
        CAPACITY = 100
        key = jax.random.key(seed)
        k1, k2, k3 = jax.random.split(key, 3)
        B, S, H, E = (8, 256, 128, EXPERT_NUM)
        x = jax.random.normal(k1, (B, S, H), dtype=jnp.float32)
        w_gate = jax.random.normal(k2, (H, E), dtype=jnp.float32) * 0.02
        w_expert = jax.random.normal(k3, (H, H), dtype=jnp.float32) * 0.02
        b_expert = jnp.zeros((H,), dtype=jnp.float32)
        return {'x': x, 'w_gate': w_gate, 'w_expert': w_expert, 'b_expert': b_expert}
    _L1_ffn_all = _L1_ffn_setup()
    _L1_ffn_in = {k: v for k, v in _L1_ffn_all.items() if k in ('w_gate', 'w_expert', 'b_expert')}
    del _L1_ffn_all
    return {'x': x, 'ctx_1024': ctx_1024, 'L0_attn_Wp': _L0_attn_in['Wp'], 'L0_attn_bp': _L0_attn_in['bp'], 'L0_attn_g1': _L0_attn_in['g1'], 'L0_attn_Whg': _L0_attn_in['Whg'], 'L0_attn_bhg': _L0_attn_in['bhg'], 'L0_attn_Wo': _L0_attn_in['Wo'], 'L0_attn_bo': _L0_attn_in['bo'], 'L0_attn_g2': _L0_attn_in['g2'], 'L0_attn_gf': _L0_attn_in['gf'], 'L0_attn_Wf': _L0_attn_in['Wf'], 'L0_attn_bf': _L0_attn_in['bf'], 'L0_xattn_Wq': _L0_xattn_in['Wq'], 'L0_xattn_bq': _L0_xattn_in['bq'], 'L0_xattn_Wk': _L0_xattn_in['Wk'], 'L0_xattn_bk': _L0_xattn_in['bk'], 'L0_xattn_Wv': _L0_xattn_in['Wv'], 'L0_xattn_bv': _L0_xattn_in['bv'], 'L0_xattn_Wo': _L0_xattn_in['Wo'], 'L0_xattn_bo': _L0_xattn_in['bo'], 'L0_xattn_w1': _L0_xattn_in['w1'], 'L0_xattn_b1': _L0_xattn_in['b1'], 'L0_xattn_w2': _L0_xattn_in['w2'], 'L0_xattn_b2': _L0_xattn_in['b2'], 'L0_xattn_w3': _L0_xattn_in['w3'], 'L0_xattn_b3': _L0_xattn_in['b3'], 'L0_ffn_signatures_raw': _L0_ffn_in['signatures_raw'], 'L0_ffn_knot_values': _L0_ffn_in['knot_values'], 'L0_ffn_temperature': _L0_ffn_in['temperature'], 'L0_ffn_compress_w1': _L0_ffn_in['compress_w1'], 'L0_ffn_compress_b1': _L0_ffn_in['compress_b1'], 'L0_ffn_compress_w2': _L0_ffn_in['compress_w2'], 'L0_ffn_compress_b2': _L0_ffn_in['compress_b2'], 'L0_ffn_spline_w1': _L0_ffn_in['spline_w1'], 'L0_ffn_spline_b1': _L0_ffn_in['spline_b1'], 'L0_ffn_spline_w2': _L0_ffn_in['spline_w2'], 'L0_ffn_spline_b2': _L0_ffn_in['spline_b2'], 'L0_ffn_directions': _L0_ffn_in['directions'], 'L0_ffn_norm_gamma': _L0_ffn_in['norm_gamma'], 'L0_ffn_norm_beta': _L0_ffn_in['norm_beta'], 'L0_ffn_output_scale': _L0_ffn_in['output_scale'], 'L1_attn_adaptive_scale': _L1_attn_in['adaptive_scale'], 'L1_attn_Wq': _L1_attn_in['Wq'], 'L1_attn_bq': _L1_attn_in['bq'], 'L1_attn_Wk': _L1_attn_in['Wk'], 'L1_attn_bk': _L1_attn_in['bk'], 'L1_attn_Wv': _L1_attn_in['Wv'], 'L1_attn_bv': _L1_attn_in['bv'], 'L1_attn_Wo': _L1_attn_in['Wo'], 'L1_attn_bo': _L1_attn_in['bo'], 'L1_attn_gamma': _L1_attn_in['gamma'], 'L1_attn_beta': _L1_attn_in['beta'], 'L1_xattn_W_Q': _L1_xattn_in['W_Q'], 'L1_xattn_b_Q': _L1_xattn_in['b_Q'], 'L1_xattn_W_K': _L1_xattn_in['W_K'], 'L1_xattn_b_K': _L1_xattn_in['b_K'], 'L1_xattn_W_V': _L1_xattn_in['W_V'], 'L1_xattn_b_V': _L1_xattn_in['b_V'], 'L1_xattn_W_O': _L1_xattn_in['W_O'], 'L1_xattn_b_O': _L1_xattn_in['b_O'], 'L1_ffn_w_gate': _L1_ffn_in['w_gate'], 'L1_ffn_w_expert': _L1_ffn_in['w_expert'], 'L1_ffn_b_expert': _L1_ffn_in['b_expert']}

def reference(x, ctx_1024, L0_attn_Wp, L0_attn_bp, L0_attn_g1, L0_attn_Whg, L0_attn_bhg, L0_attn_Wo, L0_attn_bo, L0_attn_g2, L0_attn_gf, L0_attn_Wf, L0_attn_bf, L0_xattn_Wq, L0_xattn_bq, L0_xattn_Wk, L0_xattn_bk, L0_xattn_Wv, L0_xattn_bv, L0_xattn_Wo, L0_xattn_bo, L0_xattn_w1, L0_xattn_b1, L0_xattn_w2, L0_xattn_b2, L0_xattn_w3, L0_xattn_b3, L0_ffn_signatures_raw, L0_ffn_knot_values, L0_ffn_temperature, L0_ffn_compress_w1, L0_ffn_compress_b1, L0_ffn_compress_w2, L0_ffn_compress_b2, L0_ffn_spline_w1, L0_ffn_spline_b1, L0_ffn_spline_w2, L0_ffn_spline_b2, L0_ffn_directions, L0_ffn_norm_gamma, L0_ffn_norm_beta, L0_ffn_output_scale, L1_attn_adaptive_scale, L1_attn_Wq, L1_attn_bq, L1_attn_Wk, L1_attn_bk, L1_attn_Wv, L1_attn_bv, L1_attn_Wo, L1_attn_bo, L1_attn_gamma, L1_attn_beta, L1_xattn_W_Q, L1_xattn_b_Q, L1_xattn_W_K, L1_xattn_b_K, L1_xattn_W_V, L1_xattn_b_V, L1_xattn_W_O, L1_xattn_b_O, L1_ffn_w_gate, L1_ffn_w_expert, L1_ffn_b_expert):
    import jax
    import jax.numpy as jnp

    def _L0_attn_ref(x, Wp, bp, g1, Whg, bhg, Wo, bo, g2, gf, Wf, bf):
        import jax, jax.numpy as jnp
        import numpy as np
        DIM = 128
        HID = 256
        L = 4
        DI = int(HID * 1.5)
        B, T = (4, 256)

        def rmsnorm(x, gamma, dim):
            n = jnp.sqrt(jnp.sum(x * x, axis=-1, keepdims=True))
            return x / jnp.maximum(n, 1e-12) * dim ** 0.5 * (gamma + 1.0)

        def log_g(x):
            return jnp.where(x >= 0, jnp.log(jax.nn.relu(x) + 0.5), -jax.nn.softplus(-x))

        def heinsen_scan_log(log_coeffs, log_values):
            a_star = jnp.cumsum(log_coeffs, axis=1)
            log_h = a_star + jax.lax.cumlogsumexp(log_values - a_star, axis=1)
            return jnp.exp(log_h)
        h = x @ Wp + bp
        for i in range(L):
            xn = rmsnorm(h, g1[i], HID)
            hg = xn @ Whg[i] + bhg[i]
            hid, gate = (hg[..., :DI], hg[..., DI:])
            log_coeffs = -jax.nn.softplus(gate)
            log_values = -jax.nn.softplus(-gate) + log_g(hid)
            pad = ((0, 0), (1, 0), (0, 0))
            out_scan = heinsen_scan_log(jnp.pad(log_coeffs, pad), jnp.pad(log_values, pad))
            gru = out_scan[:, 1:, :] @ Wo[i] + bo[i]
            h = gru + h
            h = rmsnorm(h, g2[i], HID) + h
        h = rmsnorm(h, gf, HID)
        return h @ Wf + bf

    def _L0_xattn_ref(query, key, value, Wq, bq, Wk, bk, Wv, bv, Wo, bo, w1, b1, w2, b2, w3, b3):
        import jax, jax.numpy as jnp
        import numpy as np
        import math
        B, S, D, H = (1, 256, 128, 16)
        DK = D // H
        DH = 64
        LOG_T_MIN = math.log(0.1)
        LOG_T_MAX = math.log(10.0)

        def _linear(x, W, b):
            return x @ W.T + b
        b, sq, d = query.shape
        sk = key.shape[1]
        h, dk = (H, DK)
        Q = _linear(query, Wq, bq).reshape(b, sq, h, dk).transpose(0, 2, 1, 3)
        K = _linear(key, Wk, bk).reshape(b, sk, h, dk).transpose(0, 2, 1, 3)
        V = _linear(value, Wv, bv).reshape(b, sk, h, dk).transpose(0, 2, 1, 3)
        qk = jnp.einsum('bhqd,bhkd->bhqk', Q, K)
        scores = qk / math.sqrt(dk)
        mean_sim = scores.mean(axis=(-2, -1))
        max_sim = scores.max(axis=-1).mean(axis=-1)
        probs = jax.nn.softmax(scores, axis=-1)
        entropy_proxy = jnp.var(probs, axis=-1, ddof=1).mean(axis=-1)
        feats = jnp.stack([mean_sim, max_sim, entropy_proxy], axis=-1)
        hidden = jax.nn.gelu(_linear(feats, w1, b1), approximate=False)
        hidden = jax.nn.gelu(_linear(hidden, w2, b2), approximate=False)
        log_t = jnp.clip(_linear(hidden, w3, b3), LOG_T_MIN, LOG_T_MAX)
        t = jnp.exp(log_t)[..., None]
        attn_scores = qk / (2.0 * t)
        attn = jax.nn.softmax(attn_scores, axis=-1)
        attn = jnp.nan_to_num(attn, nan=0.0)
        out = jnp.einsum('bhqk,bhkd->bhqd', attn, V)
        out = out.transpose(0, 2, 1, 3).reshape(b, sq, d)
        return _linear(out, Wo, bo)

    def _L0_ffn_ref(x, signatures_raw, knot_values, temperature, compress_w1, compress_b1, compress_w2, compress_b2, spline_w1, spline_b1, spline_w2, spline_b2, directions, norm_gamma, norm_beta, output_scale):
        import jax, jax.numpy as jnp
        import numpy as np
        D_MODEL = 128
        NUM_TILES = 64
        TPC = 8
        NUM_CLUSTERS = NUM_TILES // TPC
        GRID = 16
        COMP_H = 32
        NUM_KNOTS = 8
        EPS_LN = 1e-05

        def _calibrate(scores, knots, temperature):
            K = knots.shape[0]
            normalized = jax.nn.sigmoid(scores / (temperature[0] + 1e-06))
            idx_float = normalized * (K - 1)
            idx_low = jnp.clip(idx_float.astype(jnp.int32), 0, K - 2)
            idx_high = idx_low + 1
            t = idx_float - idx_low.astype(scores.dtype)
            val_low = knots[idx_low]
            val_high = knots[idx_high]
            return val_low + t * (val_high - val_low)

        def _forward(x, signatures_raw, knot_values, temperature, compress_w1, compress_b1, compress_w2, compress_b2, spline_w1, spline_b1, spline_w2, spline_b2, directions, norm_gamma, norm_beta, output_scale):
            B, T, D = x.shape
            xf = x.reshape(-1, D)
            q = jnp.where(signatures_raw > 0.3, 1.0, jnp.where(signatures_raw < -0.3, -1.0, 0.0)).astype(signatures_raw.dtype)
            sigs = signatures_raw + jax.lax.stop_gradient(q - signatures_raw)
            cluster_sigs = jnp.sign(sigs.reshape(NUM_CLUSTERS, TPC, D).mean(axis=1))
            cluster_scores = xf @ cluster_sigs.T
            cluster_gates = _calibrate(cluster_scores, knot_values, temperature)
            cluster_idx = jnp.argmax(cluster_gates, axis=-1)
            tile_scores = xf @ sigs.T
            tile_gates = _calibrate(tile_scores, knot_values, temperature)
            gates_by_cluster = tile_gates.reshape(-1, NUM_CLUSTERS, TPC)
            sel_gates = jnp.take_along_axis(gates_by_cluster, cluster_idx[:, None, None], axis=1)[:, 0, :]
            local_idx = jnp.argmax(sel_gates, axis=-1)
            tile_idx = cluster_idx * TPC + local_idx
            h = jax.nn.gelu(xf @ compress_w1 + compress_b1, approximate=False)
            comp = jnp.tanh(h @ compress_w2 + compress_b2)
            w1 = spline_w1[tile_idx]
            b1 = spline_b1[tile_idx]
            hh = jax.nn.relu(jnp.einsum('ni,nig->ng', comp, w1) + b1)
            w2 = spline_w2[tile_idx]
            b2 = spline_b2[tile_idx]
            mag = jnp.einsum('ng,ngo->no', hh, w2) + b2
            ffn_out = mag * directions[tile_idx] * output_scale[0]
            y = xf + ffn_out
            mu = y.mean(axis=-1, keepdims=True)
            var = ((y - mu) ** 2).mean(axis=-1, keepdims=True)
            y = (y - mu) / jnp.sqrt(var + EPS_LN) * norm_gamma + norm_beta
            return y.reshape(B, T, D)
        return _forward(x, signatures_raw, knot_values, temperature, compress_w1, compress_b1, compress_w2, compress_b2, spline_w1, spline_b1, spline_w2, spline_b2, directions, norm_gamma, norm_beta, output_scale)

    def _L1_attn_ref(x, adaptive_scale, Wq, bq, Wk, bk, Wv, bv, Wo, bo, gamma, beta):
        import jax, jax.numpy as jnp
        import numpy as np
        H, HD, D = (16, 64, 128)
        SCALE = HD ** (-0.5)
        TEMP = 1.0
        EPS = 1e-05
        B, N, _ = x.shape
        Q = (x @ Wq.T + bq).reshape(B, N, H, HD)
        K = (x @ Wk.T + bk).reshape(B, N, H, HD)
        V = (x @ Wv.T + bv).reshape(B, N, H, HD)
        scores = jnp.einsum('bnhd,bmhd->bhnm', Q, K)
        scores = scores * (SCALE * adaptive_scale)[None, :, None, None] / TEMP
        w = jax.nn.softmax(scores, axis=-1)
        attn = jnp.einsum('bhnm,bmhd->bnhd', w, V).reshape(B, N, H * HD)
        y = x + (attn @ Wo.T + bo)
        mu = jnp.mean(y, axis=-1, keepdims=True)
        var = jnp.var(y, axis=-1, keepdims=True)
        return (y - mu) / jnp.sqrt(var + EPS) * gamma + beta

    def _L1_xattn_ref(Q, K, V, W_Q, b_Q, W_K, b_K, W_V, b_V, W_O, b_O):
        import jax, jax.numpy as jnp
        import numpy as np
        NUM_HEADS = 16
        D_MODEL = 128
        D_K = D_MODEL // NUM_HEADS

        def _split_heads(x):
            B, S, _ = x.shape
            return x.reshape(B, S, NUM_HEADS, D_K).transpose(0, 2, 1, 3)
        q = _split_heads(Q @ W_Q + b_Q)
        k = _split_heads(K @ W_K + b_K)
        v = _split_heads(V @ W_V + b_V)
        inv_sqrt_dk = jnp.asarray(1.0 / np.sqrt(D_K), q.dtype)
        scores = jnp.einsum('bhqd,bhkd->bhqk', q, k) * inv_sqrt_dk
        weights = jax.nn.softmax(scores, axis=-1)
        out = jnp.einsum('bhqk,bhkd->bhqd', weights, v)
        B, _, S, _ = out.shape
        combined = out.transpose(0, 2, 1, 3).reshape(B, S, D_MODEL)
        return combined @ W_O + b_O

    def _L1_ffn_ref(x, w_gate, w_expert, b_expert):
        import jax, jax.numpy as jnp
        import numpy as np
        EXPERT_NUM = 8
        CAPACITY = 100
        B, S, H = x.shape
        E, C = (EXPERT_NUM, CAPACITY)
        hs = x.reshape(-1, H)
        logits = hs @ w_gate
        probs = jax.nn.softmax(logits, axis=1)
        best = jnp.argmax(probs, axis=1)
        mask = jax.nn.one_hot(best, E, dtype=jnp.int32)
        gate = jnp.sum(probs * mask.astype(probs.dtype), axis=1)
        locations = jnp.cumsum(mask, axis=0) - 1
        mask = mask * (locations < C).astype(jnp.int32)
        loc_sum = jnp.sum(locations * mask, axis=1)
        new_gates = gate[:, None] * mask.astype(probs.dtype)
        loc_oh = jax.nn.one_hot(loc_sum, C, dtype=probs.dtype)
        combine = new_gates[:, :, None] * loc_oh[:, None, :]
        dispatch = (combine != 0).astype(hs.dtype)
        dispatched = jnp.einsum('tec,th->ech', dispatch, hs).reshape(E * C, H)
        expert_out = dispatched @ w_expert + b_expert
        combined = combine.reshape(-1, E * C) @ expert_out
        return combined.reshape(B, S, H)
    x = _layernorm(x + _L0_attn_ref(x, L0_attn_Wp, L0_attn_bp, L0_attn_g1, L0_attn_Whg, L0_attn_bhg, L0_attn_Wo, L0_attn_bo, L0_attn_g2, L0_attn_gf, L0_attn_Wf, L0_attn_bf), axis=-1)
    x = _layernorm(x + _L0_xattn_ref(x, ctx_1024, ctx_1024, L0_xattn_Wq, L0_xattn_bq, L0_xattn_Wk, L0_xattn_bk, L0_xattn_Wv, L0_xattn_bv, L0_xattn_Wo, L0_xattn_bo, L0_xattn_w1, L0_xattn_b1, L0_xattn_w2, L0_xattn_b2, L0_xattn_w3, L0_xattn_b3), axis=-1)
    x = _layernorm(x + _L0_ffn_ref(x, L0_ffn_signatures_raw, L0_ffn_knot_values, L0_ffn_temperature, L0_ffn_compress_w1, L0_ffn_compress_b1, L0_ffn_compress_w2, L0_ffn_compress_b2, L0_ffn_spline_w1, L0_ffn_spline_b1, L0_ffn_spline_w2, L0_ffn_spline_b2, L0_ffn_directions, L0_ffn_norm_gamma, L0_ffn_norm_beta, L0_ffn_output_scale), axis=-1)
    x = _layernorm(x + _L1_attn_ref(x, L1_attn_adaptive_scale, L1_attn_Wq, L1_attn_bq, L1_attn_Wk, L1_attn_bk, L1_attn_Wv, L1_attn_bv, L1_attn_Wo, L1_attn_bo, L1_attn_gamma, L1_attn_beta), axis=-1)
    x = _layernorm(x + _L1_xattn_ref(x, ctx_1024, ctx_1024, L1_xattn_W_Q, L1_xattn_b_Q, L1_xattn_W_K, L1_xattn_b_K, L1_xattn_W_V, L1_xattn_b_V, L1_xattn_W_O, L1_xattn_b_O), axis=-1)
    x = _layernorm(x + _L1_ffn_ref(x, L1_ffn_w_gate, L1_ffn_w_expert, L1_ffn_b_expert), axis=-1)
    return x

_drawn_inputs = setup_inputs


def setup_inputs(seed=0):
    import zlib

    import numpy as np

    out = dict(_drawn_inputs(seed))
    spreads = {'L0_attn_bp': (0.0, 0.1),
     'L0_attn_bhg': (0.0, 0.39),
     'L0_attn_bo': (0.0, 0.1),
     'L0_attn_bf': (0.0, 0.1),
     'L0_ffn_compress_b1': (0.0, 0.8),
     'L0_ffn_compress_b2': (0.0, 2.0),
     'L0_ffn_spline_b1': (0.0, 0.8),
     'L0_ffn_spline_b2': (0.0, 2.0),
     'L0_ffn_norm_gamma': (1.0, 0.2),
     'L0_ffn_norm_beta': (0.0, 0.1),
     'L1_attn_adaptive_scale': (1.0, 0.6),
     'L1_attn_gamma': (1.0, 0.2),
     'L1_attn_beta': (0.0, 0.1),
     'L1_ffn_b_expert': (0.0, 0.8)}
    factors = {'L0_attn_g1': 8.0,
     'L0_attn_g2': 8.0,
     'L0_attn_gf': 8.0,
     'L0_xattn_Wq': 8.0,
     'L0_xattn_bq': 8.0,
     'L0_xattn_Wk': 8.0,
     'L0_xattn_bk': 53.223,
     'L0_xattn_bv': 8.0,
     'L0_xattn_w1': 8.0,
     'L0_xattn_b1': 53.223,
     'L0_xattn_w2': 53.223,
     'L0_xattn_b2': 8.0,
     'L0_xattn_w3': 53.223,
     'L0_ffn_signatures_raw': 8.0,
     'L0_ffn_knot_values': 8.0,
     'L0_ffn_compress_w1': 8.0,
     'L0_ffn_compress_w2': 8.0,
     'L0_ffn_spline_w1': 8.0,
     'L0_ffn_spline_w2': 8.0,
     'L0_ffn_directions': 8.0,
     'L1_attn_Wq': 2.876,
     'L1_attn_bq': 8.0,
     'L1_attn_Wk': 2.871,
     'L1_attn_bk': 64.0,
     'L1_xattn_b_Q': 8.0,
     'L1_xattn_b_K': 64.0,
     'L1_xattn_b_V': 2.82,
     'L1_xattn_b_O': 2.796,
     'L1_ffn_w_gate': 5.618,
     'L1_ffn_w_expert': 3.324}
    for name, (base, spread) in spreads.items():
        noise = np.random.default_rng([zlib.crc32(name.encode()), seed]).standard_normal(out[name].shape)
        drawn = base * np.exp(spread * noise) if base else spread * noise
        out[name] = jnp.asarray(drawn.astype(out[name].dtype))
    for name, factor in factors.items():
        out[name] = (out[name] * factor).astype(out[name].dtype)
    return out
```

```python
from contextlib import ExitStack

import numpy as np

import concourse.bass as bass
from concourse import mybir

F32 = mybir.dt.float32
I32 = mybir.dt.int32
U32 = mybir.dt.uint32
ALU = mybir.AluOpType
ACT = mybir.ActivationFunctionType
AX = mybir.AxisListType

P = 128
B = 32
T = 128
D = 128
NT = B * T
GB = 4
GROUP = GB * T
NG = NT // GROUP
S = 77
H = 16
DK = D // H
EPS = 1e-5
DMA = 16


class Count:

    def __init__(self, ctx, nc, name, per=1, weight=1, credits=0):
        self.sem = ctx.enter_context(nc.semaphore(name))
        self.per, self.weight, self.credits = per, weight, credits

    def after(self, i, k=1):
        return i * (self.per * self.weight) + (k + self.credits) * self.weight

    def free(self, i, n=0):
        return i * (self.per * self.weight) + (n + 1) * self.weight

    def give(self, engine):
        engine.sem_inc(self.sem, self.credits * self.weight)


class Tools:

    def __init__(self, ctx, nc, tag):
        self.ctx, self.nc, self.tag, self.numbers = ctx, nc, tag, []

    def sb(self, name, shape, dt=F32):
        return self.ctx.enter_context(self.nc.sbuf_tensor(f"{self.tag}_{name}", shape, dt))

    def ps(self, name, shape, dt=F32):
        return self.ctx.enter_context(self.nc.psum_tensor(f"{self.tag}_{name}", shape, dt))

    def count(self, name, per=1, weight=1, credits=0):
        c = Count(self.ctx, self.nc, f"{self.tag}_{name}", per, weight, credits)
        self.numbers.append(c.sem.num)
        return c

    def clear_counts(self):
        numbers = sorted(self.numbers)
        with self.nc.Block() as block:

            @block.sync
            def _(sp):
                first = last = numbers[0]
                for n in numbers[1:] + [None]:
                    if n != last + 1:
                        sp.sem_clear(range(first, last + 1))
                        first = n
                    last = n


def constants(nc, ctx):
    t = Tools(ctx, nc, "const")
    c = {
        "ident": t.sb("ident", [P, P]),
        "ones": t.sb("ones", [P, P]),
        "mean": t.sb("mean", [P, P]),
        "eps": t.sb("eps", [P, 1]),
        "tiny": t.sb("tiny", [P, 1]),
        "rms_bias": t.sb("rms_bias", [P, 1]),
    }
    cleared = t.count("cleared")
    with nc.Block() as block:

        @block.gpsimd
        def _(pool):
            pool.memset(c["ident"][:, :], 0.0).then_inc(cleared.sem, 1)
            pool.memset(c["ones"][:, :], 1.0)
            pool.memset(c["mean"][:, :], 1.0 / D)
            pool.memset(c["eps"][:, :], EPS)
            pool.memset(c["tiny"][:, :], RMS_TINY)
            pool.memset(c["rms_bias"][:, :], 0.5 * RMS_SHIFT * float(np.log(2.0)))
            pool.wait_ge(cleared.sem, 1)
            pool.affine_select(out=c["ident"][:, :], in_=c["ident"][:, :], compare_op=ALU.not_equal,
                               fill=1.0, base=0, pattern=[[-1, P]], channel_multiplier=1)
    return c


RMS_SHIFT = 24
RMS_TINY = 2.0 ** -64
RMS_SCALE = 2.0 ** RMS_SHIFT
INV_NORM_MAX = 1e12


HID = 256
DI = 384
NL = 4
KH = HID // P
KI = DI // P
TP = T + 1


def min_gru(nc, const, xT, x, Wp, bp, g1, Whg, bhg, Wo, bo, g2, gf, Wf, bf):
    with ExitStack() as ctx:
        t = Tools(ctx, nc, "gru")
        U = 2
        NORMS = 2 * NL + 2
        wp = t.sb("wp", [P, HID])
        whg = t.sb("whg", [P, NL, KH, 2 * DI])
        wo = t.sb("wo", [P, NL, KI, HID])
        wf = t.sb("wf", [P, KH, D])
        bp_c = t.sb("bp_c", [P, KH])
        bhg_c = t.sb("bhg_c", [P, NL, 2 * KI])
        nbg_c = t.sb("nbg_c", [P, NL, 2 * KI])
        bo_c = t.sb("bo_c", [P, NL, KH])
        g1_c = t.sb("g1_c", [P, NL, KH])
        g2_c = t.sb("g2_c", [P, NL, KH])
        gf_c = t.sb("gf_c", [P, KH])
        bf_c = t.sb("bf_c", [P, 1])
        xin = [t.sb(f"xin{u}", [P, GB, D]) for u in range(U)]
        xg = [t.sb(f"xg{u}", [P, GROUP]) for u in range(U)]
        h = [t.sb(f"h{u}", [P, KH, GROUP]) for u in range(U)]
        sq = [t.sb(f"sq{u}", [P, KH, GROUP]) for u in range(U)]
        xn = [t.sb(f"xn{u}", [P, KH, GROUP]) for u in range(U)]
        lnr = [t.sb(f"lnr{u}", [P, GROUP]) for u in range(U)]
        inv = [t.sb(f"inv{u}", [P, GROUP]) for u in range(U)]
        y = [t.sb(f"y{u}", [P, KI, GB * TP]) for u in range(U)]
        decay = [t.sb(f"decay{r}", [P, GB * TP]) for r in range(2)]
        value = [t.sb(f"value{r}", [P, GB * TP]) for r in range(2)]
        zgate = [t.sb(f"zgate{r}", [P, GROUP]) for r in range(2)]
        sighid = [t.sb(f"sighid{r}", [P, GROUP]) for r in range(2)]
        relhid = [t.sb(f"relhid{r}", [P, GROUP]) for r in range(2)]
        ghid = [t.sb(f"ghid{r}", [P, GROUP]) for r in range(2)]
        gain = [t.sb(f"gain{m}", [P, GROUP]) for m in range(KH)]
        ps_stat = [t.ps(f"stat{u}", [P, GROUP]) for u in range(U)]
        ps_hid = [t.ps(f"hid{r}", [P, GROUP]) for r in range(2)]
        ps_gate = [t.ps(f"gate{r}", [P, GROUP]) for r in range(2)]
        ps_out = [t.ps(f"out{m}", [P, GROUP]) for m in range(KH)]

        loaded = [t.count(f"loaded{n}", weight=DMA) for n in range(NL + 1)]
        gains_ready = t.count("gains_ready")
        scaled = [t.count(f"scaled{n}") for n in range(NL + 1)]
        pads_ready = t.count("pads_ready")
        x_loaded = [t.count(f"x_loaded{u}", 1, DMA) for u in range(U)]
        x_turned = t.count("x_turned", U)
        xg_ready = t.count("xg_ready", U)
        sq_ready = [t.count(f"sq_ready{u}", NORMS) for u in range(U)]
        stat_ready = [t.count(f"stat_ready{u}", NORMS + 1) for u in range(U)]
        ln_ready = [t.count(f"ln_ready{u}", NORMS) for u in range(U)]
        inv_ready = [t.count(f"inv_ready{u}", NORMS) for u in range(U)]
        xn_ready = [t.count(f"xn_ready{u}", NL + 1) for u in range(U)]
        h_ready = [t.count(f"h_ready{u}", KH * (1 + 2 * NL)) for u in range(U)]
        gain_ready = t.count("gain_ready", U * KH * NL)
        sum_ready = [t.count(f"sum_ready{u}", 2) for u in range(U)]
        NCH = U * NL * KI
        hg_ready = t.count("hg_ready", NCH)
        gates_ready = t.count("gates_ready", NCH, credits=2)
        ghid_ready = t.count("ghid_ready", NCH)
        value_ready = t.count("value_ready", NCH)
        scan_ready = t.count("scan_ready", NCH, credits=2)
        NOUT = U * (KH * (1 + NL) + 1)
        out_ready = t.count("out_ready", NOUT)
        out_free = t.count("out_free", NOUT, credits=2)
        xT_ready = t.count("xT_ready", U, credits=U)

        ITER = NG // U
        ORDER = [("load", u, 0) for u in range(U)]
        for l in range(NL):
            ORDER += [("pre", u, l) for u in range(U)]
            ORDER += [("rec", u, l) for u in range(U)]
            for u in range(U):
                ORDER += [("mix", u, l), ("post", u, l)]
        ORDER += [("final", u, 0) for u in range(U)]

        def chunk_no(u, l, c):
            return (l * U + u) * KI + c

        def out_no(kind, u, l, m):
            if kind == "load":
                return u * KH + m
            if kind == "mix":
                return U * KH + (l * U + u) * KH + m
            return U * KH * (1 + NL) + u

        with nc.Block() as block:

            @block.sync
            def _(sp):
                cols = lambda v, n: v.rearrange("(n p) -> p n", p=P)
                sp.dma_start(xin[0][:, :, :], x[0:GB].rearrange("b t d -> t b d")).then_inc(x_loaded[0].sem, DMA)
                sp.dma_start(xin[1][:, :, :], x[GB:2 * GB].rearrange("b t d -> t b d")).then_inc(x_loaded[1].sem, DMA)
                for dst, src in (
                    (wp[:, :], Wp), (bp_c[:, :], cols(bp, KH)), (gf_c[:, :], cols(gf, KH)), (bf_c[:, :], cols(bf, 1)),
                    (g1_c[:, :, :], g1.rearrange("l (k p) -> p l k", p=P)),
                    (g2_c[:, :, :], g2.rearrange("l (k p) -> p l k", p=P)),
                    (bo_c[:, :, :], bo.rearrange("l (k p) -> p l k", p=P)),
                    (bhg_c[:, :, :], bhg.rearrange("l (k p) -> p l k", p=P)),
                    (wf[:, :, :], Wf.rearrange("(k p) n -> p k n", p=P)),
                ):
                    sp.dma_start(dst, src, allow_slow_non_contiguous=True).then_inc(loaded[NL].sem, DMA)
                for l in range(NL):
                    sp.dma_start(whg[:, l, :, :], Whg[l].rearrange("(k p) n -> p k n", p=P)).then_inc(loaded[l].sem, DMA)
                    sp.dma_start(wo[:, l, :, :], Wo[l].rearrange("(k p) n -> p k n", p=P)).then_inc(loaded[l].sem, DMA)
                with sp.Fori(0, ITER - 1) as i:
                    for u in range(U):
                        sp.wait_ge(x_turned.sem, x_turned.after(i, u + 1))
                        src = x[bass.ds((i + 1) * (U * GB) + u * GB, GB)].rearrange("b t d -> t b d")
                        sp.dma_start(xin[u][:, :, :], src).then_inc(x_loaded[u].sem, DMA)

            @block.tensor
            def _(pe):
                mm = nc.tensor.matmul

                def stat(i, u, q, w, cols, n):
                    for k in range(n):
                        last = mm(ps_stat[u][:, :], w[:, :], cols[:, k, :], start=(k == 0), stop=(k == n - 1))
                    last.then_inc(stat_ready[u].sem, 1)

                with pe.Fori(0, ITER) as i:
                    for kind, u, l in ORDER:
                        if kind == "load":
                            pe.wait_ge(x_loaded[u].sem, x_loaded[u].after(i))
                            pe.wait_ge(out_free.sem, out_free.free(i, out_no(kind, u, l, 0)))
                            for b in range(GB):
                                last = nc.tensor.transpose(ps_out[0][:, b * T:(b + 1) * T], xin[u][:, b, :], const["ident"][:, :])
                            last.then_inc(x_turned.sem, 1)
                            pe.wait_ge(xg_ready.sem, xg_ready.after(i, u + 1))
                            pe.wait_ge(loaded[NL].sem, loaded[NL].after(0, 9))
                            for m in range(KH):
                                if m:
                                    pe.wait_ge(out_free.sem, out_free.free(i, out_no(kind, u, l, m)))
                                mm(ps_out[m][:, :], wp[:, m * P:(m + 1) * P], xg[u][:, :], start=True, stop=True).then_inc(out_ready.sem, 1)
                        elif kind in ("pre", "post"):
                            q = 2 * l + (kind == "post")
                            pe.wait_ge(sq_ready[u].sem, sq_ready[u].after(i, q + 1))
                            stat(i, u, q, const["ones"], sq[u], KH)
                        elif kind == "rec":
                            pe.wait_ge(xn_ready[u].sem, xn_ready[u].after(i, l + 1))
                            pe.wait_ge(scaled[l].sem, KH)
                            for c in range(KI):
                                n = chunk_no(u, l, c)
                                pe.wait_ge(gates_ready.sem, gates_ready.free(i, n))
                                for bank, off in ((ps_hid[n % 2], c * P), (ps_gate[n % 2], DI + c * P)):
                                    for k in range(KH):
                                        last = mm(bank[:, :], whg[:, l, k, off:off + P], xn[u][:, k, :], start=(k == 0), stop=(k == KH - 1))
                                last.then_inc(hg_ready.sem, 1)
                        elif kind == "mix":
                            pe.wait_ge(scan_ready.sem, scan_ready.after(i, chunk_no(u, l, KI - 1) + 1))
                            for m in range(KH):
                                pe.wait_ge(out_free.sem, out_free.free(i, out_no(kind, u, l, m)))
                                for k in range(KI):
                                    seqs = y[u][:, k, :].rearrange("p (b t) -> p b t", t=TP)[:, :, 1:]
                                    last = mm(ps_out[m][:, :], wo[:, l, k, m * P:(m + 1) * P], seqs, start=(k == 0), stop=(k == KI - 1))
                                last.then_inc(out_ready.sem, 1)
                        else:
                            q = 2 * NL
                            pe.wait_ge(sq_ready[u].sem, sq_ready[u].after(i, q + 1))
                            stat(i, u, q, const["ones"], sq[u], KH)
                            pe.wait_ge(xn_ready[u].sem, xn_ready[u].after(i, NL + 1))
                            pe.wait_ge(scaled[NL].sem, KH)
                            pe.wait_ge(out_free.sem, out_free.free(i, out_no(kind, u, l, 0)))
                            for k in range(KH):
                                last = mm(ps_out[u][:, :], wf[:, k, :], xn[u][:, k, :], start=(k == 0), stop=(k == KH - 1))
                            last.then_inc(out_ready.sem, 1)
                            pe.wait_ge(sum_ready[u].sem, sum_ready[u].after(i, 1))
                            mm(ps_stat[u][:, :], const["mean"][:, :], xg[u][:, :], start=True, stop=True).then_inc(stat_ready[u].sem, 1)
                            pe.wait_ge(sq_ready[u].sem, sq_ready[u].after(i, NORMS))
                            mm(ps_stat[u][:, :], const["mean"][:, :], sq[u][:, 0, :], start=True, stop=True).then_inc(stat_ready[u].sem, 1)

            @block.scalar
            def _(act):
                f = nc.scalar.activation
                act.wait_ge(loaded[NL].sem, loaded[NL].after(0, 9))
                nc.scalar.mul(nbg_c[:, :, :], bhg_c[:, :, :], -1.0).then_inc(gains_ready.sem, 1)
                act.wait_ge(gains_ready.sem, 1)
                act.wait_ge(pads_ready.sem, 4)

                def inverse(i, u, q, s, bias, scale, shift):
                    if u == 0:
                        nc.scalar.preload_act_table_set("natural_log_exp_and_others")
                    act.wait_ge(stat_ready[u].sem, stat_ready[u].after(i, s))
                    f(lnr[u][:, :], ps_stat[u][:, :], ACT.Ln, bias=bias, scale=scale).then_inc(ln_ready[u].sem, 1)
                    act.wait_ge(ln_ready[u].sem, ln_ready[u].after(i, q + 1))
                    f(inv[u][:, :], lnr[u][:, :], ACT.Exp, bias=shift, scale=-0.5).then_inc(inv_ready[u].sem, 1)

                with act.Fori(0, ITER) as i:
                    for kind, u, l in ORDER:
                        if kind == "load":
                            act.wait_ge(x_turned.sem, x_turned.after(i, u + 1))
                            act.wait_ge(xT_ready.sem, xT_ready.free(i, u))
                            f(xg[u][:, :], ps_out[0][:, :], ACT.Copy).then_inc(xg_ready.sem, 1)
                        elif kind in ("pre", "post"):
                            q = 2 * l + (kind == "post")
                            act.wait_ge(h_ready[u].sem, h_ready[u].after(i, KH * (q + 1)))
                            f(sq[u][:, :, :], h[u][:, :, :], ACT.Square).then_inc(sq_ready[u].sem, 1)
                            inverse(i, u, q, q + 1, const["tiny"][:, :], RMS_SCALE, const["rms_bias"][:, :])
                        elif kind == "rec":
                            for c in range(KI):
                                n = chunk_no(u, l, c)
                                r = n % 2
                                act.wait_ge(hg_ready.sem, hg_ready.after(i, n + 1))
                                act.wait_ge(scan_ready.sem, scan_ready.free(i, n))
                                seqs = lambda v: v.rearrange("p (b t) -> p b t", t=T)
                                gate = ps_gate[r][:, :]
                                f(zgate[r][:, :], gate, ACT.Sigmoid, bias=bhg_c[:, l, KI + c:KI + c + 1])
                                f(decay[r][:, :].rearrange("p (b t) -> p b t", t=TP)[:, :, 1:], seqs(gate), ACT.Sigmoid,
                                  bias=nbg_c[:, l, KI + c:KI + c + 1], scale=-1.0)
                                f(sighid[r][:, :], ps_hid[r][:, :], ACT.Sigmoid, bias=bhg_c[:, l, c:c + 1])
                                f(relhid[r][:, :], ps_hid[r][:, :], ACT.Relu, bias=bhg_c[:, l, c:c + 1]).then_inc(gates_ready.sem, 1)
                        elif kind == "final":
                            q = 2 * NL
                            act.wait_ge(h_ready[u].sem, h_ready[u].after(i, KH * (q + 1)))
                            f(sq[u][:, :, :], h[u][:, :, :], ACT.Square).then_inc(sq_ready[u].sem, 1)
                            inverse(i, u, q, q + 1, const["tiny"][:, :], RMS_SCALE, const["rms_bias"][:, :])
                            act.wait_ge(sum_ready[u].sem, sum_ready[u].after(i, 2))
                            f(sq[u][:, 0, :], xg[u][:, :], ACT.Square).then_inc(sq_ready[u].sem, 1)
                            inverse(i, u, NORMS - 1, NORMS + 1, const["eps"][:, :], 1.0, 0.0)

            @block.vector
            def _(dve):
                v = nc.vector
                dve.wait_ge(loaded[NL].sem, loaded[NL].after(0, 9))
                root = float(HID) ** 0.5
                for g in (g1_c[:, :, :], g2_c[:, :, :], gf_c[:, :]):
                    v.tensor_scalar(g, g, 1.0, root, ALU.add, ALU.mult).then_inc(gains_ready.sem, 1)
                dve.wait_ge(gains_ready.sem, 4)
                for r in range(2):
                    v.memset(decay[r][:, :].rearrange("p (b t) -> p b t", t=TP)[:, :, 0:1], 0.0).then_inc(pads_ready.sem, 1)
                    v.memset(value[r][:, :].rearrange("p (b t) -> p b t", t=TP)[:, :, 0:1], 1.0).then_inc(pads_ready.sem, 1)
                for l in range(NL):
                    dve.wait_ge(loaded[l].sem, loaded[l].after(0, 2))
                    for k in range(KH):
                        v.tensor_scalar(whg[:, l, k, :], whg[:, l, k, :], g1_c[:, l, k:k + 1], None, ALU.mult).then_inc(scaled[l].sem, 1)
                for k in range(KH):
                    v.tensor_scalar(wf[:, k, :], wf[:, k, :], gf_c[:, k:k + 1], None, ALU.mult).then_inc(scaled[NL].sem, 1)
                out_free.give(dve)
                gates_ready.give(dve)
                scan_ready.give(dve)
                xT_ready.give(dve)

                with dve.Fori(0, ITER) as i:
                    for kind, u, l in ORDER:
                        if kind == "load":
                            for m in range(KH):
                                dve.wait_ge(out_ready.sem, out_ready.after(i, out_no(kind, u, l, m) + 1))
                                v.tensor_scalar(h[u][:, m, :], ps_out[m][:, :], bp_c[:, m:m + 1], None, ALU.add).then_inc(h_ready[u].sem, 1)
                            dve.wait_ge(h_ready[u].sem, h_ready[u].after(i, KH))
                            dve.sem_inc(out_free.sem, KH)
                        elif kind == "pre":
                            q = 2 * l
                            dve.wait_ge(inv_ready[u].sem, inv_ready[u].after(i, q + 1))
                            both = inv[u][:, :].rearrange("p (k t) -> p k t", k=1).broadcast_to([P, KH, GROUP])
                            v.scalar_tensor_tensor(xn[u][:, :, :], both, INV_NORM_MAX, h[u][:, :, :], ALU.min, ALU.mult).then_inc(xn_ready[u].sem, 1)
                        elif kind == "rec":
                            for c in range(KI):
                                n = chunk_no(u, l, c)
                                r = n % 2
                                dve.wait_ge(gates_ready.sem, gates_ready.after(i, n + 1))
                                v.scalar_tensor_tensor(ghid[r][:, :], sighid[r][:, :], 0.5, relhid[r][:, :], ALU.min, ALU.add).then_inc(ghid_ready.sem, 1)
                                dve.wait_ge(ghid_ready.sem, ghid_ready.after(i, n + 1))
                                seqs = lambda w: w.rearrange("p (b t) -> p b t", t=T)
                                v.tensor_tensor(value[r][:, :].rearrange("p (b t) -> p b t", t=TP)[:, :, 1:], seqs(ghid[r][:, :]),
                                                seqs(zgate[r][:, :]), ALU.mult).then_inc(value_ready.sem, 1)
                                dve.wait_ge(value_ready.sem, value_ready.after(i, n + 1))
                                v.tensor_tensor_scan(y[u][:, c, :], decay[r][:, :], value[r][:, :], 0.0, ALU.mult, ALU.add).then_inc(scan_ready.sem, 1)
                        elif kind == "mix":
                            for m in range(KH):
                                dve.wait_ge(out_ready.sem, out_ready.after(i, out_no(kind, u, l, m) + 1))
                                v.scalar_tensor_tensor(h[u][:, m, :], ps_out[m][:, :], bo_c[:, l, m:m + 1], h[u][:, m, :], ALU.add, ALU.add).then_inc(h_ready[u].sem, 1)
                            dve.wait_ge(h_ready[u].sem, h_ready[u].after(i, KH * (2 * l + 2)))
                            dve.sem_inc(out_free.sem, KH)
                        elif kind == "post":
                            q = 2 * l + 1
                            dve.wait_ge(inv_ready[u].sem, inv_ready[u].after(i, q + 1))
                            for m in range(KH):
                                g = (l * U + u) * KH + m
                                v.tensor_scalar(gain[m][:, :], inv[u][:, :], INV_NORM_MAX, g2_c[:, l, m:m + 1], ALU.min, ALU.mult).then_inc(gain_ready.sem, 1)
                            for m in range(KH):
                                g = (l * U + u) * KH + m
                                dve.wait_ge(gain_ready.sem, gain_ready.after(i, g + 1))
                                v.scalar_tensor_tensor(h[u][:, m, :], gain[m][:, :], 1.0, h[u][:, m, :], ALU.add, ALU.mult).then_inc(h_ready[u].sem, 1)
                        else:
                            q = 2 * NL
                            dve.wait_ge(inv_ready[u].sem, inv_ready[u].after(i, q + 1))
                            both = inv[u][:, :].rearrange("p (k t) -> p k t", k=1).broadcast_to([P, KH, GROUP])
                            v.scalar_tensor_tensor(xn[u][:, :, :], both, INV_NORM_MAX, h[u][:, :, :], ALU.min, ALU.mult).then_inc(xn_ready[u].sem, 1)
                            dve.wait_ge(out_ready.sem, out_ready.after(i, out_no(kind, u, l, 0) + 1))
                            v.scalar_tensor_tensor(xg[u][:, :], ps_out[u][:, :], bf_c[:, 0:1], xg[u][:, :], ALU.add, ALU.add).then_inc(sum_ready[u].sem, 1)
                            dve.wait_ge(sum_ready[u].sem, sum_ready[u].after(i, 1))
                            dve.sem_inc(out_free.sem, 1)
                            dve.wait_ge(stat_ready[u].sem, stat_ready[u].after(i, NORMS))
                            v.tensor_tensor(xg[u][:, :], xg[u][:, :], ps_stat[u][:, :], ALU.subtract).then_inc(sum_ready[u].sem, 1)
                            dve.wait_ge(inv_ready[u].sem, inv_ready[u].after(i, NORMS))
                            dst = xT[:, bass.ds(i * (U * GROUP) + u * GROUP, GROUP)]
                            v.tensor_tensor(dst, xg[u][:, :], inv[u][:, :], ALU.mult).then_inc(xT_ready.sem, 1)
        t.clear_counts()


class Norm:

    def __init__(self, t, const, name, per, y, sq, logs, inv, bank):
        self.const, self.y, self.sq, self.logs, self.inv, self.bank = const, y, sq, logs, inv, bank
        self.y_ready = t.count(f"{name}_y_ready", per)
        self.mean_ready = t.count(f"{name}_mean_ready", per)
        self.centred = t.count(f"{name}_centred", per)
        self.sq_ready = t.count(f"{name}_sq_ready", per)
        self.var_ready = t.count(f"{name}_var_ready", per)
        self.log_ready = t.count(f"{name}_log_ready", per, credits=1)
        self.inv_ready = t.count(f"{name}_inv_ready", per)

    def tensor(self, nc, pe, i, n):
        pe.wait_ge(self.y_ready.sem, self.y_ready.after(i, n + 1))
        nc.tensor.matmul(self.bank[:, :], self.const["mean"][:, :], self.y[:, :], start=True, stop=True).then_inc(self.mean_ready.sem, 1)
        pe.wait_ge(self.sq_ready.sem, self.sq_ready.after(i, n + 1))
        nc.tensor.matmul(self.bank[:, :], self.const["mean"][:, :], self.sq[:, :], start=True, stop=True).then_inc(self.var_ready.sem, 1)

    def scalar(self, nc, act, i, n):
        act.wait_ge(self.centred.sem, self.centred.after(i, n + 1))
        nc.scalar.activation(self.sq[:, :], self.y[:, :], ACT.Square).then_inc(self.sq_ready.sem, 1)
        nc.scalar.preload_act_table_set("natural_log_exp_and_others")
        act.wait_ge(self.var_ready.sem, self.var_ready.after(i, n + 1))
        nc.scalar.activation(self.logs[:, :], self.bank[:, :], ACT.Ln, bias=self.const["eps"][:, :]).then_inc(self.log_ready.sem, 1)
        act.wait_ge(self.log_ready.sem, self.log_ready.after(i, n + 1))
        nc.scalar.activation(self.inv[:, :], self.logs[:, :], ACT.Exp, scale=-0.5).then_inc(self.inv_ready.sem, 1)

    def centre(self, nc, dve, i, n):
        dve.wait_ge(self.mean_ready.sem, self.mean_ready.after(i, n + 1))
        nc.vector.tensor_tensor(self.y[:, :], self.y[:, :], self.bank[:, :], ALU.subtract).then_inc(self.centred.sem, 1)

    def divide(self, nc, dve, i, n, out, done):
        dve.wait_ge(self.inv_ready.sem, self.inv_ready.after(i, n + 1))
        nc.vector.tensor_tensor(out, self.y[:, :], self.inv[:, :], ALU.mult).then_inc(done.sem, 1)


def group_of(xT, i, u, U):
    return xT[:, bass.ds(i * (U * GROUP) + u * GROUP, GROUP)]


def load_transposed(nc, const, tag, pairs, bank):
    with ExitStack() as ctx:
        t = Tools(ctx, nc, tag)
        blocks = []
        for dst, src in pairs:
            n = max(1, dst.shape[1] // P)
            if n == 1:
                blocks.append((dst, src))
            else:
                blocks += [(dst[:, k * P:(k + 1) * P], src[k * P:(k + 1) * P, :] if src.shape[0] == n * P else src[:, k * P:(k + 1) * P])
                           for k in range(n)]
        raw = t.sb("raw", [P, len(blocks), P])
        loaded = t.count("loaded", weight=DMA)
        turned = t.count("turned")
        kept = t.count("kept")
        with nc.Block() as block:

            @block.sync
            def _(sp):
                for n, (_, src) in enumerate(blocks):
                    sp.dma_start(raw[0:src.shape[0], n, 0:src.shape[1]], src).then_inc(loaded.sem, DMA)

            @block.tensor
            def _(pe):
                pe.wait_ge(loaded.sem, len(blocks) * DMA)
                for n, (_, src) in enumerate(blocks):
                    a, b = src.shape
                    if n >= 2:
                        pe.wait_ge(kept.sem, n - 1)
                    nc.tensor.transpose(bank[n % 2][0:b, 0:a], raw[0:a, n, 0:b], const["ident"][0:a, 0:a]).then_inc(turned.sem, 1)

            @block.vector
            def _(dve):
                for n, (dst, src) in enumerate(blocks):
                    a, b = src.shape
                    dve.wait_ge(turned.sem, n + 1)
                    nc.vector.tensor_copy(dst[0:b, 0:a], bank[n % 2][0:b, 0:a]).then_inc(kept.sem, 1)
        t.clear_counts()


MLP = 64
LOG_T_MIN, LOG_T_MAX = float(np.log(0.1)), float(np.log(10.0))


def cross_attention(nc, const, tag, xT, context, wq, bq, wk, bk, wv, bv, wo, bo, turn, temper=None):
    with ExitStack() as ctx:
        t = Tools(ctx, nc, tag)
        U = 2
        ITER = NG // U
        NB = U * GB
        KS = GB * S
        BANKS = [(0, 6), (6, 6), (12, 4)]
        w = {n: t.sb(f"w_{n}", [P, D]) for n in "qkvo"}
        bias = {n: t.sb(f"b_{n}", [P, 1]) for n in "qko"}
        bv_row = t.sb("bv_row", [S, D])
        heads = t.sb("heads", [P, H])
        ctx_in = [t.sb(f"ctx_in{u}", [S, GB, D]) for u in range(U)]
        cT = [t.sb(f"cT{u}", [P, KS]) for u in range(U)]
        kT = [t.sb(f"kT{u}", [P, KS]) for u in range(U)]
        q = [t.sb(f"q{u}", [P, GROUP]) for u in range(U)]
        vaug = [t.sb(f"vaug{u}", [S, GB, H, DK + 1]) for u in range(U)]
        kbd = [t.sb(f"kbd{r}", [P, H, S]) for r in range(2)]
        m = [t.sb(f"m{u}", [P, GB, H]) for u in range(U)]
        dist = [t.sb(f"dist{u}", [P, GB, H, S]) for u in range(U)]
        probs = [t.sb(f"probs{r}", [P, H, S]) for r in range(2)]
        pt = [t.sb(f"pt{r}", [S, H * T]) for r in range(2)]
        rz = [t.sb(f"rz{r}", [P, H]) for r in range(2)]
        zmax = [t.sb(f"zmax{r}", [P, H]) for r in range(2)]
        o = [t.sb(f"o{u}", [P, GB, H, DK]) for u in range(U)]
        oT = t.sb("oT", [P, GROUP])
        y = t.sb("y", [P, GROUP])
        sq = t.sb("sq", [P, GROUP])
        logs = t.sb("logs", [P, GROUP])
        inv = t.sb("inv", [P, GROUP])
        ps_s = t.ps("scores", [P, 3, 512])
        ps_x = t.ps("proj", [P, 512])
        ps_t = [t.ps(f"turned{r}", [P, 512]) for r in range(2)]
        ps_o = t.ps("out", [P, 512])
        ps_n = t.ps("norm", [P, 512])
        if temper:
            tw1, tb1, tw2, tb2, tw3, tb3 = temper
            w1raw = t.sb("w1raw", [P, MLP, 3])
            w1b = t.sb("w1b", [P, 3, P])
            w2T = t.sb("w2T", [P, P])
            w3raw = t.sb("w3raw", [P, 1])
            w3b = t.sb("w3b", [P, P])
            mb1, mb2, mb3 = t.sb("mb1", [P, 1]), t.sb("mb2", [P, 1]), t.sb("mb3", [P, 1])
            half = t.sb("half", [P, 1])
            e1 = [t.sb(f"e1_{r}", [P, H, S]) for r in range(2)]
            e1sq = [t.sb(f"e1sq_{r}", [P, H, S]) for r in range(2)]
            qs = [t.sb(f"qs{u}", [P, GB]) for u in range(U)]
            ks = [t.sb(f"ks{u}", [P, GB]) for u in range(U)]
            qk = [t.sb(f"qk{u}", [P, GB]) for u in range(U)]
            mean_f = [t.sb(f"mean_f{u}", [P, GB, H]) for u in range(U)]
            z1 = [t.sb(f"z1_{u}", [P, GB, H]) for u in range(U)]
            s2 = [t.sb(f"s2_{u}", [P, GB, H]) for u in range(U)]
            var_f = [t.sb(f"var_f{u}", [P, GB, H]) for u in range(U)]
            g1 = [t.sb(f"g1_{u}", [P, GB * H]) for u in range(U)]
            g2 = [t.sb(f"g2_{u}", [P, GB * H]) for u in range(U)]
            lt = [t.sb(f"lt{u}", [P, GB * H]) for u in range(U)]
            rt = [t.sb(f"rt{u}", [P, GB * H]) for u in range(U)]

        loaded = t.count("loaded", weight=DMA)
        masked = t.count("masked")
        prepared = t.count("prepared")
        ctx_loaded = [t.count(f"ctx_loaded{u}", 1, DMA) for u in range(U)]
        ctx_turned = t.count("ctx_turned", U)
        ct_ready = t.count("ct_ready", U)
        k_mm = t.count("k_mm", U)
        k_ready = t.count("k_ready", U)
        v_mm = t.count("v_mm", U)
        v_ready = t.count("v_ready", U)
        q_mm = t.count("q_mm", U)
        q_ready = t.count("q_ready", U, credits=1)
        kbd_ready = t.count("kbd_ready", NB)
        s_ready = t.count("s_ready", NB, credits=2)
        m_ready = t.count("m_ready", NB)
        d_ready = t.count("d_ready", NB, credits=1)
        p_ready = t.count("p_ready", NB)
        t_mm = [t.count(f"t_mm{r}", 2 * NB, credits=4) for r in range(2)]
        pt_ready = [t.count(f"pt_ready{r}", 2 * NB, credits=1) for r in range(2)]
        pv_mm = t.count("pv_mm", NB, credits=2)
        z_ready = t.count("z_ready", NB)
        rz_ready = t.count("rz_ready", NB)
        o_ready = t.count("o_ready", NB, credits=1)
        ot_mm = t.count("ot_mm", U)
        ot_ready = t.count("ot_ready", U)
        wo_mm = t.count("wo_mm", U)
        xT_ready = t.count("xT_ready", U)
        norm = Norm(t, const, "ln", U, y, sq, logs, inv, ps_n)
        if temper:
            e1_ready = t.count("e1_ready", NB)
            e1sq_ready = t.count("e1sq_ready", NB)
            s2_ready = t.count("s2_ready", NB, credits=2)
            small = t.count("small", 5 * U)
            mean_ready = t.count("mean_ready", U)
            feat_ready = t.count("feat_ready", U)
            hid_mm = t.count("hid_mm", U)
            g1_ready = t.count("g1_ready", U)
            h2_mm = t.count("h2_mm", U)
            g2_ready = t.count("g2_ready", U)
            logt_mm = t.count("logt_mm", U)
            lt_ready = t.count("lt_ready", 2 * U, credits=2)
            rt_ready = t.count("rt_ready", U)
            pre_ready = t.count("pre_ready", NB)

        ORDER = [("proj", 0, 0), ("proj", 1, 0)]
        ORDER += [("score", 0, b) for b in range(GB)]
        ORDER += [("temp", 0, 0)]
        for b in range(GB):
            ORDER += [("score", 1, b), ("attend", 0, b)]
        ORDER += [("temp", 1, 0), ("out", 0, 0)]
        ORDER += [("attend", 1, b) for b in range(GB)]
        ORDER += [("out", 1, 0)]

        if turn:
            load_transposed(nc, const, f"{tag}_w", [(w[n][:, :], a) for n, a in zip("qkvo", (wq, wk, wv, wo))], ps_t)
        NPRE = 5
        with nc.Block() as block:

            @block.sync
            def _(sp):
                loads = [(bias["q"][:, :], bq.rearrange("(p a) -> p a", a=1)), (bias["k"][:, :], bk.rearrange("(p a) -> p a", a=1)),
                         (bias["o"][:, :], bo.rearrange("(p a) -> p a", a=1)), (bv_row[:, :], bv.partition_broadcast(S))]
                if not turn:
                    loads += [(w[n][:, :], a) for n, a in zip("qkvo", (wq, wk, wv, wo))]
                for dst, src in loads:
                    sp.dma_start(dst, src).then_inc(loaded.sem, DMA)
                if temper:
                    sp.wait_ge(masked.sem, 2 + NPRE)
                    for dst, src in ((w1raw[:, :, :].rearrange("p a b -> p (a b)"), tw1.rearrange("a b -> (a b)").partition_broadcast(P)),
                                     (mb1[0:MLP, :], tb1.rearrange("(p a) -> p a", a=1)), (mb2[0:MLP, :], tb2.rearrange("(p a) -> p a", a=1)),
                                     (w3raw[0:MLP, :], tw3.rearrange("a p -> p a")), (mb3[:, :], tb3.partition_broadcast(P))):
                        sp.dma_start(dst, src, allow_slow_non_contiguous=True).then_inc(loaded.sem, DMA)
                sp.wait_ge(loaded.sem, (len(loads) + (5 if temper else 0)) * DMA)

            @block.gpsimd
            def _(pool):
                pool.memset(heads[:, :], 1.0).then_inc(masked.sem, 1)
                pool.wait_ge(masked.sem, 1)
                pool.affine_select(out=heads[:, :], in_=heads[:, :], compare_op=ALU.is_ge, fill=0.0, base=0,
                                   pattern=[[-DK, H]], channel_multiplier=1).then_inc(masked.sem, 1)
                if temper:
                    for z in (w1b[:, :, :], w2T[:, :], w3raw[:, :], mb1[:, :], mb2[:, :]):
                        pool.memset(z, 0.0).then_inc(masked.sem, 1)
                    pool.memset(half[:, :], float(np.log(0.5)))
                pool.wait_ge(masked.sem, 2)
                pool.affine_select(out=heads[:, :], in_=heads[:, :], compare_op=ALU.is_ge, fill=0.0, base=DK - 1,
                                   pattern=[[DK, H]], channel_multiplier=-1)

            @block.vector
            def _(dve):
                for u in range(U):
                    nc.vector.memset(vaug[u][:, :, :, DK:DK + 1], 1.0)
                if temper:
                    dve.wait_ge(loaded.sem, (4 + 5) * DMA)
                    root = float(np.sqrt(DK))
                    for f, s in enumerate((1.0 / (root * T * S), 1.0 / (root * T), 1.0 / T)):
                        nc.vector.tensor_scalar(w1b[:, f, 0:MLP], w1raw[:, :, f], s, None, ALU.mult)
                    nc.vector.tensor_scalar(w3b[:, :], const["ones"][:, :], w3raw[:, 0:1], None, ALU.mult)
        if temper:
            load_transposed(nc, const, f"{tag}_w2", [(w2T[:, :], tw2)], ps_t)

        with nc.Block() as block:

            @block.sync
            def _(sp):
                def load(u, first):
                    sp.dma_start(ctx_in[u][:, :, :], context[first].rearrange("b s d -> s b d")).then_inc(ctx_loaded[u].sem, DMA)
                for u in range(U):
                    load(u, slice(u * GB, (u + 1) * GB))
                with sp.Fori(0, ITER - 1) as i:
                    for u in range(U):
                        sp.wait_ge(ctx_turned.sem, ctx_turned.after(i, u + 1))
                        load(u, bass.ds((i + 1) * NB + u * GB, GB))

            @block.tensor
            def _(pe):
                mm, turn_ = nc.tensor.matmul, nc.tensor.transpose
                ident = const["ident"]
                with pe.Fori(0, ITER) as i:
                    for kind, u, b in ORDER:
                        n = u * GB + b
                        if kind == "proj":
                            pe.wait_ge(ctx_loaded[u].sem, ctx_loaded[u].after(i))
                            pe.wait_ge(q_ready.sem, q_ready.free(i, u))
                            if temper and u == 0:
                                pe.wait_ge(lt_ready.sem, lt_ready.free(i, 1))
                            for c in range(GB):
                                last = turn_(ps_x[:, c * S:(c + 1) * S], ctx_in[u][:, c, :], ident[0:S, 0:S])
                            last.then_inc(ctx_turned.sem, 1)
                            pe.wait_ge(ct_ready.sem, ct_ready.after(i, u + 1))
                            mm(ps_x[:, 0:KS], w["k"][:, :], cT[u][:, :], start=True, stop=True).then_inc(k_mm.sem, 1)
                            pe.wait_ge(k_ready.sem, k_ready.after(i, u + 1))
                            for c in range(GB):
                                last = mm(ps_x[0:S, c * D:(c + 1) * D], cT[u][:, c * S:(c + 1) * S], w["v"][:, :], start=True, stop=True)
                            last.then_inc(v_mm.sem, 1)
                            pe.wait_ge(v_ready.sem, v_ready.after(i, u + 1))
                            mm(ps_x[:, :], w["q"][:, :], group_of(xT, i, u, U), start=True, stop=True).then_inc(q_mm.sem, 1)
                        elif kind == "score":
                            pe.wait_ge(q_ready.sem, q_ready.after(i, u + 1))
                            pe.wait_ge(kbd_ready.sem, kbd_ready.after(i, n + 1))
                            pe.wait_ge(d_ready.sem, d_ready.free(i, n))
                            for j, (h0, nh) in enumerate(BANKS):
                                last = mm(ps_s[:, j, 0:nh * S], q[u][:, b * T:(b + 1) * T],
                                          kbd[n % 2][:, h0:h0 + nh, :].rearrange("p h s -> p (h s)"), start=True, stop=True)
                            last.then_inc(s_ready.sem, 1)
                        elif kind == "temp" and temper:
                            pe.wait_ge(feat_ready.sem, feat_ready.after(i, u + 1))
                            pe.wait_ge(q_ready.sem, q_ready.after(i, U))
                            if u:
                                pe.wait_ge(lt_ready.sem, lt_ready.after(i, 2))
                            flat = lambda a: a.rearrange("p b h -> p (b h)")
                            for f, feat in enumerate((mean_f[u], m[u], var_f[u])):
                                last = mm(ps_x[:, 0:GB * H], w1b[:, f, :], flat(feat[:, :, :]), start=(f == 0), stop=(f == 2))
                            last.then_inc(hid_mm.sem, 1)
                            pe.wait_ge(g1_ready.sem, g1_ready.after(i, u + 1))
                            mm(ps_x[:, 0:GB * H], w2T[:, :], g1[u][:, :], start=True, stop=True).then_inc(h2_mm.sem, 1)
                            pe.wait_ge(g2_ready.sem, g2_ready.after(i, u + 1))
                            mm(ps_x[:, 0:GB * H], w3b[:, :], g2[u][:, :], start=True, stop=True).then_inc(logt_mm.sem, 1)
                        elif kind == "attend":
                            pe.wait_ge(p_ready.sem, p_ready.after(i, n + 1))
                            for c in range(4):
                                r = c % 2
                                pe.wait_ge(pt_ready[r].sem, pt_ready[r].free(i, 2 * n + c // 2))
                                for j in range(4):
                                    last = turn_(ps_t[r][0:S, j * T:(j + 1) * T], probs[n % 2][:, 4 * c + j, :], ident[:, :])
                                last.then_inc(t_mm[r].sem, 1)
                            for r in range(2):
                                pe.wait_ge(pt_ready[r].sem, pt_ready[r].after(i, 2 * n + 2))
                            pe.wait_ge(o_ready.sem, o_ready.free(i, n))
                            for hd in range(H):
                                last = mm(ps_o[:, hd * (DK + 1):(hd + 1) * (DK + 1)], pt[n % 2][:, hd * T:(hd + 1) * T],
                                          vaug[u][:, b, hd, :], start=True, stop=True)
                            last.then_inc(pv_mm.sem, 1)
                        elif kind == "out":
                            pe.wait_ge(o_ready.sem, o_ready.after(i, (u + 1) * GB))
                            pe.wait_ge(norm.log_ready.sem, norm.log_ready.free(i, u))
                            for c in range(GB):
                                last = turn_(ps_n[:, c * T:(c + 1) * T], o[u][:, c, :, :].rearrange("p h d -> p (h d)"), ident[:, :])
                            last.then_inc(ot_mm.sem, 1)
                            pe.wait_ge(ot_ready.sem, ot_ready.after(i, u + 1))
                            mm(ps_n[:, :], w["o"][:, :], oT[:, :], start=True, stop=True).then_inc(wo_mm.sem, 1)
                            norm.tensor(nc, pe, i, u)

            @block.scalar
            def _(act):
                f = nc.scalar.activation
                with act.Fori(0, ITER) as i:
                    for kind, u, b in ORDER:
                        n = u * GB + b
                        if kind == "proj":
                            act.wait_ge(ctx_turned.sem, ctx_turned.after(i, u + 1))
                            f(cT[u][:, :], ps_x[:, 0:KS], ACT.Copy).then_inc(ct_ready.sem, 1)
                            act.wait_ge(k_mm.sem, k_mm.after(i, u + 1))
                            f(kT[u][:, :], ps_x[:, 0:KS], ACT.Identity, bias=bias["k"][:, :]).then_inc(k_ready.sem, 1)
                            act.wait_ge(q_mm.sem, q_mm.after(i, u + 1))
                            f(q[u][:, :], ps_x[:, :], ACT.Identity, bias=bias["q"][:, :]).then_inc(q_ready.sem, 1)
                        elif kind == "score" and temper:
                            act.wait_ge(d_ready.sem, d_ready.after(i, n + 1))
                            act.wait_ge(s2_ready.sem, s2_ready.free(i, n))
                            f(e1[n % 2][:, :, :], dist[u][:, b, :, :], ACT.Exp, scale=DK ** -0.5).then_inc(e1_ready.sem, 1)
                            act.wait_ge(e1_ready.sem, e1_ready.after(i, n + 1))
                            f(e1sq[n % 2][:, :, :], e1[n % 2][:, :, :], ACT.Square).then_inc(e1sq_ready.sem, 1)
                        elif kind == "temp" and temper:
                            act.wait_ge(hid_mm.sem, hid_mm.after(i, u + 1))
                            f(g1[u][:, :], ps_x[:, 0:GB * H], ACT.Gelu, bias=mb1[:, :]).then_inc(g1_ready.sem, 1)
                            act.wait_ge(h2_mm.sem, h2_mm.after(i, u + 1))
                            f(g2[u][:, :], ps_x[:, 0:GB * H], ACT.Gelu, bias=mb2[:, :]).then_inc(g2_ready.sem, 1)
                            act.wait_ge(lt_ready.sem, lt_ready.after(i, 2 * u + 2))
                            f(rt[u][:, :], lt[u][:, :], ACT.Exp, bias=half[:, :], scale=-1.0).then_inc(rt_ready.sem, 1)
                        elif kind == "attend":
                            if temper:
                                act.wait_ge(pre_ready.sem, pre_ready.after(i, n + 1))
                                f(probs[n % 2][:, :, :], probs[n % 2][:, :, :], ACT.Exp).then_inc(p_ready.sem, 1)
                            else:
                                act.wait_ge(d_ready.sem, d_ready.after(i, n + 1))
                                act.wait_ge(t_mm[1].sem, t_mm[1].after(i, 2 * (n - 1)))
                                f(probs[n % 2][:, :, :], dist[u][:, b, :, :], ACT.Exp, scale=DK ** -0.5).then_inc(p_ready.sem, 1)
                            act.wait_ge(pv_mm.sem, pv_mm.after(i, n - 1))
                            for c in (0, 2):
                                act.wait_ge(t_mm[0].sem, t_mm[0].after(i, 2 * n + c // 2 + 1))
                                f(pt[n % 2][:, 4 * c * T:4 * (c + 1) * T], ps_t[0][0:S, :], ACT.Relu).then_inc(pt_ready[0].sem, 1)
                        elif kind == "out":
                            act.wait_ge(ot_mm.sem, ot_mm.after(i, u + 1))
                            f(oT[:, :], ps_n[:, :], ACT.Copy).then_inc(ot_ready.sem, 1)
                            norm.scalar(nc, act, i, u)

            @block.gpsimd
            def _(pool):
                with pool.Fori(0, ITER) as i:
                    for kind, u, b in ORDER:
                        n = u * GB + b
                        if kind == "score":
                            pool.wait_ge(k_ready.sem, k_ready.after(i, u + 1))
                            pool.wait_ge(s_ready.sem, s_ready.after(i, n - 1))
                            keys = kT[u][:, b * S:(b + 1) * S].unsqueeze(1).broadcast_to([P, H, S])
                            pool.tensor_tensor(kbd[n % 2][:, :, :], keys, heads[:, :].unsqueeze(2).broadcast_to([P, H, S]), ALU.mult).then_inc(kbd_ready.sem, 1)
                        elif kind == "attend" and temper:
                            pool.wait_ge(rt_ready.sem, rt_ready.after(i, u + 1))
                            pool.wait_ge(t_mm[1].sem, t_mm[1].after(i, 2 * (n - 1)))
                            r = rt[u][:, b * H:(b + 1) * H].unsqueeze(2).broadcast_to([P, H, S])
                            pool.tensor_tensor(probs[n % 2][:, :, :], dist[u][:, b, :, :], r, ALU.mult).then_inc(pre_ready.sem, 1)

            @block.vector
            def _(dve):
                v = nc.vector
                for c in (q_ready, s_ready, d_ready, *t_mm, *pt_ready, pv_mm, o_ready, norm.log_ready):
                    c.give(dve)
                if temper:
                    s2_ready.give(dve)
                    lt_ready.give(dve)

                def sums(i, u, b):
                    n = u * GB + b
                    dve.wait_ge(e1_ready.sem, e1_ready.after(i, n + 1))
                    v.tensor_reduce(z1[u][:, b, :], e1[n % 2][:, :, :], AX.X, ALU.add)
                    dve.wait_ge(e1sq_ready.sem, e1sq_ready.after(i, n + 1))
                    v.tensor_reduce(s2[u][:, b, :], e1sq[n % 2][:, :, :], AX.X, ALU.add).then_inc(s2_ready.sem, 1)

                with dve.Fori(0, ITER) as i:
                    for kind, u, b in ORDER:
                        n = u * GB + b
                        if kind == "proj":
                            dve.wait_ge(v_mm.sem, v_mm.after(i, u + 1))
                            row = bv_row[:, :].unsqueeze(1).broadcast_to([S, GB, D]).rearrange("p b (h d) -> p b h d", d=DK)
                            v.tensor_tensor(vaug[u][:, :, :, 0:DK], ps_x[0:S, :].rearrange("p (b h d) -> p b h d", b=GB, d=DK),
                                            row, ALU.add).then_inc(v_ready.sem, 1)
                            if temper:
                                dve.wait_ge(q_ready.sem, q_ready.after(i, u + 1))
                                v.tensor_reduce(qs[u][:, :], q[u][:, :].rearrange("p (b t) -> p b t", b=GB), AX.X, ALU.add)
                                v.tensor_reduce(ks[u][:, :], kT[u][:, :].rearrange("p (b s) -> p b s", b=GB), AX.X, ALU.add).then_inc(small.sem, 1)
                                dve.wait_ge(small.sem, small.after(i, 2 * u + 1))
                                v.tensor_tensor(qk[u][:, :], qs[u][:, :], ks[u][:, :], ALU.mult).then_inc(small.sem, 1)
                                dve.wait_ge(small.sem, small.after(i, 2 * u + 2))
                                v.tensor_tensor(mean_f[u][:, :, :], heads[:, :].unsqueeze(1).broadcast_to([P, GB, H]),
                                                qk[u][:, :].unsqueeze(2).broadcast_to([P, GB, H]), ALU.mult).then_inc(mean_ready.sem, 1)
                        elif kind == "score":
                            dve.wait_ge(s_ready.sem, s_ready.after(i, n + 1))
                            two = ps_s[:, 0:2, 0:6 * S].rearrange("p j (h s) -> p j h s", s=S)
                            rest = ps_s[:, 2, 0:4 * S].rearrange("p (h s) -> p h s", s=S)
                            v.tensor_reduce(m[u][:, b, 0:12].rearrange("p (j h) -> p j h", j=2), two, AX.X, ALU.max)
                            v.tensor_reduce(m[u][:, b, 12:16], rest, AX.X, ALU.max).then_inc(m_ready.sem, 1)
                            dve.wait_ge(m_ready.sem, m_ready.after(i, n + 1))
                            v.tensor_tensor(dist[u][:, b, 0:12, :].rearrange("p (j h) s -> p j h s", j=2), two,
                                            m[u][:, b, 0:12].unsqueeze(2).broadcast_to([P, 12, S]).rearrange("p (j h) s -> p j h s", j=2), ALU.subtract)
                            v.tensor_tensor(dist[u][:, b, 12:16, :], rest, m[u][:, b, 12:16].unsqueeze(2).broadcast_to([P, 4, S]),
                                            ALU.subtract).then_inc(d_ready.sem, 1)
                            if temper and b:
                                sums(i, u, b - 1)
                        elif kind == "temp" and temper:
                            sums(i, u, GB - 1)
                            dve.wait_ge(s2_ready.sem, s2_ready.after(i, (u + 1) * GB))
                            v.reciprocal(z1[u][:, :, :], z1[u][:, :, :]).then_inc(small.sem, 1)
                            dve.wait_ge(small.sem, small.after(i, 5 + 3 * u))
                            v.tensor_tensor(s2[u][:, :, :], s2[u][:, :, :], z1[u][:, :, :], ALU.mult).then_inc(small.sem, 1)
                            dve.wait_ge(small.sem, small.after(i, 6 + 3 * u))
                            v.tensor_tensor(s2[u][:, :, :], s2[u][:, :, :], z1[u][:, :, :], ALU.mult).then_inc(small.sem, 1)
                            dve.wait_ge(small.sem, small.after(i, 7 + 3 * u))
                            v.tensor_scalar(var_f[u][:, :, :], s2[u][:, :, :], 1.0 / (S - 1), -1.0 / (S * (S - 1)), ALU.mult, ALU.add).then_inc(feat_ready.sem, 1)
                            dve.wait_ge(logt_mm.sem, logt_mm.after(i, u + 1))
                            v.tensor_scalar(lt[u][:, :], ps_x[:, 0:GB * H], mb3[:, 0:1], LOG_T_MIN, ALU.add, ALU.max).then_inc(lt_ready.sem, 1)
                            dve.wait_ge(lt_ready.sem, lt_ready.after(i, 2 * u + 1))
                            v.tensor_scalar(lt[u][:, :], lt[u][:, :], LOG_T_MAX, None, ALU.min).then_inc(lt_ready.sem, 1)
                        elif kind == "attend":
                            for c in (1, 3):
                                dve.wait_ge(t_mm[1].sem, t_mm[1].after(i, 2 * n + c // 2 + 1))
                                if c == 1:
                                    dve.wait_ge(pv_mm.sem, pv_mm.after(i, n - 1))
                                v.tensor_scalar(pt[n % 2][:, 4 * c * T:4 * (c + 1) * T], ps_t[1][0:S, :], 0.0, None, ALU.max).then_inc(pt_ready[1].sem, 1)
                            dve.wait_ge(pv_mm.sem, pv_mm.after(i, n + 1))
                            heads_out = ps_o[:, 0:H * (DK + 1)].rearrange("p (h d) -> p h d", d=DK + 1)
                            v.tensor_scalar(zmax[n % 2][:, :], heads_out[:, :, DK:DK + 1].rearrange("p h a -> p (h a)"), 1e-30, None, ALU.max).then_inc(z_ready.sem, 1)
                            dve.wait_ge(z_ready.sem, z_ready.after(i, n + 1))
                            v.reciprocal(rz[n % 2][:, :], zmax[n % 2][:, :]).then_inc(rz_ready.sem, 1)
                            dve.wait_ge(rz_ready.sem, rz_ready.after(i, n + 1))
                            v.tensor_tensor(o[u][:, b, :, :], heads_out[:, :, 0:DK], rz[n % 2][:, :].unsqueeze(2).broadcast_to([P, H, DK]),
                                            ALU.mult).then_inc(o_ready.sem, 1)
                        elif kind == "out":
                            dve.wait_ge(wo_mm.sem, wo_mm.after(i, u + 1))
                            v.scalar_tensor_tensor(y[:, :], ps_n[:, :], bias["o"][:, 0:1], group_of(xT, i, u, U), ALU.add, ALU.add).then_inc(norm.y_ready.sem, 1)
                            norm.centre(nc, dve, i, u)
                            norm.divide(nc, dve, i, u, group_of(xT, i, u, U), xT_ready)
        t.clear_counts()


class DoubleNorm:

    def __init__(self, t, const, name, per, y, sq, logs, inv, bank, gamma, beta):
        self.own = Norm(t, const, f"{name}_own", per, y, sq, logs, inv, bank)
        self.stream = Norm(t, const, f"{name}_str", per, y, sq, logs, inv, bank)
        self.gained = t.count(f"{name}_gained", per)
        self.gamma, self.beta = gamma, beta

    def give(self, engine):
        self.own.log_ready.give(engine)
        self.stream.log_ready.give(engine)

    def tensor(self, nc, pe, i, n):
        self.own.tensor(nc, pe, i, n)
        self.stream.tensor(nc, pe, i, n)

    def scalar(self, nc, act, i, n):
        self.own.scalar(nc, act, i, n)
        self.stream.scalar(nc, act, i, n)

    def vector(self, nc, dve, i, n, x, out, done):
        y = self.own.y[:, :]
        self.own.centre(nc, dve, i, n)
        dve.wait_ge(self.own.inv_ready.sem, self.own.inv_ready.after(i, n + 1))
        nc.vector.scalar_tensor_tensor(y, y, self.gamma[:, 0:1], self.own.inv[:, :], ALU.mult, ALU.mult).then_inc(self.gained.sem, 1)
        dve.wait_ge(self.gained.sem, self.gained.after(i, n + 1))
        nc.vector.scalar_tensor_tensor(y, y, self.beta[:, 0:1], x, ALU.add, ALU.add).then_inc(self.stream.y_ready.sem, 1)
        self.stream.centre(nc, dve, i, n)
        self.stream.divide(nc, dve, i, n, out, done)


class Chain:

    def __init__(self, t, name, engine):
        self.done, self.engine, self.n = t.count(name), engine, 0

    def __call__(self, instruction):
        instruction.then_inc(self.done.sem, 1)
        self.n += 1
        self.engine.wait_ge(self.done.sem, self.n)


TILES, CLUSTERS, TPC = 64, 8, 8
COMP, GRID, KNOTS = 32, 16, 8


def first_max_one_hot(link, v, g, top, cand, iota, n):
    wide = lambda a: a.unsqueeze(2).broadcast_to([P, B, n])
    link(v.tensor_reduce(top, g, AX.X, ALU.max))
    link(v.tensor_tensor(cand, g, wide(top), ALU.is_equal))
    link(v.scalar_tensor_tensor(cand, cand, -float(n), iota, ALU.mult, ALU.add))
    link(v.tensor_reduce(top, cand, AX.X, ALU.min))
    link(v.tensor_tensor(cand, cand, wide(top), ALU.is_equal))


def tile_ffn(nc, const, xT, raw, knots, temp, cw1, cb1, cw2, cb2, sw1, sb1, sw2, sb2, dirs, gamma, beta, scale):
    with ExitStack() as ctx:
        t = Tools(ctx, nc, "ffn")
        U = 2
        ITER = NG // U
        NS = CLUSTERS + TILES
        TAB = 3 * GRID + GRID + 1
        rawT = t.sb("rawT", [P, TILES])
        sig = t.sb("sig", [P, NS])
        q = t.sb("q", [P, TILES])
        lt = t.sb("lt", [P, TILES])
        csum = t.sb("csum", [P, CLUSTERS])
        cneg = t.sb("cneg", [P, CLUSTERS])
        w1 = t.sb("w1", [P, COMP])
        b1 = t.sb("b1", [COMP, 1])
        w2 = t.sb("w2", [COMP, 2])
        b2 = t.sb("b2", [P, 2])
        table = t.sb("table", [TILES, TAB])
        dir_sb = t.sb("dirs", [TILES, D])
        knot = t.sb("knot", [P, KNOTS])
        slope = t.sb("slope", [P, KNOTS])
        nit = t.sb("nit", [P, 1])
        scale_c = t.sb("scale", [P, 1])
        gamma_c, beta_c = t.sb("gamma", [P, 1]), t.sb("beta", [P, 1])
        iota_i = t.sb("iota_i", [P, B, TPC], I32)
        iota = t.sb("iota", [P, B, TPC])
        scores = t.sb("scores", [P, B, NS])
        comp = t.sb("comp", [P, B, 2])
        xs = [t.sb(f"xs{u}", [P, GROUP]) for u in range(U)]
        hid = [t.sb(f"hid{u}", [COMP, GROUP]) for u in range(U)]
        e = t.sb("e", [P, B * 8])
        low = t.sb("low", [P, B * 8])
        frac = t.sb("frac", [P, B * 8])
        term = t.sb("term", [P, B * 8])
        inc = t.sb("inc", [P, B * 8])
        gates = t.sb("gates", [P, B * 8])
        top = t.sb("top", [P, B])
        cluster = t.sb("cluster", [P, B, CLUSTERS])
        local = t.sb("local", [P, B, TPC])
        picked = t.sb("picked", [P, B, CLUSTERS, TPC])
        mine = t.sb("mine", [P, B, TPC])
        oh = [t.sb(f"oh{u}", [P, GB, P]) for u in range(U)]
        ohm = [t.sb(f"ohm{u}", [P, GB, P]) for u in range(U)]
        ohT = [t.sb(f"ohT{u}", [TILES, GROUP]) for u in range(U)]
        ohmT = [t.sb(f"ohmT{u}", [TILES, GROUP]) for u in range(U)]
        ha = t.sb("ha", [P, GB, GRID])
        hb = t.sb("hb", [P, GB, GRID])
        mag = t.sb("mag", [P, GB])
        y, sq = t.sb("y", [P, GROUP]), t.sb("sq", [P, GROUP])
        logs, inv = t.sb("logs", [P, GROUP]), t.sb("inv", [P, GROUP])
        ps_a = [t.ps(f"bank_a{u}", [P, 512]) for u in range(U)]
        ps_b = [t.ps(f"bank_b{u}", [P, 512]) for u in range(U)]
        ps_c = [t.ps(f"bank_c{u}", [P, 512]) for u in range(U)]
        ps_n = t.ps("norm", [P, 512])

        load_transposed(nc, const, "ffn_sig", [(rawT[:, :], raw)], ps_a)
        loaded = t.count("loaded", weight=DMA)
        N_LOADS = 15
        table_zeroed = t.count("table_zeroed")
        xs_ready = t.count("xs_ready", U)
        sc_mm = t.count("sc_mm", U)
        sc_kept = t.count("sc_kept", U, credits=U)
        hid_mm = t.count("hid_mm", U)
        hid_ready = t.count("hid_ready", U, credits=U)
        comp_mm = t.count("comp_mm", U)
        comp_kept = t.count("comp_kept", U, credits=U)
        sig_ready = t.count("sig_ready")
        iota_made = t.count("iota_made")
        with nc.Block() as block:

            @block.sync
            def _(sp):
                col = lambda a: a.rearrange("(p a) -> p a", a=1)
                loads = [(w1[:, :], cw1), (b1[:, :], col(cb1)), (w2[:, :], cw2), (b2[:, :], cb2.partition_broadcast(P)),
                         (knot[:, :], knots.partition_broadcast(P)), (nit[:, :], temp.partition_broadcast(P)),
                         (scale_c[:, :], scale.partition_broadcast(P)), (gamma_c[:, :], col(gamma)), (beta_c[:, :], col(beta)),
                         (dir_sb[:, :], dirs), (table[:, 0:2 * GRID], sw1.rearrange("n i g -> n (i g)")),
                         (table[:, 2 * GRID:3 * GRID], sb1), (table[:, 3 * GRID:4 * GRID], sw2.rearrange("n g a -> n (g a)")),
                         (table[:, 4 * GRID:], sb2)]
                for dst, src in loads:
                    sp.dma_start(dst, src).then_inc(loaded.sem, DMA)

            @block.gpsimd
            def _(pool):
                pool.iota(iota_i[:, :, :], pattern=[[0, B], [1, TPC]], base=0, channel_multiplier=0).then_inc(iota_made.sem, 1)

            @block.vector
            def _(dve):
                v = nc.vector
                for a in (*oh, *ohm):
                    v.memset(a[:, :, TILES:], 0.0)
                link = Chain(t, "setup", dve)
                for c in (sc_kept, hid_ready, comp_kept):
                    c.give(dve)
                signs = sig[:, CLUSTERS:]
                link(v.tensor_scalar(q[:, :], rawT[:, :], 0.3, None, ALU.is_gt))
                link(v.tensor_scalar(lt[:, :], rawT[:, :], -0.3, None, ALU.is_lt))
                link(v.tensor_tensor(q[:, :], q[:, :], lt[:, :], ALU.subtract))
                link(v.tensor_tensor(q[:, :], q[:, :], rawT[:, :], ALU.subtract))
                link(v.tensor_tensor(signs, rawT[:, :], q[:, :], ALU.add))
                link(v.tensor_reduce(csum[:, :], signs.rearrange("p (c t) -> p c t", t=TPC), AX.X, ALU.add))
                link(v.tensor_scalar(cneg[:, :], csum[:, :], 0.0, None, ALU.is_lt))
                link(v.tensor_scalar(csum[:, :], csum[:, :], 0.0, None, ALU.is_gt))
                link(v.tensor_tensor(sig[:, 0:CLUSTERS], csum[:, :], cneg[:, :], ALU.subtract))
                dve.wait_ge(loaded.sem, 14 * DMA)
                link(v.tensor_tensor(slope[:, 0:KNOTS - 1], knot[:, 1:KNOTS], knot[:, 0:KNOTS - 1], ALU.subtract))
                link(v.tensor_scalar(nit[:, :], nit[:, :], 1e-6, None, ALU.add))
                link(v.reciprocal(nit[:, :], nit[:, :]))
                link(v.tensor_scalar(nit[:, :], nit[:, :], -1.0, None, ALU.mult))
                dve.wait_ge(iota_made.sem, 1)
                link(v.tensor_copy(iota[:, :, :], iota_i[:, :, :]))

        with nc.Block() as block:

            @block.tensor
            def _(pe):
                mm = nc.tensor.matmul
                with pe.Fori(0, ITER) as i:
                    for u in range(U):
                        pe.wait_ge(xs_ready.sem, xs_ready.after(i, u + 1))
                        pe.wait_ge(sc_kept.sem, sc_kept.free(i, u))
                        for b in range(GB):
                            last = mm(ps_a[u][:, b * NS:(b + 1) * NS], xs[u][:, b * T:(b + 1) * T], sig[:, :], start=True, stop=True)
                        last.then_inc(sc_mm.sem, 1)
                        pe.wait_ge(hid_ready.sem, hid_ready.free(i, u))
                        mm(ps_b[u][0:COMP, :], w1[:, :], xs[u][:, :], start=True, stop=True).then_inc(hid_mm.sem, 1)
                    for u in range(U):
                        pe.wait_ge(hid_ready.sem, hid_ready.after(i, u + 1))
                        pe.wait_ge(comp_kept.sem, comp_kept.free(i, u))
                        for b in range(GB):
                            last = mm(ps_c[u][:, 2 * b:2 * b + 2], hid[u][:, b * T:(b + 1) * T], w2[:, :], start=True, stop=True)
                        last.then_inc(comp_mm.sem, 1)

            @block.scalar
            def _(act):
                f = nc.scalar.activation
                with act.Fori(0, ITER) as i:
                    for u in range(U):
                        act.wait_ge(hid_ready.sem, hid_ready.free(i, u))
                        f(xs[u][:, :], group_of(xT, i, u, U), ACT.Copy).then_inc(xs_ready.sem, 1)
                    for u in range(U):
                        act.wait_ge(hid_mm.sem, hid_mm.after(i, u + 1))
                        act.wait_ge(comp_kept.sem, comp_kept.free(i, u))
                        f(hid[u][:, :], ps_b[u][0:COMP, :], ACT.Gelu, bias=b1[:, :]).then_inc(hid_ready.sem, 1)

            @block.vector
            def _(dve):
                v = nc.vector
                with dve.Fori(0, ITER) as i:
                    for u in range(U):
                        first = i * (U * GB) + u * GB
                        dve.wait_ge(sc_mm.sem, sc_mm.after(i, u + 1))
                        v.tensor_copy(scores[:, bass.ds(first, GB), :], ps_a[u][:, 0:GB * NS].rearrange("p (b n) -> p b n", b=GB)).then_inc(sc_kept.sem, 1)
                    for u in range(U):
                        first = i * (U * GB) + u * GB
                        dve.wait_ge(comp_mm.sem, comp_mm.after(i, u + 1))
                        v.tensor_tensor(comp[:, bass.ds(first, GB), :], ps_c[u][:, 0:GB * 2].rearrange("p (b n) -> p b n", b=GB),
                                        b2[:, :].unsqueeze(1).broadcast_to([P, GB, 2]), ALU.add).then_inc(comp_kept.sem, 1)

        exp_asked = t.count("exp_asked")
        exp_ready = t.count("exp_ready")
        with nc.Block() as block:

            @block.scalar
            def _(act):
                f = nc.scalar.activation
                f(comp[:, :, :], comp[:, :, :], ACT.Tanh)
                e3 = e[:, :].rearrange("p (b n) -> p b n", n=8)
                f(e3, scores[:, :, 0:CLUSTERS], ACT.Exp, scale=nit[:, :]).then_inc(exp_ready.sem, 1)
                act.wait_ge(exp_asked.sem, 1)
                f(e3, mine[:, :, :], ACT.Exp, scale=nit[:, :]).then_inc(exp_ready.sem, 1)

            @block.vector
            def _(dve):
                v = nc.vector
                link = Chain(t, "route", dve)

                def calibrate(n):
                    dve.wait_ge(exp_ready.sem, n)
                    link(v.tensor_scalar(e[:, :], e[:, :], 1.0, None, ALU.add))
                    link(v.reciprocal(e[:, :], e[:, :]))
                    link(v.tensor_scalar(e[:, :], e[:, :], float(KNOTS - 1), None, ALU.mult))
                    link(v.tensor_scalar(low[:, :], e[:, :], 1.0, None, ALU.is_ge))
                    for k in range(2, KNOTS - 1):
                        link(v.scalar_tensor_tensor(low[:, :], e[:, :], float(k), low[:, :], ALU.is_ge, ALU.add))
                    v.tensor_tensor(frac[:, :], e[:, :], low[:, :], ALU.subtract)
                    v.tensor_scalar(gates[:, :], low[:, :], 0.0, knot[:, 0:1], ALU.is_equal, ALU.mult)
                    link(v.tensor_scalar(inc[:, :], low[:, :], 0.0, slope[:, 0:1], ALU.is_equal, ALU.mult))
                    for k in range(1, KNOTS - 1):
                        for acc, of in ((gates, knot), (inc, slope)):
                            link(v.tensor_scalar(term[:, :], low[:, :], float(k), of[:, k:k + 1], ALU.is_equal, ALU.mult))
                            link(v.tensor_tensor(acc[:, :], acc[:, :], term[:, :], ALU.add))
                    link(v.tensor_tensor(inc[:, :], inc[:, :], frac[:, :], ALU.mult))
                    link(v.tensor_tensor(gates[:, :], gates[:, :], inc[:, :], ALU.add))

                g3 = gates[:, :].rearrange("p (b n) -> p b n", n=8)
                calibrate(1)
                first_max_one_hot(link, v, g3, top[:, :], cluster[:, :, :], iota[:, :, :], CLUSTERS)
                link(v.tensor_tensor(picked[:, :, :, :], scores[:, :, CLUSTERS:].rearrange("p b (c j) -> p b c j", c=CLUSTERS),
                                     cluster[:, :, :].unsqueeze(3).broadcast_to([P, B, CLUSTERS, TPC]), ALU.mult))
                v.tensor_reduce(mine[:, :, :], picked[:, :, :, :].rearrange("p b c j -> p b j c"), AX.X, ALU.add).then_inc(exp_asked.sem, 1)
                calibrate(2)
                first_max_one_hot(link, v, g3, top[:, :], local[:, :, :], iota[:, :, :], TPC)

        oh_ready = t.count("oh_ready", U)
        ohT_mm = t.count("ohT_mm", U)
        ohT_ready = t.count("ohT_ready", U)
        row_mm = t.count("row_mm", U)
        mag_steps = 8
        hh = t.count("hh", mag_steps * U)
        ohm_ready = t.count("ohm_ready", U)
        ohmT_mm = t.count("ohmT_mm", U)
        ohmT_ready = t.count("ohmT_ready", U)
        dir_mm = t.count("dir_mm", U)
        xT_ready = t.count("xT_ready", U)
        norm = DoubleNorm(t, const, "ln", U, y, sq, logs, inv, ps_n, gamma_c, beta_c)
        a_free = t.count("a_free", U, credits=U)
        with nc.Block() as block:

            @block.tensor
            def _(pe):
                mm, turn = nc.tensor.matmul, nc.tensor.transpose
                with pe.Fori(0, ITER) as i:
                    for u in range(U):
                        pe.wait_ge(oh_ready.sem, oh_ready.after(i, u + 1))
                        pe.wait_ge(a_free.sem, a_free.free(i, u))
                        for b in range(GB):
                            last = turn(ps_a[u][:, b * T:(b + 1) * T], oh[u][:, b, :], const["ident"][:, :])
                        last.then_inc(ohT_mm.sem, 1)
                    for u in range(U):
                        pe.wait_ge(ohT_ready.sem, ohT_ready.after(i, u + 1))
                        for b in range(GB):
                            last = mm(ps_b[u][:, b * TAB:(b + 1) * TAB], ohT[u][:, b * T:(b + 1) * T], table[:, :], start=True, stop=True)
                        last.then_inc(row_mm.sem, 1)
                    for u in range(U):
                        pe.wait_ge(ohm_ready.sem, ohm_ready.after(i, u + 1))
                        for b in range(GB):
                            last = turn(ps_c[u][:, b * T:(b + 1) * T], ohm[u][:, b, :], const["ident"][:, :])
                        last.then_inc(ohmT_mm.sem, 1)
                    for u in range(U):
                        pe.wait_ge(ohmT_ready.sem, ohmT_ready.after(i, u + 1))
                        mm(ps_a[u][:, :], dir_sb[:, :], ohmT[u][:, :], start=True, stop=True).then_inc(dir_mm.sem, 1)
                        norm.tensor(nc, pe, i, u)

            @block.scalar
            def _(act):
                f = nc.scalar.activation
                with act.Fori(0, ITER) as i:
                    for u in range(U):
                        act.wait_ge(ohT_mm.sem, ohT_mm.after(i, u + 1))
                        f(ohT[u][:, :], ps_a[u][0:TILES, :], ACT.Copy).then_inc(ohT_ready.sem, 1)
                    for u in range(U):
                        act.wait_ge(ohmT_mm.sem, ohmT_mm.after(i, u + 1))
                        f(ohmT[u][:, :], ps_c[u][0:TILES, :], ACT.Copy).then_inc(ohmT_ready.sem, 1)
                    for u in range(U):
                        norm.scalar(nc, act, i, u)

            @block.vector
            def _(dve):
                v = nc.vector
                a_free.give(dve)
                norm.give(dve)
                with dve.Fori(0, ITER) as i:
                    for u in range(U):
                        first = i * (U * GB) + u * GB
                        shape = [P, GB, CLUSTERS, TPC]
                        v.tensor_tensor(oh[u][:, :, 0:TILES].rearrange("p b (c j) -> p b c j", c=CLUSTERS),
                                        cluster[:, bass.ds(first, GB), :].unsqueeze(3).broadcast_to(shape),
                                        local[:, bass.ds(first, GB), :].unsqueeze(2).broadcast_to(shape), ALU.mult).then_inc(oh_ready.sem, 1)
                    for u in range(U):
                        first = i * (U * GB) + u * GB
                        rows = ps_b[u][:, 0:GB * TAB].rearrange("p (b n) -> p b n", b=GB)
                        dve.wait_ge(row_mm.sem, row_mm.after(i, u + 1))
                        step = [u * mag_steps]

                        def link(instruction):
                            instruction.then_inc(hh.sem, 1)
                            step[0] += 1
                            dve.wait_ge(hh.sem, hh.after(i, step[0]))

                        c = lambda n: comp[:, bass.ds(first, GB), n:n + 1].broadcast_to([P, GB, GRID])
                        v.tensor_tensor(ha[:, :, :], rows[:, :, 0:GRID], c(0), ALU.mult)
                        link(v.tensor_tensor(hb[:, :, :], rows[:, :, GRID:2 * GRID], c(1), ALU.mult))
                        link(v.tensor_tensor(ha[:, :, :], ha[:, :, :], hb[:, :, :], ALU.add))
                        link(v.tensor_tensor(ha[:, :, :], ha[:, :, :], rows[:, :, 2 * GRID:3 * GRID], ALU.add))
                        link(v.tensor_scalar(ha[:, :, :], ha[:, :, :], 0.0, None, ALU.max))
                        link(v.tensor_tensor(ha[:, :, :], ha[:, :, :], rows[:, :, 3 * GRID:4 * GRID], ALU.mult))
                        link(v.tensor_reduce(mag[:, :], ha[:, :, :], AX.X, ALU.add))
                        link(v.tensor_tensor(mag[:, :], mag[:, :], rows[:, :, 4 * GRID:TAB].rearrange("p b a -> p (b a)"), ALU.add))
                        link(v.tensor_scalar(mag[:, :], mag[:, :], scale_c[:, 0:1], None, ALU.mult))
                        v.tensor_tensor(ohm[u][:, :, 0:TILES], oh[u][:, :, 0:TILES], mag[:, :].unsqueeze(2).broadcast_to([P, GB, TILES]), ALU.mult).then_inc(ohm_ready.sem, 1)
                    for u in range(U):
                        x = group_of(xT, i, u, U)
                        dve.wait_ge(dir_mm.sem, dir_mm.after(i, u + 1))
                        v.tensor_tensor(y[:, :], ps_a[u][:, :], x, ALU.add).then_inc(norm.own.y_ready.sem, 1)
                        dve.wait_ge(norm.own.y_ready.sem, norm.own.y_ready.after(i, u + 1))
                        dve.sem_inc(a_free.sem, 1)
                        norm.vector(nc, dve, i, u, x, x, xT_ready)
                        dve.wait_ge(xT_ready.sem, xT_ready.after(i, u + 1))
        t.clear_counts()


HD = 64
INNER = H * HD
PAIRS = H // 2
HALF = 4


def self_attention(nc, const, xT, scale, wq, bq, wk, bk, wv, bv, wo, bo, gamma, beta):
    with ExitStack() as ctx:
        t = Tools(ctx, nc, "self")
        HALVES = GB * 2
        w = {n: t.sb(f"w_{n}", [P, INNER]) for n in "qkvo"}
        bq_c, bk_c, sc_c = t.sb("bq", [P, PAIRS]), t.sb("bk", [P, PAIRS]), t.sb("scale", [P, PAIRS])
        bo_c, gamma_c, beta_c = t.sb("bo", [P, 1]), t.sb("gamma", [P, 1]), t.sb("beta", [P, 1])
        bv_row = t.sb("bv_row", [P, INNER])
        xs = t.sb("xs", [P, GROUP])
        qT, kT = t.sb("qT", [P, PAIRS, GROUP]), t.sb("kT", [P, PAIRS, GROUP])
        vs = t.sb("v", [P, GB, INNER])
        neg = [t.sb(f"neg{r}", [P, 2, HALF]) for r in range(2)]
        probs = [t.sb(f"probs{r}", [P, 2, HALF, T]) for r in range(2)]
        z = [t.sb(f"z{r}", [P, 2, HALF]) for r in range(2)]
        rz = [t.sb(f"rz{r}", [P, 2, HALF]) for r in range(2)]
        pt = [t.sb(f"pt{r}", [P, 2, HALF, T]) for r in range(2)]
        o = [t.sb(f"o{r}", [P, HALF, 2, HD]) for r in range(2)]
        oT = t.sb("oT", [P, PAIRS, GROUP])
        y, sq = t.sb("y", [P, GROUP]), t.sb("sq", [P, GROUP])
        logs, inv = t.sb("logs", [P, GROUP]), t.sb("inv", [P, GROUP])
        ps_s = [t.ps(f"scores{r}", [P, 2, 512]) for r in range(2)]
        ps_t = [t.ps(f"turned{r}", [P, 512]) for r in range(2)]
        ps_o = t.ps("out", [P, 512])
        ps_n = t.ps("norm", [P, 512])

        load_transposed(nc, const, "self_w", [(w[n][:, :], a) for n, a in zip("qkvo", (wq, wk, wv, wo))], ps_t)
        loaded = t.count("loaded", weight=DMA)
        scaled = t.count("scaled")
        with nc.Block() as block:

            @block.sync
            def _(sp):
                cols = lambda a: a.rearrange("(n p) -> p n", p=P)
                loads = [(bq_c[:, :], cols(bq)), (bk_c[:, :], cols(bk)), (bo_c[:, :], cols(bo)), (gamma_c[:, :], cols(gamma)),
                         (beta_c[:, :], cols(beta)), (bv_row[:, :], bv.partition_broadcast(P)),
                         (sc_c[0:HD, :], scale.rearrange("(c a) -> a c", a=2)[0:1, :].broadcast_to([HD, PAIRS])),
                         (sc_c[HD:P, :], scale.rearrange("(c a) -> a c", a=2)[1:2, :].broadcast_to([HD, PAIRS]))]
                for dst, src in loads:
                    sp.dma_start(dst, src, allow_slow_non_contiguous=True).then_inc(loaded.sem, DMA)

            @block.vector
            def _(dve):
                dve.wait_ge(loaded.sem, 8 * DMA)
                nc.vector.tensor_scalar(sc_c[:, :], sc_c[:, :], HD ** -0.5, None, ALU.mult).then_inc(scaled.sem, 1)
                dve.wait_ge(scaled.sem, 1)
                nc.vector.tensor_tensor(bq_c[:, :], bq_c[:, :], sc_c[:, :], ALU.mult)

        NQK = 2 * PAIRS
        NT_ = NQK // 2 + HALVES
        xs_ready = t.count("xs_ready")
        fill = [t.count(f"fill{r}", NT_) for r in range(2)]
        kept = [t.count(f"kept{r}", NT_, credits=1) for r in range(2)]
        v_mm = t.count("v_mm", GB)
        v_ready = t.count("v_ready", GB)
        s_mm = t.count("s_mm", HALVES)
        max_ready = t.count("max_ready", HALVES)
        neg_ready = t.count("neg_ready", HALVES)
        p_ready = t.count("p_ready", HALVES, credits=2)
        pv_mm = t.count("pv_mm", HALVES, credits=2)
        rz_ready = t.count("rz_ready", HALVES)
        o_ready = t.count("o_ready", HALVES, credits=1)
        ot_mm = t.count("ot_mm", HALVES, credits=2)
        ot_ready = t.count("ot_ready", HALVES, credits=1)
        wo_mm = t.count("wo_mm")
        xT_ready = t.count("xT_ready", credits=1)
        norm = DoubleNorm(t, const, "ln", 1, y, sq, logs, inv, ps_n, gamma_c, beta_c)

        ORDER = [("project", 0), ("scores", 0)]
        for k in range(HALVES):
            if k + 1 < HALVES:
                ORDER.append(("scores", k + 1))
            ORDER.append(("attend", k))
            if k:
                ORDER.append(("turn", k - 1))
        ORDER += [("turn", HALVES - 1), ("out", 0)]

        with nc.Block() as block:

            @block.tensor
            def _(pe):
                mm, turn = nc.tensor.matmul, nc.tensor.transpose
                ident = const["ident"]
                with pe.Fori(0, NG) as i:
                    for kind, k in ORDER:
                        b, half = k // 2, k % 2
                        if kind == "project":
                            pe.wait_ge(xs_ready.sem, xs_ready.after(i))
                            for n in range(NQK):
                                r = n % 2
                                wt = w["q" if n < PAIRS else "k"]
                                pe.wait_ge(kept[r].sem, kept[r].free(i, n // 2))
                                c = n % PAIRS
                                mm(ps_t[r][:, :], wt[:, c * P:(c + 1) * P], xs[:, :], start=True, stop=True).then_inc(fill[r].sem, 1)
                            for c in range(GB):
                                if c < 2:
                                    pe.wait_ge(p_ready.sem, p_ready.free(i, c))
                                else:
                                    pe.wait_ge(v_ready.sem, v_ready.after(i, c - 1))
                                for j in range(2):
                                    last = mm(ps_s[c % 2][:, j, :], xs[:, c * T:(c + 1) * T], w["v"][:, j * 512:(j + 1) * 512], start=True, stop=True)
                                last.then_inc(v_mm.sem, 1)
                        elif kind == "scores":
                            if k < 2:
                                pe.wait_ge(v_ready.sem, v_ready.after(i, GB - 1 + k))
                                if k == 0:
                                    for r in range(2):
                                        pe.wait_ge(kept[r].sem, kept[r].after(i, NQK // 2))
                            else:
                                pe.wait_ge(p_ready.sem, p_ready.free(i, k))
                            for j in range(HALF):
                                c = half * HALF + j
                                for e in range(2):
                                    rows = slice(e * HD, (e + 1) * HD)
                                    last = mm(ps_s[k % 2][:, e, j * T:(j + 1) * T], qT[rows, c, b * T:(b + 1) * T],
                                              kT[rows, c, b * T:(b + 1) * T], start=True, stop=True)
                            last.then_inc(s_mm.sem, 1)
                        elif kind == "attend":
                            pe.wait_ge(p_ready.sem, p_ready.after(i, k + 1))
                            for e in range(2):
                                pe.wait_ge(kept[e].sem, kept[e].free(i, NQK // 2 + k))
                                for j in range(HALF):
                                    last = turn(ps_t[e][:, j * T:(j + 1) * T], probs[k % 2][:, e, j, :], ident[:, :])
                                last.then_inc(fill[e].sem, 1)
                            for e in range(2):
                                pe.wait_ge(kept[e].sem, kept[e].after(i, NQK // 2 + k + 1))
                            pe.wait_ge(o_ready.sem, o_ready.free(i, k))
                            for j in range(HALF):
                                for e in range(2):
                                    head = 2 * (half * HALF + j) + e
                                    last = mm(ps_o[:, (2 * j + e) * HD:(2 * j + e + 1) * HD], pt[k % 2][:, e, j, :],
                                              vs[:, b, head * HD:(head + 1) * HD], start=True, stop=True)
                            last.then_inc(pv_mm.sem, 1)
                        elif kind == "turn":
                            pe.wait_ge(o_ready.sem, o_ready.after(i, k + 1))
                            if k == 0:
                                pe.wait_ge(norm.stream.log_ready.sem, norm.stream.log_ready.free(i))
                            pe.wait_ge(ot_ready.sem, ot_ready.free(i, k))
                            for j in range(HALF):
                                last = turn(ps_n[:, j * T:(j + 1) * T], o[k % 2][:, j, :, :].rearrange("p e d -> p (e d)"), ident[:, :])
                            last.then_inc(ot_mm.sem, 1)
                        else:
                            pe.wait_ge(ot_ready.sem, ot_ready.after(i, HALVES))
                            for c in range(PAIRS):
                                last = mm(ps_n[:, :], w["o"][:, c * P:(c + 1) * P], oT[:, c, :], start=(c == 0), stop=(c == PAIRS - 1))
                            last.then_inc(wo_mm.sem, 1)
                            norm.tensor(nc, pe, i, 0)

            @block.scalar
            def _(act):
                f = nc.scalar.activation
                with act.Fori(0, NG) as i:
                    for kind, k in ORDER:
                        b, half = k // 2, k % 2
                        if kind == "project":
                            f(xs[:, :], group_of(xT, i, 0, 1), ACT.Copy).then_inc(xs_ready.sem, 1)
                            for n in range(0, NQK, 2):
                                c = n % PAIRS
                                act.wait_ge(fill[0].sem, fill[0].after(i, n // 2 + 1))
                                if n < PAIRS:
                                    f(qT[:, c, :], ps_t[0][:, :], ACT.Identity, bias=bq_c[:, c:c + 1], scale=sc_c[:, c:c + 1]).then_inc(kept[0].sem, 1)
                                else:
                                    f(kT[:, c, :], ps_t[0][:, :], ACT.Identity, bias=bk_c[:, c:c + 1]).then_inc(kept[0].sem, 1)
                        elif kind == "scores":
                            act.wait_ge(neg_ready.sem, neg_ready.after(i, k + 1))
                            act.wait_ge(pv_mm.sem, pv_mm.after(i, k - 1))
                            for e in range(2):
                                for j in range(HALF):
                                    last = f(probs[k % 2][:, e, j, :], ps_s[k % 2][:, e, j * T:(j + 1) * T], ACT.Exp,
                                             bias=neg[k % 2][:, e, j:j + 1], accum_out=z[k % 2][:, e, j:j + 1])
                            last.then_inc(p_ready.sem, 1)
                        elif kind == "attend":
                            act.wait_ge(fill[0].sem, fill[0].after(i, NQK // 2 + k + 1))
                            f(pt[k % 2][:, 0, :, :].rearrange("p j t -> p (j t)"), ps_t[0][:, :], ACT.Copy).then_inc(kept[0].sem, 1)
                        elif kind == "turn":
                            act.wait_ge(ot_mm.sem, ot_mm.after(i, k + 1))
                            f(oT[:, half * HALF:(half + 1) * HALF, b * T:(b + 1) * T], ps_n[:, :].rearrange("p (j t) -> p j t", t=T),
                              ACT.Copy).then_inc(ot_ready.sem, 1)
                        else:
                            norm.scalar(nc, act, i, 0)

            @block.vector
            def _(dve):
                v = nc.vector
                for c in (*kept, p_ready, pv_mm, o_ready, ot_mm, ot_ready, xT_ready, norm):
                    c.give(dve)
                with dve.Fori(0, NG) as i:
                    for kind, k in ORDER:
                        b, half = k // 2, k % 2
                        if kind == "project":
                            for n in range(1, NQK, 2):
                                c = n % PAIRS
                                dve.wait_ge(fill[1].sem, fill[1].after(i, n // 2 + 1))
                                if n < PAIRS:
                                    v.tensor_scalar(qT[:, c, :], ps_t[1][:, :], sc_c[:, c:c + 1], bq_c[:, c:c + 1], ALU.mult, ALU.add).then_inc(kept[1].sem, 1)
                                else:
                                    v.tensor_scalar(kT[:, c, :], ps_t[1][:, :], bk_c[:, c:c + 1], None, ALU.add).then_inc(kept[1].sem, 1)
                            for c in range(GB):
                                dve.wait_ge(v_mm.sem, v_mm.after(i, c + 1))
                                v.tensor_tensor(vs[:, c, :], ps_s[c % 2][:, :, :].rearrange("p j n -> p (j n)"), bv_row[:, :], ALU.add).then_inc(v_ready.sem, 1)
                        elif kind == "scores":
                            dve.wait_ge(s_mm.sem, s_mm.after(i, k + 1))
                            v.tensor_reduce(neg[k % 2][:, :, :], ps_s[k % 2][:, :, :].rearrange("p e (j t) -> p e j t", t=T), AX.X, ALU.max).then_inc(max_ready.sem, 1)
                            dve.wait_ge(max_ready.sem, max_ready.after(i, k + 1))
                            v.tensor_scalar(neg[k % 2][:, :, :], neg[k % 2][:, :, :], -1.0, None, ALU.mult).then_inc(neg_ready.sem, 1)
                        elif kind == "attend":
                            dve.wait_ge(fill[1].sem, fill[1].after(i, NQK // 2 + k + 1))
                            v.tensor_copy(pt[k % 2][:, 1, :, :].rearrange("p j t -> p (j t)"), ps_t[1][:, :]).then_inc(kept[1].sem, 1)
                            dve.wait_ge(p_ready.sem, p_ready.after(i, k + 1))
                            v.reciprocal(rz[k % 2][:, :, :], z[k % 2][:, :, :]).then_inc(rz_ready.sem, 1)
                            dve.wait_ge(rz_ready.sem, rz_ready.after(i, k + 1))
                            dve.wait_ge(pv_mm.sem, pv_mm.after(i, k + 1))
                            dve.wait_ge(ot_mm.sem, ot_mm.after(i, k - 1))
                            v.tensor_tensor(o[k % 2][:, :, :, :], ps_o[:, :].rearrange("p (j e d) -> p j e d", e=2, d=HD),
                                            rz[k % 2][:, :, :].rearrange("p e j -> p j e").unsqueeze(3).broadcast_to([P, HALF, 2, HD]),
                                            ALU.mult).then_inc(o_ready.sem, 1)
                        elif kind == "out":
                            x = group_of(xT, i, 0, 1)
                            dve.wait_ge(wo_mm.sem, wo_mm.after(i))
                            v.scalar_tensor_tensor(y[:, :], ps_n[:, :], bo_c[:, 0:1], x, ALU.add, ALU.add).then_inc(norm.own.y_ready.sem, 1)
                            norm.vector(nc, dve, i, 0, x, x, xT_ready)
        t.clear_counts()


EXPERTS, CAPACITY = 8, 100


def moe_ffn(nc, const, xT, w_gate, w_expert, b_expert, out):
    with ExitStack() as ctx:
        t = Tools(ctx, nc, "moe")
        U = 2
        ITER = NG // U
        NE = B * EXPERTS
        wg = t.sb("wg", [P, EXPERTS])
        we = t.sb("we", [P, D])
        be_row = t.sb("be_row", [P, D])
        iota_i = t.sb("iota_i", [P, B, EXPERTS], I32)
        iota = t.sb("iota", [P, B, EXPERTS])
        upto = t.sb("upto", [P, P])
        carry = t.sb("carry", [P, EXPERTS, B])
        logits = t.sb("logits", [P, B, EXPERTS])
        expert = t.sb("expert", [P, B, D])
        xtok = t.sb("xtok", [P, B, D])
        xs = [t.sb(f"xs{u}", [P, GROUP]) for u in range(U)]
        top = t.sb("top", [P, B])
        gate = t.sb("gate", [P, B])
        probs = t.sb("probs", [P, B, EXPERTS])
        best = t.sb("best", [P, B, EXPERTS])
        total = t.sb("total", [P, EXPERTS, B])
        before = t.sb("before", [P, EXPERTS, B])
        place = t.sb("place", [P, B, EXPERTS])
        yt = [t.sb(f"yt{u}", [P, GB, D]) for u in range(U)]
        stats = [t.sb(f"stats{u}", [P, GB, 6]) for u in range(U)]
        pad = t.sb("pad", [P, 1])
        mv = [t.sb(f"mv{u}", [P, GB, 2]) for u in range(U)]
        logs = [t.sb(f"logs{u}", [P, GB]) for u in range(U)]
        inv = [t.sb(f"inv{u}", [P, GB]) for u in range(U)]
        res = [t.sb(f"res{u}", [P, GB, D]) for u in range(U)]
        ps_e = [t.ps(f"bank_e{u}", [P, 512]) for u in range(U)]
        ps_g = [t.ps(f"bank_g{u}", [P, 512]) for u in range(U)]
        ps_x = [t.ps(f"bank_x{u}", [P, 512]) for u in range(U)]
        ps_c = t.ps("cum", [P, NE])
        ps_t = t.ps("tot", [P, NE])

        loaded = t.count("loaded", weight=DMA)
        made = t.count("made")
        xs_ready = t.count("xs_ready", U)
        e_mm, e_kept = t.count("e_mm", U), t.count("e_kept", U, credits=U)
        g_mm, g_kept = t.count("g_mm", U), t.count("g_kept", U, credits=U)
        x_mm, x_kept = t.count("x_mm", U, credits=U), t.count("x_kept", U, credits=U)
        with nc.Block() as block:

            @block.sync
            def _(sp):
                for dst, src in ((wg[:, :], w_gate), (we[:, :], w_expert), (be_row[:, :], b_expert.partition_broadcast(P))):
                    sp.dma_start(dst, src).then_inc(loaded.sem, DMA)

            @block.gpsimd
            def _(pool):
                pool.iota(iota_i[:, :, :], pattern=[[0, B], [1, EXPERTS]], base=0, channel_multiplier=0).then_inc(made.sem, 1)
                pool.memset(upto[:, :], 1.0).then_inc(made.sem, 1)
                pool.memset(carry[:, :, :], 1.0).then_inc(made.sem, 1)
                pool.wait_ge(made.sem, 3)
                pool.affine_select(out=upto[:, :], in_=upto[:, :], compare_op=ALU.is_ge, fill=0.0, base=0,
                                   pattern=[[1, P]], channel_multiplier=-1)
                pool.memset(carry[:, :, 0:1], 0.0)

            @block.vector
            def _(dve):
                for c in (e_kept, g_kept, x_mm, x_kept):
                    c.give(dve)
                dve.wait_ge(made.sem, 1)
                nc.vector.tensor_copy(iota[:, :, :], iota_i[:, :, :])
                dve.wait_ge(loaded.sem, 3 * DMA)

        with nc.Block() as block:

            @block.tensor
            def _(pe):
                mm, turn = nc.tensor.matmul, nc.tensor.transpose
                with pe.Fori(0, ITER) as i:
                    for u in range(U):
                        tok = lambda b: xs[u][:, b * T:(b + 1) * T]
                        pe.wait_ge(xs_ready.sem, xs_ready.after(i, u + 1))
                        pe.wait_ge(g_kept.sem, g_kept.free(i, u))
                        for b in range(GB):
                            last = mm(ps_g[u][:, b * EXPERTS:(b + 1) * EXPERTS], tok(b), wg[:, :], start=True, stop=True)
                        last.then_inc(g_mm.sem, 1)
                        pe.wait_ge(e_kept.sem, e_kept.free(i, u))
                        for b in range(GB):
                            last = mm(ps_e[u][:, b * D:(b + 1) * D], tok(b), we[:, :], start=True, stop=True)
                        last.then_inc(e_mm.sem, 1)
                        pe.wait_ge(x_kept.sem, x_kept.free(i, u))
                        for b in range(GB):
                            last = turn(ps_x[u][:, b * D:(b + 1) * D], tok(b), const["ident"][:, :])
                        last.then_inc(x_mm.sem, 1)

            @block.scalar
            def _(act):
                f = nc.scalar.activation
                with act.Fori(0, ITER) as i:
                    for u in range(U):
                        act.wait_ge(x_mm.sem, x_mm.free(i, u))
                        f(xs[u][:, :], group_of(xT, i, u, U), ACT.Copy).then_inc(xs_ready.sem, 1)
                    for u in range(U):
                        first = i * (U * GB) + u * GB
                        act.wait_ge(x_mm.sem, x_mm.after(i, u + 1))
                        f(xtok[:, bass.ds(first, GB), :], ps_x[u][:, :].rearrange("p (b d) -> p b d", d=D), ACT.Copy).then_inc(x_kept.sem, 1)

            @block.vector
            def _(dve):
                v = nc.vector
                with dve.Fori(0, ITER) as i:
                    for u in range(U):
                        first = i * (U * GB) + u * GB
                        dve.wait_ge(g_mm.sem, g_mm.after(i, u + 1))
                        v.tensor_copy(logits[:, bass.ds(first, GB), :], ps_g[u][:, 0:GB * EXPERTS].rearrange("p (b n) -> p b n", b=GB)).then_inc(g_kept.sem, 1)
                        dve.wait_ge(e_mm.sem, e_mm.after(i, u + 1))
                        v.tensor_tensor(expert[:, bass.ds(first, GB), :], ps_e[u][:, :].rearrange("p (b d) -> p b d", d=D),
                                        be_row[:, :].unsqueeze(1).broadcast_to([P, GB, D]), ALU.add).then_inc(e_kept.sem, 1)

        dist_ready = t.count("dist_ready")
        exp_ready = t.count("exp_ready")
        best_ready = t.count("best_ready")
        places_mm = t.count("places_mm")
        with nc.Block() as block:

            @block.scalar
            def _(act):
                act.wait_ge(dist_ready.sem, 1)
                nc.scalar.activation(probs[:, :, :], probs[:, :, :], ACT.Exp).then_inc(exp_ready.sem, 1)

            @block.tensor
            def _(pe):
                pe.wait_ge(best_ready.sem, 1)
                flat = best[:, :, :].rearrange("p b e -> p (b e)")
                nc.tensor.matmul(ps_c[:, :], upto[:, :], flat, start=True, stop=True)
                nc.tensor.matmul(ps_t[:, :], const["ones"][:, :], flat, start=True, stop=True).then_inc(places_mm.sem, 1)

            @block.vector
            def _(dve):
                v = nc.vector
                link = Chain(t, "route", dve)
                wide = lambda a: a[:, :].unsqueeze(2).broadcast_to([P, B, EXPERTS])
                by_seq = lambda a: a[:, :, :].rearrange("p e b -> p b e")
                link(v.tensor_reduce(top[:, :], logits[:, :, :], AX.X, ALU.max))
                v.tensor_tensor(probs[:, :, :], logits[:, :, :], wide(top), ALU.subtract).then_inc(dist_ready.sem, 1)
                dve.wait_ge(exp_ready.sem, 1)
                link(v.tensor_reduce(top[:, :], probs[:, :, :], AX.X, ALU.add))
                link(v.reciprocal(top[:, :], top[:, :]))
                link(v.tensor_tensor(probs[:, :, :], probs[:, :, :], wide(top), ALU.mult))
                link(v.tensor_reduce(gate[:, :], probs[:, :, :], AX.X, ALU.max))
                first_max_one_hot(link, v, probs[:, :, :], top[:, :], best[:, :, :], iota[:, :, :], EXPERTS)
                dve.sem_inc(best_ready.sem, 1)
                dve.wait_ge(places_mm.sem, 1)
                link(v.tensor_copy(by_seq(total), ps_t[:, :].rearrange("p (b e) -> p b e", e=EXPERTS)))
                flat = lambda a: a[:, :, :].rearrange("p e b -> p (e b)")
                link(v.tensor_tensor_scan(flat(before), flat(carry), flat(total), 0.0, ALU.mult, ALU.add))
                link(v.tensor_tensor(before[:, :, :], before[:, :, :], total[:, :, :], ALU.subtract))
                link(v.tensor_tensor(place[:, :, :], ps_c[:, :].rearrange("p (b e) -> p b e", e=EXPERTS), by_seq(before), ALU.add))
                link(v.scalar_tensor_tensor(place[:, :, :], place[:, :, :], float(CAPACITY), best[:, :, :], ALU.is_le, ALU.mult))
                link(v.tensor_reduce(top[:, :], place[:, :, :], AX.X, ALU.add))
                link(v.tensor_tensor(gate[:, :], gate[:, :], top[:, :], ALU.mult))

        y_ready = t.count("y_ready", U)
        part = t.count("part", U)
        stats_ready = t.count("stats_ready", U)
        mv_ready = t.count("mv_ready", U)
        log_ready = t.count("log_ready", U)
        inv_ready = t.count("inv_ready", U)
        res_ready = t.count("res_ready", U, credits=U)
        stored = [t.count(f"stored{u}", 1, DMA, credits=1) for u in range(U)]
        with nc.Block() as block:

            @block.sync
            def _(sp):
                with sp.Fori(0, ITER) as i:
                    for u in range(U):
                        sp.wait_ge(res_ready.sem, res_ready.after(i, u + 1))
                        dst = out[bass.ds(i * (U * GB) + u * GB, GB)].rearrange("b t d -> t b d")
                        sp.dma_start(dst, res[u][:, :, :]).then_inc(stored[u].sem, DMA)
                for u in range(U):
                    sp.wait_ge(stored[u].sem, (ITER + 1) * DMA)

            @block.scalar
            def _(act):
                f = nc.scalar.activation
                with act.Fori(0, ITER) as i:
                    for u in range(U):
                        nc.scalar.preload_act_table_set("natural_log_exp_and_others")
                        act.wait_ge(mv_ready.sem, mv_ready.after(i, u + 1))
                        f(logs[u][:, :], mv[u][:, :, 1:2].rearrange("p b a -> p (b a)"), ACT.Ln, bias=const["eps"][:, :]).then_inc(log_ready.sem, 1)
                        act.wait_ge(log_ready.sem, log_ready.after(i, u + 1))
                        f(inv[u][:, :], logs[u][:, :], ACT.Exp, scale=-0.5).then_inc(inv_ready.sem, 1)

            @block.vector
            def _(dve):
                v = nc.vector
                for u in range(U):
                    stored[u].give(dve)
                res_ready.give(dve)
                with dve.Fori(0, ITER) as i:
                    for u in range(U):
                        first = i * (U * GB) + u * GB
                        dve.wait_ge(res_ready.sem, res_ready.free(i, u))
                        v.tensor_tensor(yt[u][:, :, :], expert[:, bass.ds(first, GB), :],
                                        gate[:, bass.ds(first, GB)].unsqueeze(2).broadcast_to([P, GB, D]), ALU.mult).then_inc(part.sem, 1)
                        dve.wait_ge(part.sem, part.after(i, u + 1))
                        v.tensor_tensor(yt[u][:, :, :], yt[u][:, :, :], xtok[:, bass.ds(first, GB), :], ALU.add).then_inc(y_ready.sem, 1)
                        dve.wait_ge(y_ready.sem, y_ready.after(i, u + 1))
                        for b in range(GB):
                            last = v.bn_stats(stats[u][:, b, :], yt[u][:, b, :])
                        last.then_inc(stats_ready.sem, 1)
                        dve.wait_ge(stats_ready.sem, stats_ready.after(i, u + 1))
                        v.memset(pad[:, :], 0.0)
                        for b in range(GB):
                            last = v.bn_aggr(mv[u][:, b, :], stats[u][:, b, :])
                        last.then_inc(mv_ready.sem, 1)
                    for u in range(U):
                        dve.wait_ge(inv_ready.sem, inv_ready.after(i, u + 1))
                        dve.wait_ge(stored[u].sem, stored[u].free(i))
                        for b in range(GB):
                            last = v.tensor_scalar(res[u][:, b, :], yt[u][:, b, :], mv[u][:, b, 0:1], inv[u][:, b:b + 1], ALU.subtract, ALU.mult)
                        last.then_inc(res_ready.sem, 1)
        t.clear_counts()


def program(nc, a, out):
    def of(prefix, *names):
        return [a[f"{prefix}_{n}"] for n in names]

    with ExitStack() as ctx:
        xT = ctx.enter_context(nc.sbuf_tensor("xT", [P, NT], F32))
        const = constants(nc, ctx)
        min_gru(nc, const, xT, a["x"], *of("L0_attn", "Wp", "bp", "g1", "Whg", "bhg", "Wo", "bo", "g2", "gf", "Wf", "bf"))
        cross_attention(nc, const, "x0", xT, a["ctx_1024"], *of("L0_xattn", "Wq", "bq", "Wk", "bk", "Wv", "bv", "Wo", "bo"), turn=True,
                        temper=of("L0_xattn", "w1", "b1", "w2", "b2", "w3", "b3"))
        tile_ffn(nc, const, xT, *of("L0_ffn", "signatures_raw", "knot_values", "temperature", "compress_w1", "compress_b1",
                                    "compress_w2", "compress_b2", "spline_w1", "spline_b1", "spline_w2", "spline_b2",
                                    "directions", "norm_gamma", "norm_beta", "output_scale"))
        self_attention(nc, const, xT, *of("L1_attn", "adaptive_scale", "Wq", "bq", "Wk", "bk", "Wv", "bv", "Wo", "bo", "gamma", "beta"))
        cross_attention(nc, const, "x1", xT, a["ctx_1024"], *of("L1_xattn", "W_Q", "b_Q", "W_K", "b_K", "W_V", "b_V", "W_O", "b_O"), turn=False)
        moe_ffn(nc, const, xT, *of("L1_ffn", "w_gate", "w_expert", "b_expert"), out)


def kernel(**inputs):
    import concourse.bacc as _bacc
    from concourse.bass_utils import run_bass_kernel_spmd as _run

    nc = _bacc.Bacc("TRN2", target_bir_lowering=False, num_devices=1)
    arrays, aps = {}, {}
    for name, value in inputs.items():
        value = np.ascontiguousarray(value)
        arrays[f"in_{name}"] = value
        aps[name] = nc.dram_tensor(f"in_{name}", value.shape, mybir.dt.from_np(value.dtype), kind="ExternalInput").ap()
    out = nc.dram_tensor("out", (B, T, D), F32, kind="ExternalOutput").ap()
    program(nc, aps, out)
    r = _run(nc, [arrays], core_ids=[0])
    return r.results[0]["out"]
```

```python
from contextlib import ExitStack

import numpy as np

import concourse.bass as bass
from concourse import mybir

F32 = mybir.dt.float32
I32 = mybir.dt.int32
U32 = mybir.dt.uint32
ALU = mybir.AluOpType
ACT = mybir.ActivationFunctionType
AX = mybir.AxisListType

P = 128
B = 32
T = 128
D = 128
NT = B * T
GB = 4
GROUP = GB * T
NG = NT // GROUP
S = 77
H = 16
DK = D // H
EPS = 1e-5
DMA = 16


class Count:

    def __init__(self, ctx, nc, name, per=1, weight=1, credits=0):
        self.sem = ctx.enter_context(nc.semaphore(name))
        self.per, self.weight, self.credits = per, weight, credits

    def after(self, i, k=1):
        return i * (self.per * self.weight) + (k + self.credits) * self.weight

    def free(self, i, n=0):
        return i * (self.per * self.weight) + (n + 1) * self.weight

    def give(self, engine):
        engine.sem_inc(self.sem, self.credits * self.weight)


class Tools:

    def __init__(self, ctx, nc, tag):
        self.ctx, self.nc, self.tag, self.numbers = ctx, nc, tag, []

    def sb(self, name, shape, dt=F32):
        return self.ctx.enter_context(self.nc.sbuf_tensor(f"{self.tag}_{name}", shape, dt))

    def ps(self, name, shape, dt=F32):
        return self.ctx.enter_context(self.nc.psum_tensor(f"{self.tag}_{name}", shape, dt))

    def count(self, name, per=1, weight=1, credits=0):
        c = Count(self.ctx, self.nc, f"{self.tag}_{name}", per, weight, credits)
        self.numbers.append(c.sem.num)
        return c

    def clear_counts(self):
        numbers = sorted(self.numbers)
        with self.nc.Block() as block:

            @block.sync
            def _(sp):
                first = last = numbers[0]
                for n in numbers[1:] + [None]:
                    if n != last + 1:
                        sp.sem_clear(range(first, last + 1))
                        first = n
                    last = n


def constants(nc, ctx):
    t = Tools(ctx, nc, "const")
    c = {
        "ident": t.sb("ident", [P, P]),
        "ones": t.sb("ones", [P, P]),
        "mean": t.sb("mean", [P, P]),
        "eps": t.sb("eps", [P, 1]),
        "tiny": t.sb("tiny", [P, 1]),
        "rms_bias": t.sb("rms_bias", [P, 1]),
    }
    cleared = t.count("cleared")
    with nc.Block() as block:

        @block.gpsimd
        def _(pool):
            pool.memset(c["ident"][:, :], 0.0).then_inc(cleared.sem, 1)
            pool.memset(c["ones"][:, :], 1.0)
            pool.memset(c["mean"][:, :], 1.0 / D)
            pool.memset(c["eps"][:, :], EPS)
            pool.memset(c["tiny"][:, :], RMS_TINY)
            pool.memset(c["rms_bias"][:, :], 0.5 * RMS_SHIFT * float(np.log(2.0)))
            pool.wait_ge(cleared.sem, 1)
            pool.affine_select(out=c["ident"][:, :], in_=c["ident"][:, :], compare_op=ALU.not_equal,
                               fill=1.0, base=0, pattern=[[-1, P]], channel_multiplier=1)
    return c


RMS_SHIFT = 24
RMS_TINY = 2.0 ** -64
RMS_SCALE = 2.0 ** RMS_SHIFT
INV_NORM_MAX = 1e12


HID = 256
DI = 384
NL = 4
KH = HID // P
KI = DI // P
TP = T + 1


def min_gru(nc, const, xT, x, Wp, bp, g1, Whg, bhg, Wo, bo, g2, gf, Wf, bf):
    with ExitStack() as ctx:
        t = Tools(ctx, nc, "gru")
        U = 2
        NORMS = 2 * NL + 2
        wp = t.sb("wp", [P, HID])
        whg = t.sb("whg", [P, NL, KH, 2 * DI])
        wo = t.sb("wo", [P, NL, KI, HID])
        wf = t.sb("wf", [P, KH, D])
        bp_c = t.sb("bp_c", [P, KH])
        bhg_c = t.sb("bhg_c", [P, NL, 2 * KI])
        nbg_c = t.sb("nbg_c", [P, NL, 2 * KI])
        bo_c = t.sb("bo_c", [P, NL, KH])
        g1_c = t.sb("g1_c", [P, NL, KH])
        g2_c = t.sb("g2_c", [P, NL, KH])
        gf_c = t.sb("gf_c", [P, KH])
        bf_c = t.sb("bf_c", [P, 1])
        xin = [t.sb(f"xin{u}", [P, GB, D]) for u in range(U)]
        xg = [t.sb(f"xg{u}", [P, GROUP]) for u in range(U)]
        h = [t.sb(f"h{u}", [P, KH, GROUP]) for u in range(U)]
        sq = [t.sb(f"sq{u}", [P, KH, GROUP]) for u in range(U)]
        xn = [t.sb(f"xn{u}", [P, KH, GROUP]) for u in range(U)]
        lnr = [t.sb(f"lnr{u}", [P, GROUP]) for u in range(U)]
        inv = [t.sb(f"inv{u}", [P, GROUP]) for u in range(U)]
        y = [t.sb(f"y{u}", [P, KI, GB * TP]) for u in range(U)]
        decay = [t.sb(f"decay{r}", [P, GB * TP]) for r in range(2)]
        value = [t.sb(f"value{r}", [P, GB * TP]) for r in range(2)]
        zgate = [t.sb(f"zgate{r}", [P, GROUP]) for r in range(2)]
        sighid = [t.sb(f"sighid{r}", [P, GROUP]) for r in range(2)]
        relhid = [t.sb(f"relhid{r}", [P, GROUP]) for r in range(2)]
        ghid = [t.sb(f"ghid{r}", [P, GROUP]) for r in range(2)]
        gain = [t.sb(f"gain{m}", [P, GROUP]) for m in range(KH)]
        ps_stat = [t.ps(f"stat{u}", [P, GROUP]) for u in range(U)]
        ps_hid = [t.ps(f"hid{r}", [P, GROUP]) for r in range(2)]
        ps_gate = [t.ps(f"gate{r}", [P, GROUP]) for r in range(2)]
        ps_out = [t.ps(f"out{m}", [P, GROUP]) for m in range(KH)]

        loaded = [t.count(f"loaded{n}", weight=DMA) for n in range(NL + 1)]
        gains_ready = t.count("gains_ready")
        scaled = [t.count(f"scaled{n}") for n in range(NL + 1)]
        pads_ready = t.count("pads_ready")
        x_loaded = [t.count(f"x_loaded{u}", 1, DMA) for u in range(U)]
        x_turned = t.count("x_turned", U)
        xg_ready = t.count("xg_ready", U)
        sq_ready = [t.count(f"sq_ready{u}", NORMS) for u in range(U)]
        stat_ready = [t.count(f"stat_ready{u}", NORMS + 1) for u in range(U)]
        ln_ready = [t.count(f"ln_ready{u}", NORMS) for u in range(U)]
        inv_ready = [t.count(f"inv_ready{u}", NORMS) for u in range(U)]
        xn_ready = [t.count(f"xn_ready{u}", NL + 1) for u in range(U)]
        h_ready = [t.count(f"h_ready{u}", KH * (1 + 2 * NL)) for u in range(U)]
        gain_ready = t.count("gain_ready", U * KH * NL)
        sum_ready = [t.count(f"sum_ready{u}", 2) for u in range(U)]
        NCH = U * NL * KI
        hg_ready = t.count("hg_ready", NCH)
        gates_ready = t.count("gates_ready", NCH, credits=2)
        ghid_ready = t.count("ghid_ready", NCH)
        value_ready = t.count("value_ready", NCH)
        scan_ready = t.count("scan_ready", NCH, credits=2)
        NOUT = U * (KH * (1 + NL) + 1)
        out_ready = t.count("out_ready", NOUT)
        out_free = t.count("out_free", NOUT, credits=2)
        xT_ready = t.count("xT_ready", U, credits=U)

        ITER = NG // U
        ORDER = [("load", u, 0) for u in range(U)]
        for l in range(NL):
            ORDER += [("pre", u, l) for u in range(U)]
            ORDER += [("rec", u, l) for u in range(U)]
            for u in range(U):
                ORDER += [("mix", u, l), ("post", u, l)]
        ORDER += [("final", u, 0) for u in range(U)]

        def chunk_no(u, l, c):
            return (l * U + u) * KI + c

        def out_no(kind, u, l, m):
            if kind == "load":
                return u * KH + m
            if kind == "mix":
                return U * KH + (l * U + u) * KH + m
            return U * KH * (1 + NL) + u

        with nc.Block() as block:

            @block.sync
            def _(sp):
                cols = lambda v, n: v.rearrange("(n p) -> p n", p=P)
                sp.dma_start(xin[0][:, :, :], x[0:GB].rearrange("b t d -> t b d")).then_inc(x_loaded[0].sem, DMA)
                sp.dma_start(xin[1][:, :, :], x[GB:2 * GB].rearrange("b t d -> t b d")).then_inc(x_loaded[1].sem, DMA)
                for dst, src in (
                    (wp[:, :], Wp), (bp_c[:, :], cols(bp, KH)), (gf_c[:, :], cols(gf, KH)), (bf_c[:, :], cols(bf, 1)),
                    (g1_c[:, :, :], g1.rearrange("l (k p) -> p l k", p=P)),
                    (g2_c[:, :, :], g2.rearrange("l (k p) -> p l k", p=P)),
                    (bo_c[:, :, :], bo.rearrange("l (k p) -> p l k", p=P)),
                    (bhg_c[:, :, :], bhg.rearrange("l (k p) -> p l k", p=P)),
                    (wf[:, :, :], Wf.rearrange("(k p) n -> p k n", p=P)),
                ):
                    sp.dma_start(dst, src, allow_slow_non_contiguous=True).then_inc(loaded[NL].sem, DMA)
                for l in range(NL):
                    sp.dma_start(whg[:, l, :, :], Whg[l].rearrange("(k p) n -> p k n", p=P)).then_inc(loaded[l].sem, DMA)
                    sp.dma_start(wo[:, l, :, :], Wo[l].rearrange("(k p) n -> p k n", p=P)).then_inc(loaded[l].sem, DMA)
                with sp.Fori(0, ITER - 1) as i:
                    for u in range(U):
                        sp.wait_ge(x_turned.sem, x_turned.after(i, u + 1))
                        src = x[bass.ds((i + 1) * (U * GB) + u * GB, GB)].rearrange("b t d -> t b d")
                        sp.dma_start(xin[u][:, :, :], src).then_inc(x_loaded[u].sem, DMA)

            @block.tensor
            def _(pe):
                mm = nc.tensor.matmul

                def stat(i, u, q, w, cols, n):
                    for k in range(n):
                        last = mm(ps_stat[u][:, :], w[:, :], cols[:, k, :], start=(k == 0), stop=(k == n - 1))
                    last.then_inc(stat_ready[u].sem, 1)

                with pe.Fori(0, ITER) as i:
                    for kind, u, l in ORDER:
                        if kind == "load":
                            pe.wait_ge(x_loaded[u].sem, x_loaded[u].after(i))
                            pe.wait_ge(out_free.sem, out_free.free(i, out_no(kind, u, l, 0)))
                            for b in range(GB):
                                last = nc.tensor.transpose(ps_out[0][:, b * T:(b + 1) * T], xin[u][:, b, :], const["ident"][:, :])
                            last.then_inc(x_turned.sem, 1)
                            pe.wait_ge(xg_ready.sem, xg_ready.after(i, u + 1))
                            pe.wait_ge(loaded[NL].sem, loaded[NL].after(0, 9))
                            for m in range(KH):
                                if m:
                                    pe.wait_ge(out_free.sem, out_free.free(i, out_no(kind, u, l, m)))
                                mm(ps_out[m][:, :], wp[:, m * P:(m + 1) * P], xg[u][:, :], start=True, stop=True).then_inc(out_ready.sem, 1)
                        elif kind in ("pre", "post"):
                            q = 2 * l + (kind == "post")
                            pe.wait_ge(sq_ready[u].sem, sq_ready[u].after(i, q + 1))
                            stat(i, u, q, const["ones"], sq[u], KH)
                        elif kind == "rec":
                            pe.wait_ge(xn_ready[u].sem, xn_ready[u].after(i, l + 1))
                            pe.wait_ge(scaled[l].sem, KH)
                            for c in range(KI):
                                n = chunk_no(u, l, c)
                                pe.wait_ge(gates_ready.sem, gates_ready.free(i, n))
                                for bank, off in ((ps_hid[n % 2], c * P), (ps_gate[n % 2], DI + c * P)):
                                    for k in range(KH):
                                        last = mm(bank[:, :], whg[:, l, k, off:off + P], xn[u][:, k, :], start=(k == 0), stop=(k == KH - 1))
                                last.then_inc(hg_ready.sem, 1)
                        elif kind == "mix":
                            pe.wait_ge(scan_ready.sem, scan_ready.after(i, chunk_no(u, l, KI - 1) + 1))
                            for m in range(KH):
                                pe.wait_ge(out_free.sem, out_free.free(i, out_no(kind, u, l, m)))
                                for k in range(KI):
                                    seqs = y[u][:, k, :].rearrange("p (b t) -> p b t", t=TP)[:, :, 1:]
                                    last = mm(ps_out[m][:, :], wo[:, l, k, m * P:(m + 1) * P], seqs, start=(k == 0), stop=(k == KI - 1))
                                last.then_inc(out_ready.sem, 1)
                        else:
                            q = 2 * NL
                            pe.wait_ge(sq_ready[u].sem, sq_ready[u].after(i, q + 1))
                            stat(i, u, q, const["ones"], sq[u], KH)
                            pe.wait_ge(xn_ready[u].sem, xn_ready[u].after(i, NL + 1))
                            pe.wait_ge(scaled[NL].sem, KH)
                            pe.wait_ge(out_free.sem, out_free.free(i, out_no(kind, u, l, 0)))
                            for k in range(KH):
                                last = mm(ps_out[u][:, :], wf[:, k, :], xn[u][:, k, :], start=(k == 0), stop=(k == KH - 1))
                            last.then_inc(out_ready.sem, 1)
                            pe.wait_ge(sum_ready[u].sem, sum_ready[u].after(i, 1))
                            mm(ps_stat[u][:, :], const["mean"][:, :], xg[u][:, :], start=True, stop=True).then_inc(stat_ready[u].sem, 1)
                            pe.wait_ge(sq_ready[u].sem, sq_ready[u].after(i, NORMS))
                            mm(ps_stat[u][:, :], const["mean"][:, :], sq[u][:, 0, :], start=True, stop=True).then_inc(stat_ready[u].sem, 1)

            @block.scalar
            def _(act):
                f = nc.scalar.activation
                act.wait_ge(loaded[NL].sem, loaded[NL].after(0, 9))
                nc.scalar.mul(nbg_c[:, :, :], bhg_c[:, :, :], -1.0).then_inc(gains_ready.sem, 1)
                act.wait_ge(gains_ready.sem, 1)
                act.wait_ge(pads_ready.sem, 4)

                def inverse(i, u, q, s, bias, scale, shift):
                    if u == 0:
                        nc.scalar.preload_act_table_set("natural_log_exp_and_others")
                    act.wait_ge(stat_ready[u].sem, stat_ready[u].after(i, s))
                    f(lnr[u][:, :], ps_stat[u][:, :], ACT.Ln, bias=bias, scale=scale).then_inc(ln_ready[u].sem, 1)
                    act.wait_ge(ln_ready[u].sem, ln_ready[u].after(i, q + 1))
                    f(inv[u][:, :], lnr[u][:, :], ACT.Exp, bias=shift, scale=-0.5).then_inc(inv_ready[u].sem, 1)

                with act.Fori(0, ITER) as i:
                    for kind, u, l in ORDER:
                        if kind == "load":
                            act.wait_ge(x_turned.sem, x_turned.after(i, u + 1))
                            act.wait_ge(xT_ready.sem, xT_ready.free(i, u))
                            f(xg[u][:, :], ps_out[0][:, :], ACT.Copy).then_inc(xg_ready.sem, 1)
                        elif kind in ("pre", "post"):
                            q = 2 * l + (kind == "post")
                            act.wait_ge(h_ready[u].sem, h_ready[u].after(i, KH * (q + 1)))
                            f(sq[u][:, :, :], h[u][:, :, :], ACT.Square).then_inc(sq_ready[u].sem, 1)
                            inverse(i, u, q, q + 1, const["tiny"][:, :], RMS_SCALE, const["rms_bias"][:, :])
                        elif kind == "rec":
                            for c in range(KI):
                                n = chunk_no(u, l, c)
                                r = n % 2
                                act.wait_ge(hg_ready.sem, hg_ready.after(i, n + 1))
                                act.wait_ge(scan_ready.sem, scan_ready.free(i, n))
                                seqs = lambda v: v.rearrange("p (b t) -> p b t", t=T)
                                gate = ps_gate[r][:, :]
                                f(zgate[r][:, :], gate, ACT.Sigmoid, bias=bhg_c[:, l, KI + c:KI + c + 1])
                                f(decay[r][:, :].rearrange("p (b t) -> p b t", t=TP)[:, :, 1:], seqs(gate), ACT.Sigmoid,
                                  bias=nbg_c[:, l, KI + c:KI + c + 1], scale=-1.0)
                                f(sighid[r][:, :], ps_hid[r][:, :], ACT.Sigmoid, bias=bhg_c[:, l, c:c + 1])
                                f(relhid[r][:, :], ps_hid[r][:, :], ACT.Relu, bias=bhg_c[:, l, c:c + 1]).then_inc(gates_ready.sem, 1)
                        elif kind == "final":
                            q = 2 * NL
                            act.wait_ge(h_ready[u].sem, h_ready[u].after(i, KH * (q + 1)))
                            f(sq[u][:, :, :], h[u][:, :, :], ACT.Square).then_inc(sq_ready[u].sem, 1)
                            inverse(i, u, q, q + 1, const["tiny"][:, :], RMS_SCALE, const["rms_bias"][:, :])
                            act.wait_ge(sum_ready[u].sem, sum_ready[u].after(i, 2))
                            f(sq[u][:, 0, :], xg[u][:, :], ACT.Square).then_inc(sq_ready[u].sem, 1)
                            inverse(i, u, NORMS - 1, NORMS + 1, const["eps"][:, :], 1.0, 0.0)

            @block.vector
            def _(dve):
                v = nc.vector
                dve.wait_ge(loaded[NL].sem, loaded[NL].after(0, 9))
                root = float(HID) ** 0.5
                for g in (g1_c[:, :, :], g2_c[:, :, :], gf_c[:, :]):
                    v.tensor_scalar(g, g, 1.0, root, ALU.add, ALU.mult).then_inc(gains_ready.sem, 1)
                dve.wait_ge(gains_ready.sem, 4)
                for r in range(2):
                    v.memset(decay[r][:, :].rearrange("p (b t) -> p b t", t=TP)[:, :, 0:1], 0.0).then_inc(pads_ready.sem, 1)
                    v.memset(value[r][:, :].rearrange("p (b t) -> p b t", t=TP)[:, :, 0:1], 1.0).then_inc(pads_ready.sem, 1)
                for l in range(NL):
                    dve.wait_ge(loaded[l].sem, loaded[l].after(0, 2))
                    for k in range(KH):
                        v.tensor_scalar(whg[:, l, k, :], whg[:, l, k, :], g1_c[:, l, k:k + 1], None, ALU.mult).then_inc(scaled[l].sem, 1)
                for k in range(KH):
                    v.tensor_scalar(wf[:, k, :], wf[:, k, :], gf_c[:, k:k + 1], None, ALU.mult).then_inc(scaled[NL].sem, 1)
                out_free.give(dve)
                gates_ready.give(dve)
                scan_ready.give(dve)
                xT_ready.give(dve)

                with dve.Fori(0, ITER) as i:
                    for kind, u, l in ORDER:
                        if kind == "load":
                            for m in range(KH):
                                dve.wait_ge(out_ready.sem, out_ready.after(i, out_no(kind, u, l, m) + 1))
                                v.tensor_scalar(h[u][:, m, :], ps_out[m][:, :], bp_c[:, m:m + 1], None, ALU.add).then_inc(h_ready[u].sem, 1)
                            dve.wait_ge(h_ready[u].sem, h_ready[u].after(i, KH))
                            dve.sem_inc(out_free.sem, KH)
                        elif kind == "pre":
                            q = 2 * l
                            dve.wait_ge(inv_ready[u].sem, inv_ready[u].after(i, q + 1))
                            both = inv[u][:, :].rearrange("p (k t) -> p k t", k=1).broadcast_to([P, KH, GROUP])
                            v.scalar_tensor_tensor(xn[u][:, :, :], both, INV_NORM_MAX, h[u][:, :, :], ALU.min, ALU.mult).then_inc(xn_ready[u].sem, 1)
                        elif kind == "rec":
                            for c in range(KI):
                                n = chunk_no(u, l, c)
                                r = n % 2
                                dve.wait_ge(gates_ready.sem, gates_ready.after(i, n + 1))
                                v.scalar_tensor_tensor(ghid[r][:, :], sighid[r][:, :], 0.5, relhid[r][:, :], ALU.min, ALU.add).then_inc(ghid_ready.sem, 1)
                                dve.wait_ge(ghid_ready.sem, ghid_ready.after(i, n + 1))
                                seqs = lambda w: w.rearrange("p (b t) -> p b t", t=T)
                                v.tensor_tensor(value[r][:, :].rearrange("p (b t) -> p b t", t=TP)[:, :, 1:], seqs(ghid[r][:, :]),
                                                seqs(zgate[r][:, :]), ALU.mult).then_inc(value_ready.sem, 1)
                                dve.wait_ge(value_ready.sem, value_ready.after(i, n + 1))
                                v.tensor_tensor_scan(y[u][:, c, :], decay[r][:, :], value[r][:, :], 0.0, ALU.mult, ALU.add).then_inc(scan_ready.sem, 1)
                        elif kind == "mix":
                            for m in range(KH):
                                dve.wait_ge(out_ready.sem, out_ready.after(i, out_no(kind, u, l, m) + 1))
                                v.scalar_tensor_tensor(h[u][:, m, :], ps_out[m][:, :], bo_c[:, l, m:m + 1], h[u][:, m, :], ALU.add, ALU.add).then_inc(h_ready[u].sem, 1)
                            dve.wait_ge(h_ready[u].sem, h_ready[u].after(i, KH * (2 * l + 2)))
                            dve.sem_inc(out_free.sem, KH)
                        elif kind == "post":
                            q = 2 * l + 1
                            dve.wait_ge(inv_ready[u].sem, inv_ready[u].after(i, q + 1))
                            for m in range(KH):
                                g = (l * U + u) * KH + m
                                v.tensor_scalar(gain[m][:, :], inv[u][:, :], INV_NORM_MAX, g2_c[:, l, m:m + 1], ALU.min, ALU.mult).then_inc(gain_ready.sem, 1)
                            for m in range(KH):
                                g = (l * U + u) * KH + m
                                dve.wait_ge(gain_ready.sem, gain_ready.after(i, g + 1))
                                v.scalar_tensor_tensor(h[u][:, m, :], gain[m][:, :], 1.0, h[u][:, m, :], ALU.add, ALU.mult).then_inc(h_ready[u].sem, 1)
                        else:
                            q = 2 * NL
                            dve.wait_ge(inv_ready[u].sem, inv_ready[u].after(i, q + 1))
                            both = inv[u][:, :].rearrange("p (k t) -> p k t", k=1).broadcast_to([P, KH, GROUP])
                            v.scalar_tensor_tensor(xn[u][:, :, :], both, INV_NORM_MAX, h[u][:, :, :], ALU.min, ALU.mult).then_inc(xn_ready[u].sem, 1)
                            dve.wait_ge(out_ready.sem, out_ready.after(i, out_no(kind, u, l, 0) + 1))
                            v.scalar_tensor_tensor(xg[u][:, :], ps_out[u][:, :], bf_c[:, 0:1], xg[u][:, :], ALU.add, ALU.add).then_inc(sum_ready[u].sem, 1)
                            dve.wait_ge(sum_ready[u].sem, sum_ready[u].after(i, 1))
                            dve.sem_inc(out_free.sem, 1)
                            dve.wait_ge(stat_ready[u].sem, stat_ready[u].after(i, NORMS))
                            v.tensor_tensor(xg[u][:, :], xg[u][:, :], ps_stat[u][:, :], ALU.subtract).then_inc(sum_ready[u].sem, 1)
                            dve.wait_ge(inv_ready[u].sem, inv_ready[u].after(i, NORMS))
                            dst = xT[:, bass.ds(i * (U * GROUP) + u * GROUP, GROUP)]
                            v.tensor_tensor(dst, xg[u][:, :], inv[u][:, :], ALU.mult).then_inc(xT_ready.sem, 1)
        t.clear_counts()


LN_EXP = "natural_log_exp_and_others"

class Norm:

    def __init__(self, t, const, name, per, y, sq, logs, inv, bank):
        self.const, self.y, self.sq, self.logs, self.inv, self.bank = const, y, sq, logs, inv, bank
        self.y_ready = t.count(f"{name}_y_ready", per)
        self.mean_ready = t.count(f"{name}_mean_ready", per)
        self.centred = t.count(f"{name}_centred", per)
        self.sq_ready = t.count(f"{name}_sq_ready", per)
        self.var_ready = t.count(f"{name}_var_ready", per)
        self.log_ready = t.count(f"{name}_log_ready", per, credits=1)
        self.inv_ready = t.count(f"{name}_inv_ready", per)

    def mean(self, nc, pe, i, n):
        pe.wait_ge(self.y_ready.sem, self.y_ready.after(i, n + 1))
        nc.tensor.matmul(self.bank[:, :], self.const["mean"][:, :], self.y[:, :], start=True, stop=True).then_inc(self.mean_ready.sem, 1)

    def variance(self, nc, pe, i, n):
        pe.wait_ge(self.sq_ready.sem, self.sq_ready.after(i, n + 1))
        nc.tensor.matmul(self.bank[:, :], self.const["mean"][:, :], self.sq[:, :], start=True, stop=True).then_inc(self.var_ready.sem, 1)

    def tensor(self, nc, pe, i, n):
        self.mean(nc, pe, i, n)
        self.variance(nc, pe, i, n)

    def square(self, nc, act, i, n):
        act.wait_ge(self.centred.sem, self.centred.after(i, n + 1))
        nc.scalar.activation(self.sq[:, :], self.y[:, :], ACT.Square).then_inc(self.sq_ready.sem, 1)

    def inverse(self, nc, act, i, n):
        act.wait_ge(self.var_ready.sem, self.var_ready.after(i, n + 1))
        nc.scalar.activation(self.logs[:, :], self.bank[:, :], ACT.Ln, bias=self.const["eps"][:, :]).then_inc(self.log_ready.sem, 1)
        act.wait_ge(self.log_ready.sem, self.log_ready.after(i, n + 1))
        nc.scalar.activation(self.inv[:, :], self.logs[:, :], ACT.Exp, scale=-0.5).then_inc(self.inv_ready.sem, 1)

    def scalar(self, nc, act, i, n):
        self.square(nc, act, i, n)
        self.inverse(nc, act, i, n)

    def centre(self, nc, dve, i, n):
        dve.wait_ge(self.mean_ready.sem, self.mean_ready.after(i, n + 1))
        nc.vector.tensor_tensor(self.y[:, :], self.y[:, :], self.bank[:, :], ALU.subtract).then_inc(self.centred.sem, 1)

    def divide(self, nc, dve, i, n, out, done):
        dve.wait_ge(self.inv_ready.sem, self.inv_ready.after(i, n + 1))
        nc.vector.tensor_tensor(out, self.y[:, :], self.inv[:, :], ALU.mult).then_inc(done.sem, 1)


def group_of(xT, i, u, U):
    return xT[:, bass.ds(i * (U * GROUP) + u * GROUP, GROUP)]


def load_transposed(nc, const, tag, pairs, bank):
    with ExitStack() as ctx:
        t = Tools(ctx, nc, tag)
        blocks = []
        for dst, src in pairs:
            n = max(1, dst.shape[1] // P)
            if n == 1:
                blocks.append((dst, src))
            else:
                blocks += [(dst[:, k * P:(k + 1) * P], src[k * P:(k + 1) * P, :] if src.shape[0] == n * P else src[:, k * P:(k + 1) * P])
                           for k in range(n)]
        raw = t.sb("raw", [P, len(blocks), P])
        loaded = t.count("loaded", weight=DMA)
        turned = t.count("turned")
        kept = t.count("kept")
        with nc.Block() as block:

            @block.sync
            def _(sp):
                for n, (_, src) in enumerate(blocks):
                    sp.dma_start(raw[0:src.shape[0], n, 0:src.shape[1]], src).then_inc(loaded.sem, DMA)

            @block.tensor
            def _(pe):
                pe.wait_ge(loaded.sem, len(blocks) * DMA)
                for n, (_, src) in enumerate(blocks):
                    a, b = src.shape
                    if n >= 2:
                        pe.wait_ge(kept.sem, n - 1)
                    nc.tensor.transpose(bank[n % 2][0:b, 0:a], raw[0:a, n, 0:b], const["ident"][0:a, 0:a]).then_inc(turned.sem, 1)

            @block.vector
            def _(dve):
                for n, (dst, src) in enumerate(blocks):
                    a, b = src.shape
                    dve.wait_ge(turned.sem, n + 1)
                    nc.vector.tensor_copy(dst[0:b, 0:a], bank[n % 2][0:b, 0:a]).then_inc(kept.sem, 1)
        t.clear_counts()


MLP = 64
LOG_T_MIN, LOG_T_MAX = float(np.log(0.1)), float(np.log(10.0))


def cross_attention(nc, const, tag, xT, context, wq, bq, wk, bk, wv, bv, wo, bo, turn, temper=None):
    with ExitStack() as ctx:
        t = Tools(ctx, nc, tag)
        KS = GB * S
        UNITS = [(0, 6), (6, 6), (12, 4)]
        RING = 2 * GB
        w = {n: t.sb(f"w_{n}", [P, D]) for n in "qkvo"}
        bias = {n: t.sb(f"b_{n}", [P, 1]) for n in "qko"}
        bv_row = t.sb("bv_row", [S, D])
        heads = t.sb("heads", [P, H])
        ctx_in = t.sb("ctx_in", [S, GB, D])
        cT = t.sb("cT", [P, KS])
        kT = t.sb("kT", [P, KS])
        q = t.sb("q", [P, GROUP])
        vaug = t.sb("vaug", [S, B, H, DK + 1])
        kbd = [t.sb(f"kbd{r}", [P, H, S]) for r in range(2)]
        m = t.sb("m", [P, B, H])
        dist = t.sb("dist", [P, RING, H, S])
        probs = [t.sb(f"probs{r}", [P, H, S]) for r in range(2)]
        pt = [t.sb(f"pt{r}", [S, H * T]) for r in range(2)]
        rz = [t.sb(f"rz{r}", [P, H]) for r in range(2)]
        zmax = [t.sb(f"zmax{r}", [P, H]) for r in range(2)]
        o = t.sb("o", [P, GB, H, DK])
        oT = t.sb("oT", [P, GROUP])
        y = t.sb("y", [P, GROUP])
        sq = t.sb("sq", [P, GROUP])
        logs = t.sb("logs", [P, GROUP])
        inv = t.sb("inv", [P, GROUP])
        ps_s = t.ps("scores", [P, 3, 512])
        ps_x = t.ps("proj", [P, 512])
        ps_t = [t.ps(f"turned{r}", [P, 512]) for r in range(2)]
        ps_o = t.ps("out", [P, 512])
        ps_n = t.ps("norm", [P, 512])
        if temper:
            tw1, tb1, tw2, tb2, tw3, tb3 = temper
            w1raw = t.sb("w1raw", [P, MLP, 3])
            w1b = t.sb("w1b", [P, 3, P])
            w2T = t.sb("w2T", [P, P])
            w3raw = t.sb("w3raw", [P, 1])
            w3b = t.sb("w3b", [P, P])
            mb1, mb2, mb3 = t.sb("mb1", [P, 1]), t.sb("mb2", [P, 1]), t.sb("mb3", [P, 1])
            half = t.sb("half", [P, 1])
            e1 = [t.sb(f"e1_{r}", [P, H, S]) for r in range(2)]
            e1sq = [t.sb(f"e1sq_{r}", [P, H, S]) for r in range(2)]
            qs, ks, qk = (t.sb(n, [P, GB]) for n in ("qs", "ks", "qk"))
            mean_f, z1, s2, var_f = (t.sb(n, [P, GB, H]) for n in ("mean_f", "z1", "s2", "var_f"))
            g1, g2, lt, rt = (t.sb(n, [P, GB * H]) for n in ("g1", "g2", "lt", "rt"))

        loaded = t.count("loaded", weight=DMA)
        masked = t.count("masked")
        ctx_loaded = t.count("ctx_loaded", 1, DMA)
        ctx_turned = t.count("ctx_turned")
        ct_ready = t.count("ct_ready")
        k_mm = t.count("k_mm")
        k_ready = t.count("k_ready")
        v_mm = t.count("v_mm")
        v_ready = t.count("v_ready", credits=1)
        q_mm = t.count("q_mm")
        q_ready = t.count("q_ready")
        kbd_ready = t.count("kbd_ready", GB, credits=1)
        s_mm = [t.count(f"s_mm{k}", GB, credits=2) for k in range(3)]
        m_ready = [t.count(f"m_ready{k}", GB) for k in range(3)]
        d_ready = [t.count(f"d_ready{k}", GB, credits=1) for k in range(3)]
        p_ready = t.count("p_ready", GB, credits=RING)
        t_mm = [t.count(f"t_mm{r}", 2 * GB, credits=4) for r in range(2)]
        pt_ready = [t.count(f"pt_ready{r}", 2 * GB, credits=1) for r in range(2)]
        pv_mm = t.count("pv_mm", GB, credits=2)
        z_ready = t.count("z_ready", GB)
        rz_ready = t.count("rz_ready", GB)
        o_ready = t.count("o_ready", GB, credits=1)
        ot_mm = t.count("ot_mm", credits=1)
        ot_ready = t.count("ot_ready")
        wo_mm = t.count("wo_mm")
        xT_ready = t.count("xT_ready")
        norm = Norm(t, const, "ln", 1, y, sq, logs, inv, ps_n)
        given = [v_ready, kbd_ready, *s_mm, *d_ready, p_ready, *t_mm, *pt_ready, pv_mm, o_ready, ot_mm, norm.log_ready]
        if temper:
            e1_ready = t.count("e1_ready", GB)
            e1sq_ready = t.count("e1sq_ready", GB)
            s2_ready = t.count("s2_ready", GB, credits=2)
            small = t.count("small", 5)
            mean_ready = t.count("mean_ready", credits=1)
            feat_ready = t.count("feat_ready", credits=1)
            hid_mm = t.count("hid_mm", credits=1)
            g1_ready = t.count("g1_ready")
            h2_mm = t.count("h2_mm")
            g2_ready = t.count("g2_ready")
            logt_mm = t.count("logt_mm")
            lt_ready = t.count("lt_ready", 2, credits=2)
            rt_ready = t.count("rt_ready")
            pre_ready = t.count("pre_ready", GB, credits=RING)
            given += [s2_ready, mean_ready, feat_ready, hid_mm, lt_ready, pre_ready]

        SLOT0 = [("scale", 2, 1), ("x0", 2, 2), ("soft", 1, 3), ("s0", 0, 0), ("s1", 0, 0), ("x1", 2, 2), ("s2", 0, 0),
                 ("pre", 2, 3), ("kbd", 0, 1), ("exp", 2, 3), ("sums", 1, 3), ("feat", 1, 0), ("v0", 2, 2), ("v1", 2, 2), ("t1", 1, 0)]
        SLOT1 = [("scale", 2, 2), ("x0", 2, 3), ("s0", 0, 1), ("s1", 0, 1), ("t2", 1, 0), ("x1", 2, 3), ("s2", 0, 1),
                 ("kbd", 0, 2), ("t3", 1, 0), ("soft", 0, 0), ("sums", 0, 0), ("mean", 0, 0), ("pre", 1, 0), ("v0", 2, 3), ("v1", 2, 3)]
        SLOT2 = [("scale", 2, 3), ("soft", 0, 1), ("s0", 0, 2), ("s1", 0, 2), ("s2", 0, 2), ("collect", 2, 0), ("pre", 1, 1), ("kbd", 0, 3),
                 ("values", 0, 0), ("context", -1, 0), ("mix", 2, 0), ("exp", 1, 0), ("x0", 1, 0), ("mean0", 2, 0), ("x1", 1, 0),
                 ("keys", -1, 0), ("exp", 1, 1), ("sums", 0, 1), ("v0", 1, 0), ("v1", 1, 0)]
        SLOT3 = [("scale", 1, 0), ("x0", 1, 1), ("soft", 0, 2), ("s0", 0, 3), ("s1", 0, 3), ("x1", 1, 1), ("s2", 0, 3), ("queries", -1, 0),
                 ("pre", 1, 2), ("kbd", -1, 0), ("exp", 1, 2), ("sums", 0, 2), ("v0", 1, 1), ("var0", 2, 0), ("v1", 1, 1)]
        TEMPER_ONLY = ("soft", "sums", "feat", "mean", "t1", "t2", "t3", "pre")
        ORDER = [s for s in SLOT0 + SLOT1 + SLOT2 + SLOT3 if temper or s[0] not in TEMPER_ONLY]
        LOOP = (2, NG - 1)

        def run(engine, step):
            def peeled(g):
                for kind, lag, b in ORDER:
                    if 0 <= g - lag < NG:
                        step(kind, g - lag, b)
            for g in range(-1, LOOP[0]):
                peeled(g)
            with engine.Fori(*LOOP) as g:
                for kind, lag, b in ORDER:
                    step(kind, g - lag, b)
            for g in range(LOOP[1], NG + 2):
                peeled(g)

        if turn:
            load_transposed(nc, const, f"{tag}_w", [(w[n][:, :], a) for n, a in zip("qkvo", (wq, wk, wv, wo))], ps_t)
        NPRE = 5
        with nc.Block() as block:

            @block.sync
            def _(sp):
                loads = [(bias["q"][:, :], bq.rearrange("(p a) -> p a", a=1)), (bias["k"][:, :], bk.rearrange("(p a) -> p a", a=1)),
                         (bias["o"][:, :], bo.rearrange("(p a) -> p a", a=1)), (bv_row[:, :], bv.partition_broadcast(S))]
                if not turn:
                    loads += [(w[n][:, :], a) for n, a in zip("qkvo", (wq, wk, wv, wo))]
                for dst, src in loads:
                    sp.dma_start(dst, src).then_inc(loaded.sem, DMA)
                if temper:
                    sp.wait_ge(masked.sem, 2 + NPRE)
                    for dst, src in ((w1raw[:, :, :].rearrange("p a b -> p (a b)"), tw1.rearrange("a b -> (a b)").partition_broadcast(P)),
                                     (mb1[0:MLP, :], tb1.rearrange("(p a) -> p a", a=1)), (mb2[0:MLP, :], tb2.rearrange("(p a) -> p a", a=1)),
                                     (w3raw[0:MLP, :], tw3.rearrange("a p -> p a")), (mb3[:, :], tb3.partition_broadcast(P))):
                        sp.dma_start(dst, src, allow_slow_non_contiguous=True).then_inc(loaded.sem, DMA)
                sp.wait_ge(loaded.sem, (len(loads) + (5 if temper else 0)) * DMA)

            @block.gpsimd
            def _(pool):
                pool.memset(heads[:, :], 1.0).then_inc(masked.sem, 1)
                pool.wait_ge(masked.sem, 1)
                pool.affine_select(out=heads[:, :], in_=heads[:, :], compare_op=ALU.is_ge, fill=0.0, base=0,
                                   pattern=[[-DK, H]], channel_multiplier=1).then_inc(masked.sem, 1)
                if temper:
                    for z in (w1b[:, :, :], w2T[:, :], w3raw[:, :], mb1[:, :], mb2[:, :]):
                        pool.memset(z, 0.0).then_inc(masked.sem, 1)
                    pool.memset(half[:, :], float(np.log(0.5)))
                pool.wait_ge(masked.sem, 2)
                pool.affine_select(out=heads[:, :], in_=heads[:, :], compare_op=ALU.is_ge, fill=0.0, base=DK - 1,
                                   pattern=[[DK, H]], channel_multiplier=-1)

            @block.vector
            def _(dve):
                nc.vector.memset(vaug[:, :, :, DK:DK + 1], 1.0)
                if temper:
                    dve.wait_ge(loaded.sem, (4 + 5) * DMA)
                    root = float(np.sqrt(DK))
                    for f, s in enumerate((1.0 / (root * T * S), 1.0 / (root * T), 1.0 / T)):
                        nc.vector.tensor_scalar(w1b[:, f, 0:MLP], w1raw[:, :, f], s, None, ALU.mult)
                    nc.vector.tensor_scalar(w3b[:, :], const["ones"][:, :], w3raw[:, 0:1], None, ALU.mult)
        if temper:
            load_transposed(nc, const, f"{tag}_w2", [(w2T[:, :], tw2)], ps_t)

        def one(a, n, *rest):
            return a[(slice(None), bass.ds(n, 1)) + rest].rearrange("p a n -> p (a n)")

        def ring(j, b):
            return (j & 1) * GB + b

        with nc.Block() as block:

            @block.sync
            def _(sp):
                def load(first):
                    sp.dma_start(ctx_in[:, :, :], context[first].rearrange("b s d -> s b d")).then_inc(ctx_loaded.sem, DMA)
                load(slice(0, GB))
                with sp.Fori(0, NG - 1) as j:
                    sp.wait_ge(ctx_turned.sem, ctx_turned.after(j))
                    load(bass.ds((j + 1) * GB, GB))

            @block.tensor
            def _(pe):
                mm, turn_ = nc.tensor.matmul, nc.tensor.transpose
                ident = const["ident"]

                def step(kind, j, b):
                    if kind == "context":
                        pe.wait_ge(ctx_loaded.sem, ctx_loaded.after(j))
                        pe.wait_ge(v_ready.sem, v_ready.free(j))
                        for c in range(GB):
                            last = turn_(ps_x[:, c * S:(c + 1) * S], ctx_in[:, c, :], ident[0:S, 0:S])
                        last.then_inc(ctx_turned.sem, 1)
                    elif kind == "keys":
                        pe.wait_ge(ct_ready.sem, ct_ready.after(j))
                        mm(ps_x[:, 0:KS], w["k"][:, :], cT[:, :], start=True, stop=True).then_inc(k_mm.sem, 1)
                    elif kind == "queries":
                        pe.wait_ge(k_ready.sem, k_ready.after(j))
                        mm(ps_x[:, :], w["q"][:, :], group_of(xT, j, 0, 1), start=True, stop=True).then_inc(q_mm.sem, 1)
                    elif kind == "values":
                        pe.wait_ge(q_ready.sem, q_ready.after(j))
                        if temper:
                            pe.wait_ge(lt_ready.sem, lt_ready.free(j))
                        for c in range(GB):
                            last = mm(ps_x[0:S, c * D:(c + 1) * D], cT[:, c * S:(c + 1) * S], w["v"][:, :], start=True, stop=True)
                        last.then_inc(v_mm.sem, 1)
                    elif kind in ("s0", "s1", "s2"):
                        k = int(kind[1])
                        if k == 0:
                            pe.wait_ge(kbd_ready.sem, kbd_ready.after(j, b + 1))
                            if b == 0:
                                pe.wait_ge(q_ready.sem, q_ready.after(j))
                        pe.wait_ge(d_ready[k].sem, d_ready[k].free(j, b))
                        h0, nh = UNITS[k]
                        mm(ps_s[:, k, 0:nh * S], q[:, b * T:(b + 1) * T], kbd[b % 2][:, h0:h0 + nh, :].rearrange("p h s -> p (h s)"),
                           start=True, stop=True).then_inc(s_mm[k].sem, 1)
                    elif kind in ("x0", "x1"):
                        half_ = int(kind[1])
                        if half_ == 0:
                            pe.wait_ge(p_ready.sem, p_ready.after(j, b + 1))
                        for r in range(2):
                            pe.wait_ge(pt_ready[r].sem, pt_ready[r].free(j, 2 * b + half_))
                            for h in range(4):
                                last = turn_(ps_t[r][0:S, h * T:(h + 1) * T], probs[b % 2][:, 8 * half_ + 4 * r + h, :], ident[:, :])
                            last.then_inc(t_mm[r].sem, 1)
                    elif kind in ("v0", "v1"):
                        half_ = int(kind[1])
                        for r in range(2):
                            pe.wait_ge(pt_ready[r].sem, pt_ready[r].after(j, 2 * b + half_ + 1))
                        if half_ == 0:
                            pe.wait_ge(o_ready.sem, o_ready.free(j, b))
                            if b == 0:
                                pe.wait_ge(v_ready.sem, v_ready.after(j))
                        for h in range(8 * half_, 8 * half_ + 8):
                            last = mm(ps_o[:, h * (DK + 1):(h + 1) * (DK + 1)], pt[b % 2][:, h * T:(h + 1) * T],
                                      one(vaug, j * GB + b, h, slice(None)), start=True, stop=True)
                        if half_:
                            last.then_inc(pv_mm.sem, 1)
                    elif kind == "t1":
                        pe.wait_ge(feat_ready.sem, feat_ready.after(j))
                        if isinstance(j, int) and j == NG - 1:
                            pe.wait_ge(v_ready.sem, v_ready.after(j))
                        else:
                            pe.wait_ge(q_ready.sem, q_ready.after(j + 1))
                        for f, feat in enumerate((mean_f[:, :, :], m[:, bass.ds(j * GB, GB), :], var_f[:, :, :])):
                            last = mm(ps_x[:, 0:GB * H], w1b[:, f, :], feat.rearrange("p b h -> p (b h)"), start=(f == 0), stop=(f == 2))
                        last.then_inc(hid_mm.sem, 1)
                    elif kind == "t2":
                        pe.wait_ge(g1_ready.sem, g1_ready.after(j))
                        mm(ps_x[:, 0:GB * H], w2T[:, :], g1[:, :], start=True, stop=True).then_inc(h2_mm.sem, 1)
                    elif kind == "t3":
                        pe.wait_ge(g2_ready.sem, g2_ready.after(j))
                        mm(ps_x[:, 0:GB * H], w3b[:, :], g2[:, :], start=True, stop=True).then_inc(logt_mm.sem, 1)
                    elif kind == "collect":
                        pe.wait_ge(o_ready.sem, o_ready.after(j, GB))
                        pe.wait_ge(norm.log_ready.sem, norm.log_ready.free(j))
                        for c in range(GB):
                            last = turn_(ps_n[:, c * T:(c + 1) * T], o[:, c, :, :].rearrange("p h d -> p (h d)"), ident[:, :])
                        last.then_inc(ot_mm.sem, 1)
                    elif kind == "mix":
                        pe.wait_ge(ot_ready.sem, ot_ready.after(j))
                        mm(ps_n[:, :], w["o"][:, :], oT[:, :], start=True, stop=True).then_inc(wo_mm.sem, 1)
                    elif kind == "mean0":
                        norm.mean(nc, pe, j, 0)
                    elif kind == "var0":
                        norm.variance(nc, pe, j, 0)

                run(pe, step)

            @block.scalar
            def _(act):
                f = nc.scalar.activation
                nc.scalar.preload_act_table_set(LN_EXP)

                def step(kind, j, b):
                    if kind == "context":
                        act.wait_ge(ctx_turned.sem, ctx_turned.after(j))
                        f(cT[:, :], ps_x[:, 0:KS], ACT.Copy).then_inc(ct_ready.sem, 1)
                    elif kind == "keys":
                        act.wait_ge(kbd_ready.sem, kbd_ready.free(j))
                        if temper:
                            act.wait_ge(mean_ready.sem, mean_ready.free(j))
                        act.wait_ge(k_mm.sem, k_mm.after(j))
                        f(kT[:, :], ps_x[:, 0:KS], ACT.Identity, bias=bias["k"][:, :]).then_inc(k_ready.sem, 1)
                    elif kind == "queries":
                        act.wait_ge(q_mm.sem, q_mm.after(j))
                        f(q[:, :], ps_x[:, :], ACT.Identity, bias=bias["q"][:, :]).then_inc(q_ready.sem, 1)
                    elif kind == "soft":
                        act.wait_ge(s2_ready.sem, s2_ready.free(j, b))
                        act.wait_ge(d_ready[2].sem, d_ready[2].after(j, b + 1))
                        f(e1[b % 2][:, :, :], dist[:, bass.ds(ring(j, b), 1), :, :].rearrange("p a h s -> p (a h) s"), ACT.Exp,
                          scale=DK ** -0.5).then_inc(e1_ready.sem, 1)
                        act.wait_ge(e1_ready.sem, e1_ready.after(j, b + 1))
                        f(e1sq[b % 2][:, :, :], e1[b % 2][:, :, :], ACT.Square).then_inc(e1sq_ready.sem, 1)
                    elif kind == "t1":
                        act.wait_ge(hid_mm.sem, hid_mm.after(j))
                        f(g1[:, :], ps_x[:, 0:GB * H], ACT.Gelu, bias=mb1[:, :]).then_inc(g1_ready.sem, 1)
                    elif kind == "t2":
                        act.wait_ge(h2_mm.sem, h2_mm.after(j))
                        f(g2[:, :], ps_x[:, 0:GB * H], ACT.Gelu, bias=mb2[:, :]).then_inc(g2_ready.sem, 1)
                    elif kind == "t3":
                        nc.scalar.preload_act_table_set(LN_EXP)
                        act.wait_ge(pre_ready.sem, pre_ready.after(j, 0))
                        act.wait_ge(lt_ready.sem, lt_ready.after(j, 2))
                        f(rt[:, :], lt[:, :], ACT.Exp, bias=half[:, :], scale=-1.0).then_inc(rt_ready.sem, 1)
                    elif kind == "exp":
                        if temper:
                            act.wait_ge(pre_ready.sem, pre_ready.after(j, b + 1))
                            f(probs[b % 2][:, :, :], probs[b % 2][:, :, :], ACT.Exp).then_inc(p_ready.sem, 1)
                        else:
                            act.wait_ge(t_mm[1].sem, t_mm[1].free(j, 2 * b + 1))
                            act.wait_ge(d_ready[2].sem, d_ready[2].after(j, b + 1))
                            f(probs[b % 2][:, :, :], dist[:, bass.ds(ring(j, b), 1), :, :].rearrange("p a h s -> p (a h) s"), ACT.Exp,
                              scale=DK ** -0.5).then_inc(p_ready.sem, 1)
                    elif kind in ("x0", "x1"):
                        half_ = int(kind[1])
                        if half_ == 0:
                            act.wait_ge(pv_mm.sem, pv_mm.free(j, b))
                        for r in range(2):
                            act.wait_ge(t_mm[r].sem, t_mm[r].after(j, 2 * b + half_ + 1))
                            c = 2 * half_ + r
                            f(pt[b % 2][:, 4 * c * T:4 * (c + 1) * T], ps_t[r][0:S, :], ACT.Relu).then_inc(pt_ready[r].sem, 1)
                    elif kind == "collect":
                        act.wait_ge(ot_mm.sem, ot_mm.after(j))
                        f(oT[:, :], ps_n[:, :], ACT.Copy).then_inc(ot_ready.sem, 1)
                    elif kind == "mean0":
                        norm.square(nc, act, j, 0)
                    elif kind == "var0":
                        norm.inverse(nc, act, j, 0)

                run(act, step)

            @block.gpsimd
            def _(pool):
                def step(kind, j, b):
                    if kind == "kbd":
                        if b == 0:
                            pool.wait_ge(k_ready.sem, k_ready.after(j))
                        pool.wait_ge(s_mm[2].sem, s_mm[2].free(j, b))
                        keys = kT[:, b * S:(b + 1) * S].unsqueeze(1).broadcast_to([P, H, S])
                        pool.tensor_tensor(kbd[b % 2][:, :, :], keys, heads[:, :].unsqueeze(2).broadcast_to([P, H, S]), ALU.mult).then_inc(kbd_ready.sem, 1)
                    elif kind == "pre":
                        if b == 0:
                            pool.wait_ge(rt_ready.sem, rt_ready.after(j))
                        pool.wait_ge(t_mm[1].sem, t_mm[1].free(j, 2 * b + 1))
                        r = rt[:, b * H:(b + 1) * H].unsqueeze(2).broadcast_to([P, H, S])
                        pool.tensor_tensor(probs[b % 2][:, :, :], dist[:, bass.ds(ring(j, b), 1), :, :].rearrange("p a h s -> p (a h) s"), r,
                                           ALU.mult).then_inc(pre_ready.sem, 1)

                run(pool, step)

            @block.vector
            def _(dve):
                v = nc.vector
                for c in given:
                    c.give(dve)

                def scores(k):
                    h0, nh = UNITS[k]
                    return ps_s[:, k, 0:nh * S].rearrange("p (h s) -> p h s", s=S)

                def greatest(j, b, k):
                    h0, nh = UNITS[k]
                    dve.wait_ge(s_mm[k].sem, s_mm[k].after(j, b + 1))
                    v.tensor_reduce(one(m, j * GB + b, slice(h0, h0 + nh)), scores(k), AX.X, ALU.max).then_inc(m_ready[k].sem, 1)

                def subtract(j, b, k):
                    h0, nh = UNITS[k]
                    dve.wait_ge(m_ready[k].sem, m_ready[k].after(j, b + 1))
                    v.tensor_tensor(dist[:, bass.ds(ring(j, b), 1), h0:h0 + nh, :].rearrange("p a h s -> p (a h) s"), scores(k),
                                    one(m, j * GB + b, slice(h0, h0 + nh)).unsqueeze(2).broadcast_to([P, nh, S]),
                                    ALU.subtract).then_inc(d_ready[k].sem, 1)

                def step(kind, j, b):
                    if kind == "values":
                        dve.wait_ge(v_mm.sem, v_mm.after(j))
                        row = bv_row[:, :].unsqueeze(1).broadcast_to([S, GB, D]).rearrange("p b (h d) -> p b h d", d=DK)
                        v.tensor_tensor(vaug[:, bass.ds(j * GB, GB), :, 0:DK], ps_x[0:S, :].rearrange("p (b h d) -> p b h d", b=GB, d=DK),
                                        row, ALU.add).then_inc(v_ready.sem, 1)
                    elif kind == "mean":
                        dve.wait_ge(q_ready.sem, q_ready.after(j))
                        v.tensor_reduce(qs[:, :], q[:, :].rearrange("p (b t) -> p b t", b=GB), AX.X, ALU.add)
                        v.tensor_reduce(ks[:, :], kT[:, :].rearrange("p (b s) -> p b s", b=GB), AX.X, ALU.add).then_inc(small.sem, 1)
                        dve.wait_ge(small.sem, small.after(j, 1))
                        v.tensor_tensor(qk[:, :], qs[:, :], ks[:, :], ALU.mult).then_inc(small.sem, 1)
                        dve.wait_ge(small.sem, small.after(j, 2))
                        dve.wait_ge(hid_mm.sem, hid_mm.free(j))
                        v.tensor_tensor(mean_f[:, :, :], heads[:, :].unsqueeze(1).broadcast_to([P, GB, H]),
                                        qk[:, :].unsqueeze(2).broadcast_to([P, GB, H]), ALU.mult).then_inc(mean_ready.sem, 1)
                    elif kind == "s0":
                        used = pre_ready if temper else p_ready
                        dve.wait_ge(used.sem, used.free(j, b))
                        greatest(j, b, 0)
                    elif kind == "s1":
                        greatest(j, b, 1)
                        subtract(j, b, 0)
                    elif kind == "s2":
                        greatest(j, b, 2)
                        subtract(j, b, 1)
                        subtract(j, b, 2)
                    elif kind == "sums":
                        if b == 0:
                            dve.wait_ge(feat_ready.sem, feat_ready.free(j))
                        dve.wait_ge(e1_ready.sem, e1_ready.after(j, b + 1))
                        v.tensor_reduce(z1[:, b, :], e1[b % 2][:, :, :], AX.X, ALU.add)
                        dve.wait_ge(e1sq_ready.sem, e1sq_ready.after(j, b + 1))
                        v.tensor_reduce(s2[:, b, :], e1sq[b % 2][:, :, :], AX.X, ALU.add).then_inc(s2_ready.sem, 1)
                    elif kind == "feat":
                        dve.wait_ge(s2_ready.sem, s2_ready.after(j, GB))
                        v.reciprocal(z1[:, :, :], z1[:, :, :]).then_inc(small.sem, 1)
                        dve.wait_ge(small.sem, small.after(j, 3))
                        v.tensor_tensor(s2[:, :, :], s2[:, :, :], z1[:, :, :], ALU.mult).then_inc(small.sem, 1)
                        dve.wait_ge(small.sem, small.after(j, 4))
                        v.tensor_tensor(s2[:, :, :], s2[:, :, :], z1[:, :, :], ALU.mult).then_inc(small.sem, 1)
                        dve.wait_ge(small.sem, small.after(j, 5))
                        dve.wait_ge(hid_mm.sem, hid_mm.free(j))
                        v.tensor_scalar(var_f[:, :, :], s2[:, :, :], 1.0 / (S - 1), -1.0 / (S * (S - 1)), ALU.mult, ALU.add).then_inc(feat_ready.sem, 1)
                    elif kind == "t3":
                        dve.wait_ge(logt_mm.sem, logt_mm.after(j))
                        v.tensor_scalar(lt[:, :], ps_x[:, 0:GB * H], mb3[:, 0:1], LOG_T_MIN, ALU.add, ALU.max).then_inc(lt_ready.sem, 1)
                        dve.wait_ge(lt_ready.sem, lt_ready.after(j, 1))
                        v.tensor_scalar(lt[:, :], lt[:, :], LOG_T_MAX, None, ALU.min).then_inc(lt_ready.sem, 1)
                    elif kind == "scale":
                        dve.wait_ge(pv_mm.sem, pv_mm.after(j, b + 1))
                        heads_out = ps_o[:, 0:H * (DK + 1)].rearrange("p (h d) -> p h d", d=DK + 1)
                        v.tensor_scalar(zmax[b % 2][:, :], heads_out[:, :, DK:DK + 1].rearrange("p h a -> p (h a)"), 1e-30, None, ALU.max).then_inc(z_ready.sem, 1)
                        dve.wait_ge(z_ready.sem, z_ready.after(j, b + 1))
                        v.reciprocal(rz[b % 2][:, :], zmax[b % 2][:, :]).then_inc(rz_ready.sem, 1)
                        dve.wait_ge(rz_ready.sem, rz_ready.after(j, b + 1))
                        dve.wait_ge(ot_mm.sem, ot_mm.free(j))
                        v.tensor_tensor(o[:, b, :, :], heads_out[:, :, 0:DK], rz[b % 2][:, :].unsqueeze(2).broadcast_to([P, H, DK]),
                                        ALU.mult).then_inc(o_ready.sem, 1)
                    elif kind == "mix":
                        dve.wait_ge(wo_mm.sem, wo_mm.after(j))
                        v.scalar_tensor_tensor(y[:, :], ps_n[:, :], bias["o"][:, 0:1], group_of(xT, j, 0, 1), ALU.add, ALU.add).then_inc(norm.y_ready.sem, 1)
                    elif kind == "mean0":
                        norm.centre(nc, dve, j, 0)
                    elif kind == "var0":
                        norm.divide(nc, dve, j, 0, group_of(xT, j, 0, 1), xT_ready)

                run(dve, step)
        t.clear_counts()


class DoubleNorm:

    def __init__(self, t, const, name, per, y, sq, logs, inv, bank, gamma, beta):
        self.own = Norm(t, const, f"{name}_own", per, y, sq, logs, inv, bank)
        self.stream = Norm(t, const, f"{name}_str", per, y, sq, logs, inv, bank)
        self.gained = t.count(f"{name}_gained", per)
        self.gamma, self.beta = gamma, beta

    def give(self, engine):
        self.own.log_ready.give(engine)
        self.stream.log_ready.give(engine)

    def tensor(self, nc, pe, i, n):
        self.own.tensor(nc, pe, i, n)
        self.stream.tensor(nc, pe, i, n)

    def scalar(self, nc, act, i, n):
        self.own.scalar(nc, act, i, n)
        self.stream.scalar(nc, act, i, n)

    def gain(self, nc, dve, i, n, x):
        y = self.own.y[:, :]
        dve.wait_ge(self.own.inv_ready.sem, self.own.inv_ready.after(i, n + 1))
        nc.vector.scalar_tensor_tensor(y, y, self.gamma[:, 0:1], self.own.inv[:, :], ALU.mult, ALU.mult).then_inc(self.gained.sem, 1)
        dve.wait_ge(self.gained.sem, self.gained.after(i, n + 1))
        nc.vector.scalar_tensor_tensor(y, y, self.beta[:, 0:1], x, ALU.add, ALU.add).then_inc(self.stream.y_ready.sem, 1)

    def vector(self, nc, dve, i, n, x, out, done):
        self.own.centre(nc, dve, i, n)
        self.gain(nc, dve, i, n, x)
        self.stream.centre(nc, dve, i, n)
        self.stream.divide(nc, dve, i, n, out, done)


class Chain:

    def __init__(self, t, name, engine):
        self.done, self.engine, self.n = t.count(name), engine, 0

    def __call__(self, instruction):
        instruction.then_inc(self.done.sem, 1)
        self.n += 1
        self.engine.wait_ge(self.done.sem, self.n)


TILES, CLUSTERS, TPC = 64, 8, 8
COMP, GRID, KNOTS = 32, 16, 8


def first_max_one_hot(link, v, g, top, cand, iota, n):
    wide = lambda a: a.unsqueeze(2).broadcast_to([P, B, n])
    link(v.tensor_reduce(top, g, AX.X, ALU.max))
    link(v.tensor_tensor(cand, g, wide(top), ALU.is_equal))
    link(v.scalar_tensor_tensor(cand, cand, -float(n), iota, ALU.mult, ALU.add))
    link(v.tensor_reduce(top, cand, AX.X, ALU.min))
    link(v.tensor_tensor(cand, cand, wide(top), ALU.is_equal))


def tile_ffn(nc, const, xT, raw, knots, temp, cw1, cb1, cw2, cb2, sw1, sb1, sw2, sb2, dirs, gamma, beta, scale):
    with ExitStack() as ctx:
        t = Tools(ctx, nc, "ffn")
        U = 2
        ITER = NG // U
        NS = CLUSTERS + TILES
        TAB = 3 * GRID + GRID + 1
        rawT = t.sb("rawT", [P, TILES])
        sig = t.sb("sig", [P, NS])
        q = t.sb("q", [P, TILES])
        lt = t.sb("lt", [P, TILES])
        csum = t.sb("csum", [P, CLUSTERS])
        cneg = t.sb("cneg", [P, CLUSTERS])
        w1 = t.sb("w1", [P, COMP])
        b1 = t.sb("b1", [COMP, 1])
        w2 = t.sb("w2", [COMP, 2])
        b2 = t.sb("b2", [P, 2])
        table = t.sb("table", [TILES, TAB])
        dir_sb = t.sb("dirs", [TILES, D])
        knot = t.sb("knot", [P, KNOTS])
        slope = t.sb("slope", [P, KNOTS])
        nit = t.sb("nit", [P, 1])
        scale_c = t.sb("scale", [P, 1])
        gamma_c, beta_c = t.sb("gamma", [P, 1]), t.sb("beta", [P, 1])
        iota_i = t.sb("iota_i", [P, B, TPC], I32)
        iota = t.sb("iota", [P, B, TPC])
        scores = t.sb("scores", [P, B, NS])
        comp = t.sb("comp", [P, B, 2])
        xs = [t.sb(f"xs{u}", [P, GROUP]) for u in range(U)]
        hid = [t.sb(f"hid{u}", [COMP, GROUP]) for u in range(U)]
        e = t.sb("e", [P, B * 8])
        low = t.sb("low", [P, B * 8])
        frac = t.sb("frac", [P, B * 8])
        term = t.sb("term", [P, B * 8])
        inc = t.sb("inc", [P, B * 8])
        gates = t.sb("gates", [P, B * 8])
        top = t.sb("top", [P, B])
        cluster = t.sb("cluster", [P, B, CLUSTERS])
        local = t.sb("local", [P, B, TPC])
        picked = t.sb("picked", [P, B, CLUSTERS, TPC])
        mine = t.sb("mine", [P, B, TPC])
        oh = [t.sb(f"oh{u}", [P, GB, P]) for u in range(U)]
        ohm = [t.sb(f"ohm{u}", [P, GB, P]) for u in range(U)]
        ohT = [t.sb(f"ohT{u}", [TILES, GROUP]) for u in range(U)]
        ohmT = [t.sb(f"ohmT{u}", [TILES, GROUP]) for u in range(U)]
        ha = t.sb("ha", [P, GB, GRID])
        hb = t.sb("hb", [P, GB, GRID])
        mag = t.sb("mag", [P, GB])
        y, sq = t.sb("y", [P, GROUP]), t.sb("sq", [P, GROUP])
        logs, inv = t.sb("logs", [P, GROUP]), t.sb("inv", [P, GROUP])
        ps_a = [t.ps(f"bank_a{u}", [P, 512]) for u in range(U)]
        ps_b = [t.ps(f"bank_b{u}", [P, 512]) for u in range(U)]
        ps_c = [t.ps(f"bank_c{u}", [P, 512]) for u in range(U)]
        ps_n = t.ps("norm", [P, 512])

        load_transposed(nc, const, "ffn_sig", [(rawT[:, :], raw)], ps_a)
        loaded = t.count("loaded", weight=DMA)
        N_LOADS = 15
        table_zeroed = t.count("table_zeroed")
        xs_ready = t.count("xs_ready", U)
        sc_mm = t.count("sc_mm", U)
        sc_kept = t.count("sc_kept", U, credits=U)
        hid_mm = t.count("hid_mm", U)
        hid_ready = t.count("hid_ready", U, credits=U)
        comp_mm = t.count("comp_mm", U)
        comp_kept = t.count("comp_kept", U, credits=U)
        sig_ready = t.count("sig_ready")
        iota_made = t.count("iota_made")
        with nc.Block() as block:

            @block.sync
            def _(sp):
                col = lambda a: a.rearrange("(p a) -> p a", a=1)
                loads = [(w1[:, :], cw1), (b1[:, :], col(cb1)), (w2[:, :], cw2), (b2[:, :], cb2.partition_broadcast(P)),
                         (knot[:, :], knots.partition_broadcast(P)), (nit[:, :], temp.partition_broadcast(P)),
                         (scale_c[:, :], scale.partition_broadcast(P)), (gamma_c[:, :], col(gamma)), (beta_c[:, :], col(beta)),
                         (dir_sb[:, :], dirs), (table[:, 0:2 * GRID], sw1.rearrange("n i g -> n (i g)")),
                         (table[:, 2 * GRID:3 * GRID], sb1), (table[:, 3 * GRID:4 * GRID], sw2.rearrange("n g a -> n (g a)")),
                         (table[:, 4 * GRID:], sb2)]
                for dst, src in loads:
                    sp.dma_start(dst, src).then_inc(loaded.sem, DMA)

            @block.gpsimd
            def _(pool):
                pool.iota(iota_i[:, :, :], pattern=[[0, B], [1, TPC]], base=0, channel_multiplier=0).then_inc(iota_made.sem, 1)

            @block.vector
            def _(dve):
                v = nc.vector
                for a in (*oh, *ohm):
                    v.memset(a[:, :, TILES:], 0.0)
                link = Chain(t, "setup", dve)
                for c in (sc_kept, hid_ready, comp_kept):
                    c.give(dve)
                signs = sig[:, CLUSTERS:]
                link(v.tensor_scalar(q[:, :], rawT[:, :], 0.3, None, ALU.is_gt))
                link(v.tensor_scalar(lt[:, :], rawT[:, :], -0.3, None, ALU.is_lt))
                link(v.tensor_tensor(q[:, :], q[:, :], lt[:, :], ALU.subtract))
                link(v.tensor_tensor(q[:, :], q[:, :], rawT[:, :], ALU.subtract))
                link(v.tensor_tensor(signs, rawT[:, :], q[:, :], ALU.add))
                link(v.tensor_reduce(csum[:, :], signs.rearrange("p (c t) -> p c t", t=TPC), AX.X, ALU.add))
                link(v.tensor_scalar(cneg[:, :], csum[:, :], 0.0, None, ALU.is_lt))
                link(v.tensor_scalar(csum[:, :], csum[:, :], 0.0, None, ALU.is_gt))
                link(v.tensor_tensor(sig[:, 0:CLUSTERS], csum[:, :], cneg[:, :], ALU.subtract))
                dve.wait_ge(loaded.sem, 14 * DMA)
                link(v.tensor_tensor(slope[:, 0:KNOTS - 1], knot[:, 1:KNOTS], knot[:, 0:KNOTS - 1], ALU.subtract))
                link(v.tensor_scalar(nit[:, :], nit[:, :], 1e-6, None, ALU.add))
                link(v.reciprocal(nit[:, :], nit[:, :]))
                link(v.tensor_scalar(nit[:, :], nit[:, :], -1.0, None, ALU.mult))
                dve.wait_ge(iota_made.sem, 1)
                link(v.tensor_copy(iota[:, :, :], iota_i[:, :, :]))

        with nc.Block() as block:

            @block.tensor
            def _(pe):
                mm = nc.tensor.matmul
                with pe.Fori(0, ITER) as i:
                    for u in range(U):
                        pe.wait_ge(xs_ready.sem, xs_ready.after(i, u + 1))
                        pe.wait_ge(sc_kept.sem, sc_kept.free(i, u))
                        for b in range(GB):
                            last = mm(ps_a[u][:, b * NS:(b + 1) * NS], xs[u][:, b * T:(b + 1) * T], sig[:, :], start=True, stop=True)
                        last.then_inc(sc_mm.sem, 1)
                        pe.wait_ge(hid_ready.sem, hid_ready.free(i, u))
                        mm(ps_b[u][0:COMP, :], w1[:, :], xs[u][:, :], start=True, stop=True).then_inc(hid_mm.sem, 1)
                    for u in range(U):
                        pe.wait_ge(hid_ready.sem, hid_ready.after(i, u + 1))
                        pe.wait_ge(comp_kept.sem, comp_kept.free(i, u))
                        for b in range(GB):
                            last = mm(ps_c[u][:, 2 * b:2 * b + 2], hid[u][:, b * T:(b + 1) * T], w2[:, :], start=True, stop=True)
                        last.then_inc(comp_mm.sem, 1)

            @block.scalar
            def _(act):
                f = nc.scalar.activation
                with act.Fori(0, ITER) as i:
                    for u in range(U):
                        act.wait_ge(hid_ready.sem, hid_ready.free(i, u))
                        f(xs[u][:, :], group_of(xT, i, u, U), ACT.Copy).then_inc(xs_ready.sem, 1)
                    for u in range(U):
                        act.wait_ge(hid_mm.sem, hid_mm.after(i, u + 1))
                        act.wait_ge(comp_kept.sem, comp_kept.free(i, u))
                        f(hid[u][:, :], ps_b[u][0:COMP, :], ACT.Gelu, bias=b1[:, :]).then_inc(hid_ready.sem, 1)

            @block.vector
            def _(dve):
                v = nc.vector
                with dve.Fori(0, ITER) as i:
                    for u in range(U):
                        first = i * (U * GB) + u * GB
                        dve.wait_ge(sc_mm.sem, sc_mm.after(i, u + 1))
                        v.tensor_copy(scores[:, bass.ds(first, GB), :], ps_a[u][:, 0:GB * NS].rearrange("p (b n) -> p b n", b=GB)).then_inc(sc_kept.sem, 1)
                    for u in range(U):
                        first = i * (U * GB) + u * GB
                        dve.wait_ge(comp_mm.sem, comp_mm.after(i, u + 1))
                        v.tensor_tensor(comp[:, bass.ds(first, GB), :], ps_c[u][:, 0:GB * 2].rearrange("p (b n) -> p b n", b=GB),
                                        b2[:, :].unsqueeze(1).broadcast_to([P, GB, 2]), ALU.add).then_inc(comp_kept.sem, 1)

        exp_asked = t.count("exp_asked")
        exp_ready = t.count("exp_ready")
        with nc.Block() as block:

            @block.scalar
            def _(act):
                f = nc.scalar.activation
                f(comp[:, :, :], comp[:, :, :], ACT.Tanh)
                e3 = e[:, :].rearrange("p (b n) -> p b n", n=8)
                f(e3, scores[:, :, 0:CLUSTERS], ACT.Exp, scale=nit[:, :]).then_inc(exp_ready.sem, 1)
                act.wait_ge(exp_asked.sem, 1)
                f(e3, mine[:, :, :], ACT.Exp, scale=nit[:, :]).then_inc(exp_ready.sem, 1)

            @block.vector
            def _(dve):
                v = nc.vector
                link = Chain(t, "route", dve)

                def calibrate(n):
                    dve.wait_ge(exp_ready.sem, n)
                    link(v.tensor_scalar(e[:, :], e[:, :], 1.0, None, ALU.add))
                    link(v.reciprocal(e[:, :], e[:, :]))
                    link(v.tensor_scalar(e[:, :], e[:, :], float(KNOTS - 1), None, ALU.mult))
                    link(v.tensor_scalar(low[:, :], e[:, :], 1.0, None, ALU.is_ge))
                    for k in range(2, KNOTS - 1):
                        link(v.scalar_tensor_tensor(low[:, :], e[:, :], float(k), low[:, :], ALU.is_ge, ALU.add))
                    v.tensor_tensor(frac[:, :], e[:, :], low[:, :], ALU.subtract)
                    v.tensor_scalar(gates[:, :], low[:, :], 0.0, knot[:, 0:1], ALU.is_equal, ALU.mult)
                    link(v.tensor_scalar(inc[:, :], low[:, :], 0.0, slope[:, 0:1], ALU.is_equal, ALU.mult))
                    for k in range(1, KNOTS - 1):
                        for acc, of in ((gates, knot), (inc, slope)):
                            link(v.tensor_scalar(term[:, :], low[:, :], float(k), of[:, k:k + 1], ALU.is_equal, ALU.mult))
                            link(v.tensor_tensor(acc[:, :], acc[:, :], term[:, :], ALU.add))
                    link(v.tensor_tensor(inc[:, :], inc[:, :], frac[:, :], ALU.mult))
                    link(v.tensor_tensor(gates[:, :], gates[:, :], inc[:, :], ALU.add))

                g3 = gates[:, :].rearrange("p (b n) -> p b n", n=8)
                calibrate(1)
                first_max_one_hot(link, v, g3, top[:, :], cluster[:, :, :], iota[:, :, :], CLUSTERS)
                link(v.tensor_tensor(picked[:, :, :, :], scores[:, :, CLUSTERS:].rearrange("p b (c j) -> p b c j", c=CLUSTERS),
                                     cluster[:, :, :].unsqueeze(3).broadcast_to([P, B, CLUSTERS, TPC]), ALU.mult))
                v.tensor_reduce(mine[:, :, :], picked[:, :, :, :].rearrange("p b c j -> p b j c"), AX.X, ALU.add).then_inc(exp_asked.sem, 1)
                calibrate(2)
                first_max_one_hot(link, v, g3, top[:, :], local[:, :, :], iota[:, :, :], TPC)

        oh_ready = t.count("oh_ready", U)
        ohT_mm = t.count("ohT_mm", U)
        ohT_ready = t.count("ohT_ready", U)
        row_mm = t.count("row_mm", U)
        mag_steps = 8
        hh = t.count("hh", mag_steps * U)
        ohm_ready = t.count("ohm_ready", U)
        ohmT_mm = t.count("ohmT_mm", U)
        ohmT_ready = t.count("ohmT_ready", U)
        dir_mm = t.count("dir_mm", U)
        xT_ready = t.count("xT_ready", U)
        norm = DoubleNorm(t, const, "ln", U, y, sq, logs, inv, ps_n, gamma_c, beta_c)
        a_free = t.count("a_free", U, credits=U)
        with nc.Block() as block:

            @block.tensor
            def _(pe):
                mm, turn = nc.tensor.matmul, nc.tensor.transpose
                with pe.Fori(0, ITER) as i:
                    for u in range(U):
                        pe.wait_ge(oh_ready.sem, oh_ready.after(i, u + 1))
                        pe.wait_ge(a_free.sem, a_free.free(i, u))
                        for b in range(GB):
                            last = turn(ps_a[u][:, b * T:(b + 1) * T], oh[u][:, b, :], const["ident"][:, :])
                        last.then_inc(ohT_mm.sem, 1)
                    for u in range(U):
                        pe.wait_ge(ohT_ready.sem, ohT_ready.after(i, u + 1))
                        for b in range(GB):
                            last = mm(ps_b[u][:, b * TAB:(b + 1) * TAB], ohT[u][:, b * T:(b + 1) * T], table[:, :], start=True, stop=True)
                        last.then_inc(row_mm.sem, 1)
                    for u in range(U):
                        pe.wait_ge(ohm_ready.sem, ohm_ready.after(i, u + 1))
                        for b in range(GB):
                            last = turn(ps_c[u][:, b * T:(b + 1) * T], ohm[u][:, b, :], const["ident"][:, :])
                        last.then_inc(ohmT_mm.sem, 1)
                    for u in range(U):
                        pe.wait_ge(ohmT_ready.sem, ohmT_ready.after(i, u + 1))
                        mm(ps_a[u][:, :], dir_sb[:, :], ohmT[u][:, :], start=True, stop=True).then_inc(dir_mm.sem, 1)
                        norm.tensor(nc, pe, i, u)

            @block.scalar
            def _(act):
                f = nc.scalar.activation
                with act.Fori(0, ITER) as i:
                    nc.scalar.preload_act_table_set(LN_EXP)
                    for u in range(U):
                        act.wait_ge(ohT_mm.sem, ohT_mm.after(i, u + 1))
                        f(ohT[u][:, :], ps_a[u][0:TILES, :], ACT.Copy).then_inc(ohT_ready.sem, 1)
                    for u in range(U):
                        act.wait_ge(ohmT_mm.sem, ohmT_mm.after(i, u + 1))
                        f(ohmT[u][:, :], ps_c[u][0:TILES, :], ACT.Copy).then_inc(ohmT_ready.sem, 1)
                    for u in range(U):
                        norm.scalar(nc, act, i, u)

            @block.vector
            def _(dve):
                v = nc.vector
                a_free.give(dve)
                norm.give(dve)
                with dve.Fori(0, ITER) as i:
                    for u in range(U):
                        first = i * (U * GB) + u * GB
                        shape = [P, GB, CLUSTERS, TPC]
                        v.tensor_tensor(oh[u][:, :, 0:TILES].rearrange("p b (c j) -> p b c j", c=CLUSTERS),
                                        cluster[:, bass.ds(first, GB), :].unsqueeze(3).broadcast_to(shape),
                                        local[:, bass.ds(first, GB), :].unsqueeze(2).broadcast_to(shape), ALU.mult).then_inc(oh_ready.sem, 1)
                    for u in range(U):
                        first = i * (U * GB) + u * GB
                        rows = ps_b[u][:, 0:GB * TAB].rearrange("p (b n) -> p b n", b=GB)
                        dve.wait_ge(row_mm.sem, row_mm.after(i, u + 1))
                        step = [u * mag_steps]

                        def link(instruction):
                            instruction.then_inc(hh.sem, 1)
                            step[0] += 1
                            dve.wait_ge(hh.sem, hh.after(i, step[0]))

                        c = lambda n: comp[:, bass.ds(first, GB), n:n + 1].broadcast_to([P, GB, GRID])
                        v.tensor_tensor(ha[:, :, :], rows[:, :, 0:GRID], c(0), ALU.mult)
                        link(v.tensor_tensor(hb[:, :, :], rows[:, :, GRID:2 * GRID], c(1), ALU.mult))
                        link(v.tensor_tensor(ha[:, :, :], ha[:, :, :], hb[:, :, :], ALU.add))
                        link(v.tensor_tensor(ha[:, :, :], ha[:, :, :], rows[:, :, 2 * GRID:3 * GRID], ALU.add))
                        link(v.tensor_scalar(ha[:, :, :], ha[:, :, :], 0.0, None, ALU.max))
                        link(v.tensor_tensor(ha[:, :, :], ha[:, :, :], rows[:, :, 3 * GRID:4 * GRID], ALU.mult))
                        link(v.tensor_reduce(mag[:, :], ha[:, :, :], AX.X, ALU.add))
                        link(v.tensor_tensor(mag[:, :], mag[:, :], rows[:, :, 4 * GRID:TAB].rearrange("p b a -> p (b a)"), ALU.add))
                        link(v.tensor_scalar(mag[:, :], mag[:, :], scale_c[:, 0:1], None, ALU.mult))
                        v.tensor_tensor(ohm[u][:, :, 0:TILES], oh[u][:, :, 0:TILES], mag[:, :].unsqueeze(2).broadcast_to([P, GB, TILES]), ALU.mult).then_inc(ohm_ready.sem, 1)
                    for u in range(U):
                        x = group_of(xT, i, u, U)
                        dve.wait_ge(dir_mm.sem, dir_mm.after(i, u + 1))
                        v.tensor_tensor(y[:, :], ps_a[u][:, :], x, ALU.add).then_inc(norm.own.y_ready.sem, 1)
                        dve.wait_ge(norm.own.y_ready.sem, norm.own.y_ready.after(i, u + 1))
                        dve.sem_inc(a_free.sem, 1)
                        norm.vector(nc, dve, i, u, x, x, xT_ready)
                        dve.wait_ge(xT_ready.sem, xT_ready.after(i, u + 1))
        t.clear_counts()


HD = 64
INNER = H * HD
PAIRS = H // 2
HALF = 4


def self_attention(nc, const, xT, scale, wq, bq, wk, bk, wv, bv, wo, bo, gamma, beta):
    with ExitStack() as ctx:
        t = Tools(ctx, nc, "self")
        HALVES = GB * 2
        w = {n: t.sb(f"w_{n}", [P, INNER]) for n in "qkvo"}
        bq_c, bk_c, sc_c = t.sb("bq", [P, PAIRS]), t.sb("bk", [P, PAIRS]), t.sb("scale", [P, PAIRS])
        bo_c, gamma_c, beta_c = t.sb("bo", [P, 1]), t.sb("gamma", [P, 1]), t.sb("beta", [P, 1])
        bv_row = t.sb("bv_row", [P, INNER])
        xs = t.sb("xs", [P, GROUP])
        qT, kT = t.sb("qT", [P, PAIRS, GROUP]), t.sb("kT", [P, PAIRS, GROUP])
        vs = t.sb("v", [P, GB, INNER])
        neg = [t.sb(f"neg{r}", [P, 2, HALF]) for r in range(2)]
        probs = [t.sb(f"probs{r}", [P, 2, HALF, T]) for r in range(2)]
        z = [t.sb(f"z{r}", [P, 2, HALF]) for r in range(2)]
        rz = [t.sb(f"rz{r}", [P, 2, HALF]) for r in range(2)]
        pt = [t.sb(f"pt{r}", [P, 2, HALF, T]) for r in range(2)]
        o = [t.sb(f"o{r}", [P, HALF, 2, HD]) for r in range(2)]
        oT = t.sb("oT", [P, PAIRS, GROUP])
        y, sq = t.sb("y", [P, GROUP]), t.sb("sq", [P, GROUP])
        logs, inv = t.sb("logs", [P, GROUP]), t.sb("inv", [P, GROUP])
        ps_s = [t.ps(f"scores{r}", [P, 2, 512]) for r in range(2)]
        ps_t = [t.ps(f"turned{r}", [P, 512]) for r in range(2)]
        ps_o = t.ps("out", [P, 512])
        ps_n = t.ps("norm", [P, 512])

        load_transposed(nc, const, "self_w", [(w[n][:, :], a) for n, a in zip("qkvo", (wq, wk, wv, wo))], ps_t)
        loaded = t.count("loaded", weight=DMA)
        scaled = t.count("scaled")
        with nc.Block() as block:

            @block.sync
            def _(sp):
                cols = lambda a: a.rearrange("(n p) -> p n", p=P)
                loads = [(bq_c[:, :], cols(bq)), (bk_c[:, :], cols(bk)), (bo_c[:, :], cols(bo)), (gamma_c[:, :], cols(gamma)),
                         (beta_c[:, :], cols(beta)), (bv_row[:, :], bv.partition_broadcast(P)),
                         (sc_c[0:HD, :], scale.rearrange("(c a) -> a c", a=2)[0:1, :].broadcast_to([HD, PAIRS])),
                         (sc_c[HD:P, :], scale.rearrange("(c a) -> a c", a=2)[1:2, :].broadcast_to([HD, PAIRS]))]
                for dst, src in loads:
                    sp.dma_start(dst, src, allow_slow_non_contiguous=True).then_inc(loaded.sem, DMA)

            @block.vector
            def _(dve):
                dve.wait_ge(loaded.sem, 8 * DMA)
                nc.vector.tensor_scalar(sc_c[:, :], sc_c[:, :], HD ** -0.5, None, ALU.mult).then_inc(scaled.sem, 1)
                dve.wait_ge(scaled.sem, 1)
                nc.vector.tensor_tensor(bq_c[:, :], bq_c[:, :], sc_c[:, :], ALU.mult)

        NQK = 2 * PAIRS
        NT_ = NQK // 2 + HALVES
        xs_ready = t.count("xs_ready")
        fill = [t.count(f"fill{r}", NT_) for r in range(2)]
        kept = [t.count(f"kept{r}", NT_, credits=1) for r in range(2)]
        v_mm = t.count("v_mm", GB)
        v_ready = t.count("v_ready", GB)
        s_mm = t.count("s_mm", HALVES)
        max_ready = t.count("max_ready", HALVES)
        neg_ready = t.count("neg_ready", HALVES)
        p_ready = t.count("p_ready", HALVES, credits=2)
        pv_mm = t.count("pv_mm", HALVES, credits=2)
        rz_ready = t.count("rz_ready", HALVES)
        o_ready = t.count("o_ready", HALVES)
        ot_mm = t.count("ot_mm", HALVES, credits=2)
        ot_ready = t.count("ot_ready", HALVES, credits=1)
        wo_mm = t.count("wo_mm")
        xT_ready = t.count("xT_ready")
        norm = DoubleNorm(t, const, "ln", 1, y, sq, logs, inv, ps_n, gamma_c, beta_c)

        def order(first, last):
            steps = []
            if not last:
                steps += [("project", 0)] + [("scores_a", 0), ("scores_b", 0), ("scores_a", 1), ("scores_b", 1)]
            if not first:
                steps.append(("mix", 0))
            for k in range(HALVES):
                if not last:
                    steps.append(("turn", k))
                    if k + 2 < HALVES:
                        steps.append(("scores_a", k + 2))
                    if k:
                        steps.append(("collect", k - 1))
                    if k + 2 < HALVES:
                        steps.append(("scores_b", k + 2))
                    steps.append(("attend", k))
                if not first and k < 4:
                    steps.append(("norm", k))
            if not last:
                steps.append(("collect", HALVES - 1))
            return steps

        def run(engine, step):
            for s in order(True, False):
                step(0, *s)
            with engine.Fori(1, NG) as i:
                for s in order(False, False):
                    step(i, *s)
            for s in order(False, True):
                step(NG, *s)

        with nc.Block() as block:

            @block.tensor
            def _(pe):
                mm, turn = nc.tensor.matmul, nc.tensor.transpose
                ident = const["ident"]

                def step(i, kind, k):
                    b, half = k // 2, k % 2
                    if kind == "project":
                        pe.wait_ge(xs_ready.sem, xs_ready.after(i))
                        for n in range(NQK):
                            r = n % 2
                            wt = w["q" if n < PAIRS else "k"]
                            pe.wait_ge(kept[r].sem, kept[r].free(i, n // 2))
                            c = n % PAIRS
                            mm(ps_t[r][:, :], wt[:, c * P:(c + 1) * P], xs[:, :], start=True, stop=True).then_inc(fill[r].sem, 1)
                        for c in range(GB):
                            if c < 2:
                                pe.wait_ge(p_ready.sem, p_ready.free(i, c))
                            else:
                                pe.wait_ge(v_ready.sem, v_ready.after(i, c - 1))
                            for j in range(2):
                                last = mm(ps_s[c % 2][:, j, :], xs[:, c * T:(c + 1) * T], w["v"][:, j * 512:(j + 1) * 512], start=True, stop=True)
                            last.then_inc(v_mm.sem, 1)
                    elif kind in ("scores_a", "scores_b"):
                        part = kind == "scores_b"
                        if part:
                            pass
                        elif k < 2:
                            pe.wait_ge(v_ready.sem, v_ready.after(i, GB - 1 + k))
                            if k == 0:
                                for r in range(2):
                                    pe.wait_ge(kept[r].sem, kept[r].after(i, NQK // 2))
                        else:
                            pe.wait_ge(p_ready.sem, p_ready.free(i, k))
                        for j in range(part * 2, part * 2 + 2):
                            c = half * HALF + j
                            for e in range(2):
                                rows = slice(e * HD, (e + 1) * HD)
                                last = mm(ps_s[k % 2][:, e, j * T:(j + 1) * T], qT[rows, c, b * T:(b + 1) * T],
                                          kT[rows, c, b * T:(b + 1) * T], start=True, stop=True)
                        if part:
                            last.then_inc(s_mm.sem, 1)
                    elif kind == "turn":
                        pe.wait_ge(p_ready.sem, p_ready.after(i, k + 1))
                        for e in range(2):
                            pe.wait_ge(kept[e].sem, kept[e].free(i, NQK // 2 + k))
                            for j in range(HALF):
                                last = turn(ps_t[e][:, j * T:(j + 1) * T], probs[k % 2][:, e, j, :], ident[:, :])
                            last.then_inc(fill[e].sem, 1)
                    elif kind == "attend":
                        for e in range(2):
                            pe.wait_ge(kept[e].sem, kept[e].after(i, NQK // 2 + k + 1))
                        pe.wait_ge(ot_ready.sem, ot_ready.free(i, k))
                        for j in range(HALF):
                            for e in range(2):
                                head = 2 * (half * HALF + j) + e
                                last = mm(ps_o[:, (2 * j + e) * HD:(2 * j + e + 1) * HD], pt[k % 2][:, e, j, :],
                                          vs[:, b, head * HD:(head + 1) * HD], start=True, stop=True)
                        last.then_inc(pv_mm.sem, 1)
                    elif kind == "collect":
                        pe.wait_ge(o_ready.sem, o_ready.after(i, k + 1))
                        for j in range(HALF):
                            last = turn(ps_o[:, j * T:(j + 1) * T], o[k % 2][:, j, :, :].rearrange("p e d -> p (e d)"), ident[:, :])
                        last.then_inc(ot_mm.sem, 1)
                    elif kind == "mix":
                        pe.wait_ge(ot_ready.sem, ot_ready.after(i - 1, HALVES))
                        pe.wait_ge(norm.stream.log_ready.sem, norm.stream.log_ready.free(i - 1))
                        for c in range(PAIRS):
                            last = mm(ps_n[:, :], w["o"][:, c * P:(c + 1) * P], oT[:, c, :], start=(c == 0), stop=(c == PAIRS - 1))
                        last.then_inc(wo_mm.sem, 1)
                    else:
                        which = norm.own if k < 2 else norm.stream
                        (which.variance if k % 2 else which.mean)(nc, pe, i - 1, 0)

                run(pe, step)

            @block.scalar
            def _(act):
                f = nc.scalar.activation

                def step(i, kind, k):
                    b, half = k // 2, k % 2
                    if kind == "project":
                        nc.scalar.preload_act_table_set(LN_EXP)
                        f(xs[:, :], group_of(xT, i, 0, 1), ACT.Copy).then_inc(xs_ready.sem, 1)
                        for n in range(0, NQK, 2):
                            c = n % PAIRS
                            act.wait_ge(fill[0].sem, fill[0].after(i, n // 2 + 1))
                            if n < PAIRS:
                                f(qT[:, c, :], ps_t[0][:, :], ACT.Identity, bias=bq_c[:, c:c + 1], scale=sc_c[:, c:c + 1]).then_inc(kept[0].sem, 1)
                            else:
                                f(kT[:, c, :], ps_t[0][:, :], ACT.Identity, bias=bk_c[:, c:c + 1]).then_inc(kept[0].sem, 1)
                    elif kind == "scores_b":
                        act.wait_ge(neg_ready.sem, neg_ready.after(i, k + 1))
                        act.wait_ge(pv_mm.sem, pv_mm.after(i, k - 1))
                        for e in range(2):
                            for j in range(HALF):
                                last = f(probs[k % 2][:, e, j, :], ps_s[k % 2][:, e, j * T:(j + 1) * T], ACT.Exp,
                                         bias=neg[k % 2][:, e, j:j + 1], accum_out=z[k % 2][:, e, j:j + 1])
                        last.then_inc(p_ready.sem, 1)
                    elif kind == "collect":
                        act.wait_ge(ot_mm.sem, ot_mm.after(i, k + 1))
                        f(oT[:, half * HALF:(half + 1) * HALF, b * T:(b + 1) * T], ps_o[:, :].rearrange("p (j t) -> p j t", t=T),
                          ACT.Copy).then_inc(ot_ready.sem, 1)
                    elif kind == "norm":
                        which = norm.own if k < 2 else norm.stream
                        (which.inverse if k % 2 else which.square)(nc, act, i - 1, 0)

                run(act, step)

            @block.vector
            def _(dve):
                v = nc.vector
                for c in (*kept, p_ready, pv_mm, ot_mm, ot_ready, norm):
                    c.give(dve)

                def step(i, kind, k):
                    b, half = k // 2, k % 2
                    if kind == "project":
                        for n in range(1, NQK, 2):
                            c = n % PAIRS
                            dve.wait_ge(fill[1].sem, fill[1].after(i, n // 2 + 1))
                            if n < PAIRS:
                                v.tensor_scalar(qT[:, c, :], ps_t[1][:, :], sc_c[:, c:c + 1], bq_c[:, c:c + 1], ALU.mult, ALU.add).then_inc(kept[1].sem, 1)
                            else:
                                v.tensor_scalar(kT[:, c, :], ps_t[1][:, :], bk_c[:, c:c + 1], None, ALU.add).then_inc(kept[1].sem, 1)
                        for c in range(GB):
                            dve.wait_ge(v_mm.sem, v_mm.after(i, c + 1))
                            v.tensor_tensor(vs[:, c, :], ps_s[c % 2][:, :, :].rearrange("p j n -> p (j n)"), bv_row[:, :], ALU.add).then_inc(v_ready.sem, 1)
                    elif kind == "scores_b":
                        dve.wait_ge(s_mm.sem, s_mm.after(i, k + 1))
                        v.tensor_reduce(neg[k % 2][:, :, :], ps_s[k % 2][:, :, :].rearrange("p e (j t) -> p e j t", t=T), AX.X, ALU.max).then_inc(max_ready.sem, 1)
                        dve.wait_ge(max_ready.sem, max_ready.after(i, k + 1))
                        v.tensor_scalar(neg[k % 2][:, :, :], neg[k % 2][:, :, :], -1.0, None, ALU.mult).then_inc(neg_ready.sem, 1)
                    elif kind == "turn":
                        dve.wait_ge(pv_mm.sem, pv_mm.after(i, k - 1))
                        for e in range(2):
                            dve.wait_ge(fill[e].sem, fill[e].after(i, NQK // 2 + k + 1))
                            v.tensor_copy(pt[k % 2][:, e, :, :].rearrange("p j t -> p (j t)"), ps_t[e][:, :]).then_inc(kept[e].sem, 1)
                        dve.wait_ge(p_ready.sem, p_ready.after(i, k + 1))
                        v.reciprocal(rz[k % 2][:, :, :], z[k % 2][:, :, :]).then_inc(rz_ready.sem, 1)
                    elif kind == "attend":
                        dve.wait_ge(rz_ready.sem, rz_ready.after(i, k + 1))
                        dve.wait_ge(pv_mm.sem, pv_mm.after(i, k + 1))
                        dve.wait_ge(ot_mm.sem, ot_mm.after(i, k - 1))
                        v.tensor_tensor(o[k % 2][:, :, :, :], ps_o[:, :].rearrange("p (j e d) -> p j e d", e=2, d=HD),
                                        rz[k % 2][:, :, :].rearrange("p e j -> p j e").unsqueeze(3).broadcast_to([P, HALF, 2, HD]),
                                        ALU.mult).then_inc(o_ready.sem, 1)
                    elif kind == "mix":
                        dve.wait_ge(wo_mm.sem, wo_mm.after(i - 1))
                        v.scalar_tensor_tensor(y[:, :], ps_n[:, :], bo_c[:, 0:1], group_of(xT, i - 1, 0, 1), ALU.add, ALU.add).then_inc(norm.own.y_ready.sem, 1)
                    elif kind == "norm":
                        x = group_of(xT, i - 1, 0, 1)
                        if k == 0:
                            norm.own.centre(nc, dve, i - 1, 0)
                        elif k == 1:
                            norm.gain(nc, dve, i - 1, 0, x)
                        elif k == 2:
                            norm.stream.centre(nc, dve, i - 1, 0)
                        else:
                            norm.stream.divide(nc, dve, i - 1, 0, x, xT_ready)

                run(dve, step)
        t.clear_counts()


EXPERTS, CAPACITY = 8, 100


def moe_ffn(nc, const, xT, w_gate, w_expert, b_expert, out):
    with ExitStack() as ctx:
        t = Tools(ctx, nc, "moe")
        U = 2
        ITER = NG // U
        NE = B * EXPERTS
        wg = t.sb("wg", [P, EXPERTS])
        we = t.sb("we", [P, D])
        be_row = t.sb("be_row", [P, D])
        iota_i = t.sb("iota_i", [P, B, EXPERTS], I32)
        iota = t.sb("iota", [P, B, EXPERTS])
        upto = t.sb("upto", [P, P])
        carry = t.sb("carry", [P, EXPERTS, B])
        logits = t.sb("logits", [P, B, EXPERTS])
        expert = t.sb("expert", [P, B, D])
        xtok = t.sb("xtok", [P, B, D])
        xs = [t.sb(f"xs{u}", [P, GROUP]) for u in range(U)]
        top = t.sb("top", [P, B])
        gate = t.sb("gate", [P, B])
        probs = t.sb("probs", [P, B, EXPERTS])
        best = t.sb("best", [P, B, EXPERTS])
        total = t.sb("total", [P, EXPERTS, B])
        before = t.sb("before", [P, EXPERTS, B])
        place = t.sb("place", [P, B, EXPERTS])
        yt = [t.sb(f"yt{u}", [P, GB, D]) for u in range(U)]
        stats = [t.sb(f"stats{u}", [P, GB, 6]) for u in range(U)]
        pad = t.sb("pad", [P, 1])
        mv = [t.sb(f"mv{u}", [P, GB, 2]) for u in range(U)]
        logs = [t.sb(f"logs{u}", [P, GB]) for u in range(U)]
        inv = [t.sb(f"inv{u}", [P, GB]) for u in range(U)]
        res = [t.sb(f"res{u}", [P, GB, D]) for u in range(U)]
        ps_e = [t.ps(f"bank_e{u}", [P, 512]) for u in range(U)]
        ps_g = [t.ps(f"bank_g{u}", [P, 512]) for u in range(U)]
        ps_x = [t.ps(f"bank_x{u}", [P, 512]) for u in range(U)]
        ps_c = t.ps("cum", [P, NE])
        ps_t = t.ps("tot", [P, NE])

        loaded = t.count("loaded", weight=DMA)
        made = t.count("made")
        xs_ready = t.count("xs_ready", U)
        e_mm, e_kept = t.count("e_mm", U), t.count("e_kept", U, credits=U)
        g_mm, g_kept = t.count("g_mm", U), t.count("g_kept", U, credits=U)
        x_mm, x_kept = t.count("x_mm", U, credits=U), t.count("x_kept", U, credits=U)
        with nc.Block() as block:

            @block.sync
            def _(sp):
                for dst, src in ((wg[:, :], w_gate), (we[:, :], w_expert), (be_row[:, :], b_expert.partition_broadcast(P))):
                    sp.dma_start(dst, src).then_inc(loaded.sem, DMA)

            @block.gpsimd
            def _(pool):
                pool.iota(iota_i[:, :, :], pattern=[[0, B], [1, EXPERTS]], base=0, channel_multiplier=0).then_inc(made.sem, 1)
                pool.memset(upto[:, :], 1.0).then_inc(made.sem, 1)
                pool.memset(carry[:, :, :], 1.0).then_inc(made.sem, 1)
                pool.wait_ge(made.sem, 3)
                pool.affine_select(out=upto[:, :], in_=upto[:, :], compare_op=ALU.is_ge, fill=0.0, base=0,
                                   pattern=[[1, P]], channel_multiplier=-1)
                pool.memset(carry[:, :, 0:1], 0.0)

            @block.vector
            def _(dve):
                for c in (e_kept, g_kept, x_mm, x_kept):
                    c.give(dve)
                dve.wait_ge(made.sem, 1)
                nc.vector.tensor_copy(iota[:, :, :], iota_i[:, :, :])
                dve.wait_ge(loaded.sem, 3 * DMA)

        with nc.Block() as block:

            @block.tensor
            def _(pe):
                mm, turn = nc.tensor.matmul, nc.tensor.transpose
                with pe.Fori(0, ITER) as i:
                    for u in range(U):
                        tok = lambda b: xs[u][:, b * T:(b + 1) * T]
                        pe.wait_ge(xs_ready.sem, xs_ready.after(i, u + 1))
                        pe.wait_ge(g_kept.sem, g_kept.free(i, u))
                        for b in range(GB):
                            last = mm(ps_g[u][:, b * EXPERTS:(b + 1) * EXPERTS], tok(b), wg[:, :], start=True, stop=True)
                        last.then_inc(g_mm.sem, 1)
                        pe.wait_ge(e_kept.sem, e_kept.free(i, u))
                        for b in range(GB):
                            last = mm(ps_e[u][:, b * D:(b + 1) * D], tok(b), we[:, :], start=True, stop=True)
                        last.then_inc(e_mm.sem, 1)
                        pe.wait_ge(x_kept.sem, x_kept.free(i, u))
                        for b in range(GB):
                            last = turn(ps_x[u][:, b * D:(b + 1) * D], tok(b), const["ident"][:, :])
                        last.then_inc(x_mm.sem, 1)

            @block.scalar
            def _(act):
                f = nc.scalar.activation
                with act.Fori(0, ITER) as i:
                    for u in range(U):
                        act.wait_ge(x_mm.sem, x_mm.free(i, u))
                        f(xs[u][:, :], group_of(xT, i, u, U), ACT.Copy).then_inc(xs_ready.sem, 1)
                    for u in range(U):
                        first = i * (U * GB) + u * GB
                        act.wait_ge(x_mm.sem, x_mm.after(i, u + 1))
                        f(xtok[:, bass.ds(first, GB), :], ps_x[u][:, :].rearrange("p (b d) -> p b d", d=D), ACT.Copy).then_inc(x_kept.sem, 1)

            @block.vector
            def _(dve):
                v = nc.vector
                with dve.Fori(0, ITER) as i:
                    for u in range(U):
                        first = i * (U * GB) + u * GB
                        dve.wait_ge(g_mm.sem, g_mm.after(i, u + 1))
                        v.tensor_copy(logits[:, bass.ds(first, GB), :], ps_g[u][:, 0:GB * EXPERTS].rearrange("p (b n) -> p b n", b=GB)).then_inc(g_kept.sem, 1)
                        dve.wait_ge(e_mm.sem, e_mm.after(i, u + 1))
                        v.tensor_tensor(expert[:, bass.ds(first, GB), :], ps_e[u][:, :].rearrange("p (b d) -> p b d", d=D),
                                        be_row[:, :].unsqueeze(1).broadcast_to([P, GB, D]), ALU.add).then_inc(e_kept.sem, 1)

        dist_ready = t.count("dist_ready")
        exp_ready = t.count("exp_ready")
        best_ready = t.count("best_ready")
        places_mm = t.count("places_mm")
        with nc.Block() as block:

            @block.scalar
            def _(act):
                act.wait_ge(dist_ready.sem, 1)
                nc.scalar.activation(probs[:, :, :], probs[:, :, :], ACT.Exp).then_inc(exp_ready.sem, 1)

            @block.tensor
            def _(pe):
                pe.wait_ge(best_ready.sem, 1)
                flat = best[:, :, :].rearrange("p b e -> p (b e)")
                nc.tensor.matmul(ps_c[:, :], upto[:, :], flat, start=True, stop=True)
                nc.tensor.matmul(ps_t[:, :], const["ones"][:, :], flat, start=True, stop=True).then_inc(places_mm.sem, 1)

            @block.vector
            def _(dve):
                v = nc.vector
                link = Chain(t, "route", dve)
                wide = lambda a: a[:, :].unsqueeze(2).broadcast_to([P, B, EXPERTS])
                by_seq = lambda a: a[:, :, :].rearrange("p e b -> p b e")
                link(v.tensor_reduce(top[:, :], logits[:, :, :], AX.X, ALU.max))
                v.tensor_tensor(probs[:, :, :], logits[:, :, :], wide(top), ALU.subtract).then_inc(dist_ready.sem, 1)
                dve.wait_ge(exp_ready.sem, 1)
                link(v.tensor_reduce(top[:, :], probs[:, :, :], AX.X, ALU.add))
                link(v.reciprocal(top[:, :], top[:, :]))
                link(v.tensor_tensor(probs[:, :, :], probs[:, :, :], wide(top), ALU.mult))
                link(v.tensor_reduce(gate[:, :], probs[:, :, :], AX.X, ALU.max))
                first_max_one_hot(link, v, probs[:, :, :], top[:, :], best[:, :, :], iota[:, :, :], EXPERTS)
                dve.sem_inc(best_ready.sem, 1)
                dve.wait_ge(places_mm.sem, 1)
                link(v.tensor_copy(by_seq(total), ps_t[:, :].rearrange("p (b e) -> p b e", e=EXPERTS)))
                flat = lambda a: a[:, :, :].rearrange("p e b -> p (e b)")
                link(v.tensor_tensor_scan(flat(before), flat(carry), flat(total), 0.0, ALU.mult, ALU.add))
                link(v.tensor_tensor(before[:, :, :], before[:, :, :], total[:, :, :], ALU.subtract))
                link(v.tensor_tensor(place[:, :, :], ps_c[:, :].rearrange("p (b e) -> p b e", e=EXPERTS), by_seq(before), ALU.add))
                link(v.scalar_tensor_tensor(place[:, :, :], place[:, :, :], float(CAPACITY), best[:, :, :], ALU.is_le, ALU.mult))
                link(v.tensor_reduce(top[:, :], place[:, :, :], AX.X, ALU.add))
                link(v.tensor_tensor(gate[:, :], gate[:, :], top[:, :], ALU.mult))

        y_ready = t.count("y_ready", U)
        part = t.count("part", U)
        stats_ready = t.count("stats_ready", U)
        mv_ready = t.count("mv_ready", U)
        log_ready = t.count("log_ready", U)
        inv_ready = t.count("inv_ready", U)
        res_ready = t.count("res_ready", U, credits=U)
        stored = [t.count(f"stored{u}", 1, DMA, credits=1) for u in range(U)]
        with nc.Block() as block:

            @block.sync
            def _(sp):
                with sp.Fori(0, ITER) as i:
                    for u in range(U):
                        sp.wait_ge(res_ready.sem, res_ready.after(i, u + 1))
                        dst = out[bass.ds(i * (U * GB) + u * GB, GB)].rearrange("b t d -> t b d")
                        sp.dma_start(dst, res[u][:, :, :]).then_inc(stored[u].sem, DMA)
                for u in range(U):
                    sp.wait_ge(stored[u].sem, (ITER + 1) * DMA)

            @block.scalar
            def _(act):
                f = nc.scalar.activation
                with act.Fori(0, ITER) as i:
                    for u in range(U):
                        nc.scalar.preload_act_table_set("natural_log_exp_and_others")
                        act.wait_ge(mv_ready.sem, mv_ready.after(i, u + 1))
                        f(logs[u][:, :], mv[u][:, :, 1:2].rearrange("p b a -> p (b a)"), ACT.Ln, bias=const["eps"][:, :]).then_inc(log_ready.sem, 1)
                        act.wait_ge(log_ready.sem, log_ready.after(i, u + 1))
                        f(inv[u][:, :], logs[u][:, :], ACT.Exp, scale=-0.5).then_inc(inv_ready.sem, 1)

            @block.vector
            def _(dve):
                v = nc.vector
                for u in range(U):
                    stored[u].give(dve)
                res_ready.give(dve)
                with dve.Fori(0, ITER) as i:
                    for u in range(U):
                        first = i * (U * GB) + u * GB
                        dve.wait_ge(res_ready.sem, res_ready.free(i, u))
                        v.tensor_tensor(yt[u][:, :, :], expert[:, bass.ds(first, GB), :],
                                        gate[:, bass.ds(first, GB)].unsqueeze(2).broadcast_to([P, GB, D]), ALU.mult).then_inc(part.sem, 1)
                        dve.wait_ge(part.sem, part.after(i, u + 1))
                        v.tensor_tensor(yt[u][:, :, :], yt[u][:, :, :], xtok[:, bass.ds(first, GB), :], ALU.add).then_inc(y_ready.sem, 1)
                        dve.wait_ge(y_ready.sem, y_ready.after(i, u + 1))
                        for b in range(GB):
                            last = v.bn_stats(stats[u][:, b, :], yt[u][:, b, :])
                        last.then_inc(stats_ready.sem, 1)
                        dve.wait_ge(stats_ready.sem, stats_ready.after(i, u + 1))
                        v.memset(pad[:, :], 0.0)
                        for b in range(GB):
                            last = v.bn_aggr(mv[u][:, b, :], stats[u][:, b, :])
                        last.then_inc(mv_ready.sem, 1)
                    for u in range(U):
                        dve.wait_ge(inv_ready.sem, inv_ready.after(i, u + 1))
                        dve.wait_ge(stored[u].sem, stored[u].free(i))
                        for b in range(GB):
                            last = v.tensor_scalar(res[u][:, b, :], yt[u][:, b, :], mv[u][:, b, 0:1], inv[u][:, b:b + 1], ALU.subtract, ALU.mult)
                        last.then_inc(res_ready.sem, 1)
        t.clear_counts()


def program(nc, a, out):
    def of(prefix, *names):
        return [a[f"{prefix}_{n}"] for n in names]

    with ExitStack() as ctx:
        xT = ctx.enter_context(nc.sbuf_tensor("xT", [P, NT], F32))
        const = constants(nc, ctx)
        min_gru(nc, const, xT, a["x"], *of("L0_attn", "Wp", "bp", "g1", "Whg", "bhg", "Wo", "bo", "g2", "gf", "Wf", "bf"))
        cross_attention(nc, const, "x0", xT, a["ctx_1024"], *of("L0_xattn", "Wq", "bq", "Wk", "bk", "Wv", "bv", "Wo", "bo"), turn=True,
                        temper=of("L0_xattn", "w1", "b1", "w2", "b2", "w3", "b3"))
        tile_ffn(nc, const, xT, *of("L0_ffn", "signatures_raw", "knot_values", "temperature", "compress_w1", "compress_b1",
                                    "compress_w2", "compress_b2", "spline_w1", "spline_b1", "spline_w2", "spline_b2",
                                    "directions", "norm_gamma", "norm_beta", "output_scale"))
        self_attention(nc, const, xT, *of("L1_attn", "adaptive_scale", "Wq", "bq", "Wk", "bk", "Wv", "bv", "Wo", "bo", "gamma", "beta"))
        cross_attention(nc, const, "x1", xT, a["ctx_1024"], *of("L1_xattn", "W_Q", "b_Q", "W_K", "b_K", "W_V", "b_V", "W_O", "b_O"), turn=False)
        moe_ffn(nc, const, xT, *of("L1_ffn", "w_gate", "w_expert", "b_expert"), out)


def kernel(**inputs):
    import concourse.bacc as _bacc
    from concourse.bass_utils import run_bass_kernel_spmd as _run

    nc = _bacc.Bacc("TRN2", target_bir_lowering=False, num_devices=1)
    arrays, aps = {}, {}
    for name, value in inputs.items():
        value = np.ascontiguousarray(value)
        arrays[f"in_{name}"] = value
        aps[name] = nc.dram_tensor(f"in_{name}", value.shape, mybir.dt.from_np(value.dtype), kind="ExternalInput").ap()
    out = nc.dram_tensor("out", (B, T, D), F32, kind="ExternalOutput").ap()
    program(nc, aps, out)
    r = _run(nc, [arrays], core_ids=[0])
    return r.results[0]["out"]
```

```python
from contextlib import ExitStack

import numpy as np

import concourse.bass as bass
from concourse import mybir

F32 = mybir.dt.float32
I32 = mybir.dt.int32
U32 = mybir.dt.uint32
ALU = mybir.AluOpType
ACT = mybir.ActivationFunctionType
AX = mybir.AxisListType

P = 128
B = 32
T = 128
D = 128
NT = B * T
GB = 4
GROUP = GB * T
NG = NT // GROUP
S = 77
H = 16
DK = D // H
EPS = 1e-5
DMA = 16


class Count:

    def __init__(self, ctx, nc, name, per=1, weight=1, credits=0):
        self.sem = ctx.enter_context(nc.semaphore(name))
        self.per, self.weight, self.credits = per, weight, credits

    def after(self, i, k=1):
        return i * (self.per * self.weight) + (k + self.credits) * self.weight

    def free(self, i, n=0):
        return i * (self.per * self.weight) + (n + 1) * self.weight

    def give(self, engine):
        engine.sem_inc(self.sem, self.credits * self.weight)


class Tools:

    def __init__(self, ctx, nc, tag):
        self.ctx, self.nc, self.tag, self.numbers = ctx, nc, tag, []

    def sb(self, name, shape, dt=F32):
        return self.ctx.enter_context(self.nc.sbuf_tensor(f"{self.tag}_{name}", shape, dt))

    def ps(self, name, shape, dt=F32):
        return self.ctx.enter_context(self.nc.psum_tensor(f"{self.tag}_{name}", shape, dt))

    def count(self, name, per=1, weight=1, credits=0):
        c = Count(self.ctx, self.nc, f"{self.tag}_{name}", per, weight, credits)
        self.numbers.append(c.sem.num)
        return c

    def clear_counts(self):
        numbers = sorted(self.numbers)
        with self.nc.Block() as block:

            @block.sync
            def _(sp):
                first = last = numbers[0]
                for n in numbers[1:] + [None]:
                    if n != last + 1:
                        sp.sem_clear(range(first, last + 1))
                        first = n
                    last = n


def constants(nc, ctx):
    t = Tools(ctx, nc, "const")
    c = {
        "ident": t.sb("ident", [P, P]),
        "ones": t.sb("ones", [P, P]),
        "mean": t.sb("mean", [P, P]),
        "eps": t.sb("eps", [P, 1]),
        "tiny": t.sb("tiny", [P, 1]),
        "rms_bias": t.sb("rms_bias", [P, 1]),
    }
    cleared = t.count("cleared")
    with nc.Block() as block:

        @block.gpsimd
        def _(pool):
            pool.memset(c["ident"][:, :], 0.0).then_inc(cleared.sem, 1)
            pool.memset(c["ones"][:, :], 1.0)
            pool.memset(c["mean"][:, :], 1.0 / D)
            pool.memset(c["eps"][:, :], EPS)
            pool.memset(c["tiny"][:, :], RMS_TINY)
            pool.memset(c["rms_bias"][:, :], 0.5 * RMS_SHIFT * float(np.log(2.0)))
            pool.wait_ge(cleared.sem, 1)
            pool.affine_select(out=c["ident"][:, :], in_=c["ident"][:, :], compare_op=ALU.not_equal,
                               fill=1.0, base=0, pattern=[[-1, P]], channel_multiplier=1)
    return c


RMS_SHIFT = 24
RMS_TINY = 2.0 ** -64
RMS_SCALE = 2.0 ** RMS_SHIFT
INV_NORM_MAX = 1e12


HID = 256
DI = 384
NL = 4
KH = HID // P
KI = DI // P
SIGMOIDS = "sigmoid_and_others"
TP = T + 1


def min_gru(nc, const, xT, x, Wp, bp, g1, Whg, bhg, Wo, bo, g2, gf, Wf, bf):
    with ExitStack() as ctx:
        t = Tools(ctx, nc, "gru")
        U = 2
        QN = 2 * NL
        wp = t.sb("wp", [P, HID])
        whg = t.sb("whg", [P, NL, KH, 2 * DI])
        wo = t.sb("wo", [P, NL, KI, HID])
        wf = t.sb("wf", [P, KH, D])
        bp_c = t.sb("bp_c", [P, KH])
        bhg_c = t.sb("bhg_c", [P, NL, 2 * KI])
        half_c = t.sb("half_c", [P, NL, 2 * KI])
        nbg_c = t.sb("nbg_c", [P, NL, 2 * KI])
        bo_c = t.sb("bo_c", [P, NL, KH])
        g1_c = t.sb("g1_c", [P, NL, KH])
        g2_c = t.sb("g2_c", [P, NL, KH])
        gf_c = t.sb("gf_c", [P, KH])
        bf_c = t.sb("bf_c", [P, 1])
        xin = [t.sb(f"xin{u}", [P, GB, D]) for u in range(U)]
        xg = [t.sb(f"xg{u}", [P, 2, GROUP]) for u in range(U)]
        h = [t.sb(f"h{u}", [P, 2, KH, GROUP]) for u in range(U)]
        sq = [t.sb(f"sq{u}", [P, KH, GROUP]) for u in range(U)]
        xn = [t.sb(f"xn{u}", [P, KH, GROUP]) for u in range(U)]
        xf = t.sb("xf", [P, KH, GROUP])
        total = [t.sb(f"total{u}", [P, GROUP]) for u in range(U)]
        lnr = [t.sb(f"lnr{u}", [P, GROUP]) for u in range(U)]
        inv = [t.sb(f"inv{u}", [P, GROUP]) for u in range(U)]
        y = [t.sb(f"y{u}", [P, KI, GB * TP]) for u in range(U)]
        decay = [t.sb(f"decay{r}", [P, GB * TP]) for r in range(2)]
        value = [t.sb(f"value{r}", [P, GB * TP]) for r in range(2)]
        zgate = [t.sb(f"zgate{r}", [P, GROUP]) for r in range(2)]
        sighid = [t.sb(f"sighid{r}", [P, GROUP]) for r in range(2)]
        ghid = [t.sb(f"ghid{r}", [P, GROUP]) for r in range(2)]
        gain = [t.sb(f"gain{m}", [P, GROUP]) for m in range(KH)]
        ps_stat = [t.ps(f"stat{u}", [P, GROUP]) for u in range(U)]
        ps_hid = [t.ps(f"hid{r}", [P, GROUP]) for r in range(2)]
        ps_gate = [t.ps(f"gate{r}", [P, GROUP]) for r in range(2)]
        ps_out = [t.ps(f"out{m}", [P, GROUP]) for m in range(KH)]

        first_loaded = t.count("first_loaded", weight=DMA)
        loaded = [t.count(f"loaded{n}", weight=DMA) for n in range(NL + 1)]
        gains_ready = t.count("gains_ready")
        negated = t.count("negated")
        scaled = [t.count(f"scaled{n}") for n in range(NL + 1)]
        pads_ready = t.count("pads_ready")

        def lanes(name, per=1, weight=1, credits=0):
            return [t.count(f"{name}{u}", per, weight, credits) for u in range(U)]

        x_loaded = lanes("x_loaded", 1, DMA)
        x_turned = lanes("x_turned")
        xg_ready = lanes("xg_ready")
        first_mm = lanes("first_mm", KH)
        first_ready = lanes("first_ready", KH)
        sq_ready = lanes("sq_ready", KH * QN)
        sq_summed = lanes("sq_summed", QN)
        stat_ready = lanes("stat_ready", QN)
        ln_ready = lanes("ln_ready", QN)
        inv_ready = lanes("inv_ready", QN)
        xn_ready = lanes("xn_ready", KH * NL)
        h_ready = lanes("h_ready", KH * QN)
        gain_ready = lanes("gain_ready", KH * NL)
        end_sq = lanes("end_sq", 2)
        end_summed = lanes("end_summed")
        end_stat = lanes("end_stat", 2)
        end_ln = lanes("end_ln", 2)
        end_inv = lanes("end_inv", 2)
        xf_ready = lanes("xf_ready", KH)
        wf_mm = lanes("wf_mm", credits=1)
        total_ready = lanes("total_ready")
        mean_mm = lanes("mean_mm")
        centred = lanes("centred")
        xT_ready = lanes("xT_ready")
        NCH = U * NL * KI
        hg_ready = t.count("hg_ready", NCH)
        gates_ready = t.count("gates_ready", NCH)
        ghid_ready = t.count("ghid_ready", NCH, credits=2)
        value_ready = t.count("value_ready", NCH)
        scan_ready = t.count("scan_ready", NCH, credits=2)
        NOUT = U * KH * NL
        out_ready = t.count("out_ready", NOUT)
        out_free = t.count("out_free", NOUT, credits=2)

        ITER = NG // U
        ORDER = []
        waiting = [("pre_stat", 0, 0, 0, 0)]
        for l in range(NL):
            for u in range(U):
                if u == 0:
                    lag, below = (0, l - 1) if l else (1, NL - 1)
                    nxt, above = 0, l
                else:
                    lag, below = 0, l
                    nxt, above = (0, l + 1) if l < NL - 1 else (-1, 0)
                other = 1 - u
                extras = {0: (["end_square1"], ["end_stat1"], ["end_scale", "wf"], ["end_mean"]),
                          1: (["end_square2"], ["end_stat2"], [], []),
                          2: ([], ["load1"], ["load2"], ["load3"]),
                          3: ([], [], [], [])}[l]
                of = -1 if l == 2 else 1
                own = [[(kind, of, u, 0, 0) for kind in part] for part in extras]
                mix = [[("mix", lag, other, below, k)] for k in range(KI)]
                ORDER += mix[0] + waiting + mix[1] + mix[2] + [("post_square", lag, other, below, 0)]
                ORDER += own[0] + [("rec", 0, u, l, 0), ("post", lag, other, below, 0)] + own[1]
                ORDER += [("sigmoids", 0, u, l, 0), ("gain", lag, other, below, 0), ("rec", 0, u, l, 1)] + own[2]
                ORDER += [("pre_square", nxt, other, above, 0), ("rec", 0, u, l, 2), ("pre", nxt, other, above, 0), ("sigmoids", 0, u, l, 0)] + own[3]
                waiting = [("pre_stat", nxt, other, above, 0)]

        def run(engine, step):
            def peeled(i):
                for kind, lag, u, l, c in ORDER:
                    if 0 <= i - lag < ITER:
                        step(kind, i - lag, u, l, c)
            for i in (-1, 0):
                peeled(i)
            with engine.Fori(1, ITER - 1) as i:
                for kind, lag, u, l, c in ORDER:
                    step(kind, i - lag, u, l, c)
            for i in (ITER - 1, ITER):
                peeled(i)

        def at(i, where):
            return isinstance(i, int) and i == where

        def chunk_no(u, l, c):
            return (l * U + u) * KI + c

        def out_no(u, l, m):
            return (l * U + u) * KH + m

        def seqs(a):
            return a.rearrange("p (b t) -> p b t", t=T)

        def padded(a):
            return a.rearrange("p (b t) -> p b t", t=TP)[:, :, 1:]

        def hidden(u, i):
            return h[u][:, bass.ds(i & 1, 1), :, :].rearrange("p a k t -> p (a k) t")

        def hidden_chunk(u, i, m):
            return h[u][:, bass.ds(i & 1, 1), m, :].rearrange("p a t -> p (a t)")

        def group_in(u, i):
            return xg[u][:, bass.ds(i & 1, 1), :].rearrange("p a t -> p (a t)")

        with nc.Block() as block:

            @block.sync
            def _(sp):
                cols = lambda v, n: v.rearrange("(n p) -> p n", p=P)
                for u in range(U):
                    sp.dma_start(xin[u][:, :, :], x[u * GB:(u + 1) * GB].rearrange("b t d -> t b d")).then_inc(x_loaded[u].sem, DMA)
                    if u == 0:
                        sp.dma_start(wp[:, :], Wp).then_inc(first_loaded.sem, DMA)
                        sp.dma_start(bp_c[:, :], cols(bp, KH), allow_slow_non_contiguous=True).then_inc(first_loaded.sem, DMA)
                for dst, src in (
                    (g1_c[:, :, :], g1.rearrange("l (k p) -> p l k", p=P)),
                    (g2_c[:, :, :], g2.rearrange("l (k p) -> p l k", p=P)),
                    (gf_c[:, :], cols(gf, KH)), (bf_c[:, :], cols(bf, 1)),
                    (bhg_c[:, :, :], bhg.rearrange("l (k p) -> p l k", p=P)),
                    (bo_c[:, :, :], bo.rearrange("l (k p) -> p l k", p=P)),
                    (wf[:, :, :], Wf.rearrange("(k p) n -> p k n", p=P)),
                ):
                    sp.dma_start(dst, src, allow_slow_non_contiguous=True).then_inc(loaded[NL].sem, DMA)
                with sp.Fori(0, ITER - 1) as i:
                    for u in range(U):
                        sp.wait_ge(x_turned[u].sem, x_turned[u].after(i))
                        src = x[bass.ds((i + 1) * (U * GB) + u * GB, GB)].rearrange("b t d -> t b d")
                        sp.dma_start(xin[u][:, :, :], src).then_inc(x_loaded[u].sem, DMA)

            @block.tensor
            def _(pe):
                mm = nc.tensor.matmul

                def squares(u, done):
                    mm(ps_stat[u][:, :], const["ones"][:, :], sq[u][:, 0, :], start=True, stop=True).then_inc(done.sem, 1)

                def step(kind, i, u, l, c):
                    if kind == "load1":
                        pe.wait_ge(x_loaded[u].sem, x_loaded[u].after(i))
                        if not at(i, 0):
                            pe.wait_ge(ln_ready[u].sem, ln_ready[u].after(i - 1, 5))
                        for b in range(GB):
                            last = nc.tensor.transpose(ps_stat[u][:, b * T:(b + 1) * T], xin[u][:, b, :], const["ident"][:, :])
                        last.then_inc(x_turned[u].sem, 1)
                    elif kind in ("load2", "load3"):
                        m = int(kind[4]) - 2
                        if m == 0:
                            pe.wait_ge(xg_ready[u].sem, xg_ready[u].after(i))
                            pe.wait_ge(first_loaded.sem, 2 * DMA)
                        else:
                            pe.wait_ge(first_ready[u].sem, first_ready[u].after(i))
                        mm(ps_stat[u][:, :], wp[:, m * P:(m + 1) * P], group_in(u, i), start=True, stop=True).then_inc(first_mm[u].sem, 1)
                    elif kind in ("pre_stat", "post"):
                        q = 2 * l + (kind == "post")
                        pe.wait_ge(sq_summed[u].sem, sq_summed[u].after(i, q + 1))
                        if q:
                            pe.wait_ge(ln_ready[u].sem, ln_ready[u].after(i, q))
                        elif not at(i, 0):
                            pe.wait_ge(ln_ready[u].sem, ln_ready[u].after(i - 1, QN))
                        if q == 1 and not at(i, 0):
                            pe.wait_ge(centred[u].sem, centred[u].after(i - 1))
                        if q == 3 and not at(i, 0):
                            pe.wait_ge(end_ln[u].sem, end_ln[u].after(i - 1, 2))
                        if q == 5 and not at(i, ITER - 1):
                            pe.wait_ge(first_ready[u].sem, first_ready[u].after(i + 1, KH))
                        squares(u, stat_ready[u])
                    elif kind == "rec":
                        n = chunk_no(u, l, c)
                        if c == 0:
                            if at(i, 0):
                                pe.wait_ge(scaled[l].sem, KH)
                                if l == NL - 1:
                                    pe.wait_ge(scaled[NL].sem, KH)
                        pe.wait_ge(ghid_ready.sem, ghid_ready.free(i, n))
                        for bank, off in ((ps_gate[n % 2], DI + c * P), (ps_hid[n % 2], c * P)):
                            for k in range(KH):
                                if c == 0 and bank is ps_gate[n % 2]:
                                    pe.wait_ge(xn_ready[u].sem, xn_ready[u].after(i, KH * l + k + 1))
                                last = mm(bank[:, :], whg[:, l, k, off:off + P], xn[u][:, k, :], start=(k == 0), stop=(k == KH - 1))
                        last.then_inc(hg_ready.sem, 1)
                    elif kind == "mix":
                        pe.wait_ge(scan_ready.sem, scan_ready.after(i, chunk_no(u, l, c) + 1))
                        for m in range(KH):
                            if c == 0:
                                pe.wait_ge(out_free.sem, out_free.free(i, out_no(u, l, m)))
                            last = mm(ps_out[m][:, :], wo[:, l, c, m * P:(m + 1) * P], padded(y[u][:, c, :]), start=(c == 0), stop=(c == KI - 1))
                            if c == KI - 1:
                                last.then_inc(out_ready.sem, 1)
                    elif kind == "end_stat1":
                        pe.wait_ge(end_summed[u].sem, end_summed[u].after(i))
                        if not at(i, ITER - 1):
                            pe.wait_ge(ln_ready[u].sem, ln_ready[u].after(i + 1, 1))
                        squares(u, end_stat[u])
                    elif kind == "wf":
                        pe.wait_ge(xf_ready[u].sem, xf_ready[u].after(i, KH))
                        for k in range(KH):
                            last = mm(ps_stat[u][:, :], wf[:, k, :], xf[:, k, :], start=(k == 0), stop=(k == KH - 1))
                        last.then_inc(wf_mm[u].sem, 1)
                    elif kind == "end_mean":
                        pe.wait_ge(total_ready[u].sem, total_ready[u].after(i))
                        mm(ps_stat[u][:, :], const["mean"][:, :], total[u][:, :], start=True, stop=True).then_inc(mean_mm[u].sem, 1)
                    elif kind == "end_stat2":
                        pe.wait_ge(end_sq[u].sem, end_sq[u].after(i, 2))
                        if not at(i, ITER - 1):
                            pe.wait_ge(ln_ready[u].sem, ln_ready[u].after(i + 1, 3))
                        mm(ps_stat[u][:, :], const["mean"][:, :], sq[u][:, 0, :], start=True, stop=True).then_inc(end_stat[u].sem, 1)

                run(pe, step)

            @block.scalar
            def _(act):
                f = nc.scalar.activation
                for l in range(NL):
                    act.dma_start(whg[:, l, :, :], Whg[l].rearrange("(k p) n -> p k n", p=P)).then_inc(loaded[l].sem, DMA)
                    act.dma_start(wo[:, l, :, :], Wo[l].rearrange("(k p) n -> p k n", p=P)).then_inc(loaded[l].sem, DMA)
                act.wait_ge(loaded[NL].sem, loaded[NL].after(0, 7))
                nc.scalar.mul(nbg_c[:, :, :], bhg_c[:, :, :], -1.0).then_inc(negated.sem, 1)
                act.wait_ge(negated.sem, 1)
                act.wait_ge(pads_ready.sem, 4)

                def inverse(u, i, k, stat, ln, done, bias, scale, shift):
                    act.wait_ge(stat[u].sem, stat[u].after(i, k))
                    f(lnr[u][:, :], ps_stat[u][:, :], ACT.Ln, bias=bias, scale=scale).then_inc(ln[u].sem, 1)
                    act.wait_ge(ln[u].sem, ln[u].after(i, k))
                    f(inv[u][:, :], lnr[u][:, :], ACT.Exp, bias=shift, scale=-0.5).then_inc(done[u].sem, 1)

                rms = (const["tiny"][:, :], RMS_SCALE, const["rms_bias"][:, :])

                def step(kind, i, u, l, c):
                    if kind == "load1":
                        act.wait_ge(x_turned[u].sem, x_turned[u].after(i))
                        act.nop(nofuse=True)
                        f(group_in(u, i), ps_stat[u][:, :], ACT.Copy).then_inc(xg_ready[u].sem, 1)
                    elif kind in ("pre_square", "post_square"):
                        q = 2 * l + (kind == "post_square")
                        for m in range(KH):
                            if q:
                                act.wait_ge(h_ready[u].sem, h_ready[u].after(i, KH * (q - 1) + m + 1))
                            else:
                                act.wait_ge(first_ready[u].sem, first_ready[u].after(i, m + 1))
                            act.nop(nofuse=True)
                            f(sq[u][:, m, :], hidden_chunk(u, i, m), ACT.Square).then_inc(sq_ready[u].sem, 1)
                    elif kind in ("pre", "post"):
                        nc.scalar.preload_act_table_set(LN_EXP)
                        if kind == "post":
                            act.wait_ge(xn_ready[u].sem, xn_ready[u].after(i, KH * (l + 1)))
                            if l < 2 and not at(i, 0):
                                last = (xf_ready, xT_ready)[l][u]
                                act.wait_ge(last.sem, last.after(i - 1, last.per))
                        elif l:
                            act.wait_ge(gain_ready[u].sem, gain_ready[u].after(i, l * KH))
                        elif not at(i, 0):
                            act.wait_ge(gain_ready[u].sem, gain_ready[u].after(i - 1, NL * KH))
                        inverse(u, i, 2 * l + (kind == "post") + 1, stat_ready, ln_ready, inv_ready, *rms)
                    elif kind == "rec":
                        n = chunk_no(u, l, c)
                        r = n % 2
                        act.wait_ge(hg_ready.sem, hg_ready.after(i, n + 1))
                        act.wait_ge(scan_ready.sem, scan_ready.free(i, n))
                        f(sighid[r][:, :], ps_hid[r][:, :], ACT.Sigmoid, bias=bhg_c[:, l, c:c + 1])
                        f(zgate[r][:, :], ps_gate[r][:, :], ACT.Sigmoid, bias=bhg_c[:, l, KI + c:KI + c + 1])
                        f(padded(decay[r][:, :]), seqs(ps_gate[r][:, :]), ACT.Sigmoid, bias=nbg_c[:, l, KI + c:KI + c + 1],
                          scale=-1.0).then_inc(gates_ready.sem, 1)
                    elif kind == "sigmoids":
                        nc.scalar.preload_act_table_set(SIGMOIDS)
                    elif kind == "end_square1":
                        act.wait_ge(h_ready[u].sem, h_ready[u].after(i, KH * QN))
                        act.nop(nofuse=True)
                        f(sq[u][:, :, :], hidden(u, i), ACT.Square).then_inc(end_sq[u].sem, 1)
                    elif kind == "end_stat1":
                        if not at(i, ITER - 1):
                            act.wait_ge(xn_ready[u].sem, xn_ready[u].after(i + 1, KH))
                        inverse(u, i, 1, end_stat, end_ln, end_inv, *rms)
                    elif kind == "end_square2":
                        act.wait_ge(centred[u].sem, centred[u].after(i))
                        f(sq[u][:, 0, :], total[u][:, :], ACT.Square).then_inc(end_sq[u].sem, 1)
                    elif kind == "end_stat2":
                        act.wait_ge(xf_ready[u].sem, xf_ready[u].after(i, KH))
                        if not at(i, ITER - 1):
                            act.wait_ge(xn_ready[u].sem, xn_ready[u].after(i + 1, 2 * KH))
                        inverse(u, i, 2, end_stat, end_ln, end_inv, const["eps"][:, :], 1.0, 0.0)

                run(act, step)

            @block.vector
            def _(dve):
                v = nc.vector
                out_free.give(dve)
                ghid_ready.give(dve)
                scan_ready.give(dve)
                for c in wf_mm:
                    c.give(dve)
                for r in range(2):
                    v.memset(decay[r][:, :].rearrange("p (b t) -> p b t", t=TP)[:, :, 0:1], 0.0).then_inc(pads_ready.sem, 1)
                    v.memset(value[r][:, :].rearrange("p (b t) -> p b t", t=TP)[:, :, 0:1], 1.0).then_inc(pads_ready.sem, 1)
                dve.wait_ge(loaded[NL].sem, loaded[NL].after(0, 7))
                root = float(HID) ** 0.5
                for g in (g1_c[:, :, :], g2_c[:, :, :], gf_c[:, :]):
                    v.tensor_scalar(g, g, 1.0, root, ALU.add, ALU.mult).then_inc(gains_ready.sem, 1)
                dve.wait_ge(gains_ready.sem, 3)
                v.tensor_scalar(half_c[:, :, :], bhg_c[:, :, :], 0.5, None, ALU.add).then_inc(gains_ready.sem, 1)
                dve.wait_ge(gains_ready.sem, 4)

                for k in range(KH):
                    v.tensor_scalar(wf[:, k, :], wf[:, k, :], gf_c[:, k:k + 1], None, ALU.mult).then_inc(scaled[NL].sem, 1)

                def scale_weights(l):
                    dve.wait_ge(loaded[l].sem, loaded[l].after(0, 2))
                    for k in range(KH):
                        v.tensor_scalar(whg[:, l, k, :], whg[:, l, k, :], g1_c[:, l, k:k + 1], None, ALU.mult).then_inc(scaled[l].sem, 1)

                def normed(u, i, out, ready):
                    for m in range(KH):
                        v.scalar_tensor_tensor(out[:, m, :], inv[u][:, :], INV_NORM_MAX, hidden_chunk(u, i, m), ALU.min, ALU.mult).then_inc(ready[u].sem, 1)

                def add_squares(u, done):
                    v.tensor_tensor(sq[u][:, 0, :], sq[u][:, 0, :], sq[u][:, 1, :], ALU.add).then_inc(done[u].sem, 1)

                def step(kind, i, u, l, c):
                    if kind in ("pre_square", "post_square"):
                        q = 2 * l + (kind == "post_square")
                        dve.wait_ge(sq_ready[u].sem, sq_ready[u].after(i, KH * (q + 1)))
                        add_squares(u, sq_summed)
                    elif kind == "end_square1":
                        dve.wait_ge(end_sq[u].sem, end_sq[u].after(i, 1))
                        add_squares(u, end_summed)
                    elif kind in ("load2", "load3"):
                        m = int(kind[4]) - 2
                        dve.wait_ge(first_mm[u].sem, first_mm[u].after(i, m + 1))
                        if at(i, 0):
                            dve.wait_ge(first_loaded.sem, 2 * DMA)
                        v.tensor_scalar(hidden_chunk(u, i, m), ps_stat[u][:, :], bp_c[:, m:m + 1], None, ALU.add).then_inc(first_ready[u].sem, 1)
                    elif kind == "pre":
                        if at(i, 0) and u == 0:
                            scale_weights(l)
                        dve.wait_ge(inv_ready[u].sem, inv_ready[u].after(i, 2 * l + 1))
                        normed(u, i, xn[u], xn_ready)
                    elif kind == "rec":
                        n = chunk_no(u, l, c)
                        r = n % 2
                        dve.wait_ge(gates_ready.sem, gates_ready.after(i, n + 1))
                        v.scalar_tensor_tensor(ghid[r][:, :], ps_hid[r][:, :], half_c[:, l, c:c + 1], sighid[r][:, :], ALU.add, ALU.max).then_inc(ghid_ready.sem, 1)
                        dve.wait_ge(ghid_ready.sem, ghid_ready.after(i, n + 1))
                        v.tensor_tensor(padded(value[r][:, :]), seqs(ghid[r][:, :]), seqs(zgate[r][:, :]), ALU.mult).then_inc(value_ready.sem, 1)
                        dve.wait_ge(value_ready.sem, value_ready.after(i, n + 1))
                        v.tensor_tensor_scan(y[u][:, c, :], decay[r][:, :], value[r][:, :], 0.0, ALU.mult, ALU.add).then_inc(scan_ready.sem, 1)
                    elif kind == "mix" and c == KI - 1:
                        for m in range(KH):
                            dve.wait_ge(out_ready.sem, out_ready.after(i, out_no(u, l, m) + 1))
                            hm = hidden_chunk(u, i, m)
                            v.scalar_tensor_tensor(hm, ps_out[m][:, :], bo_c[:, l, m:m + 1], hm, ALU.add, ALU.add).then_inc(h_ready[u].sem, 1)
                        dve.wait_ge(h_ready[u].sem, h_ready[u].after(i, KH * (2 * l + 1)))
                        dve.sem_inc(out_free.sem, KH)
                    elif kind == "gain":
                        q = 2 * l + 1
                        dve.wait_ge(inv_ready[u].sem, inv_ready[u].after(i, q + 1))
                        for m in range(KH):
                            v.tensor_scalar(gain[m][:, :], inv[u][:, :], INV_NORM_MAX, g2_c[:, l, m:m + 1], ALU.min, ALU.mult).then_inc(gain_ready[u].sem, 1)
                        for m in range(KH):
                            dve.wait_ge(gain_ready[u].sem, gain_ready[u].after(i, l * KH + m + 1))
                            hm = hidden_chunk(u, i, m)
                            v.scalar_tensor_tensor(hm, gain[m][:, :], 1.0, hm, ALU.add, ALU.mult).then_inc(h_ready[u].sem, 1)
                    elif kind == "end_scale":
                        dve.wait_ge(end_inv[u].sem, end_inv[u].after(i, 1))
                        dve.wait_ge(wf_mm[1 - u].sem, wf_mm[1 - u].after(i if u else i - 1))
                        normed(u, i, xf, xf_ready)
                    elif kind == "wf":
                        dve.wait_ge(wf_mm[u].sem, wf_mm[u].after(i))
                        v.scalar_tensor_tensor(total[u][:, :], ps_stat[u][:, :], bf_c[:, 0:1], group_in(u, i), ALU.add, ALU.add).then_inc(total_ready[u].sem, 1)
                    elif kind == "end_mean":
                        dve.wait_ge(mean_mm[u].sem, mean_mm[u].after(i))
                        v.tensor_tensor(total[u][:, :], total[u][:, :], ps_stat[u][:, :], ALU.subtract).then_inc(centred[u].sem, 1)
                    elif kind == "end_stat2":
                        dve.wait_ge(end_inv[u].sem, end_inv[u].after(i, 2))
                        v.tensor_tensor(group_of(xT, i, u, U), total[u][:, :], inv[u][:, :], ALU.mult).then_inc(xT_ready[u].sem, 1)

                run(dve, step)
        t.clear_counts()


LN_EXP = "natural_log_exp_and_others"

class Norm:

    def __init__(self, t, const, name, per, y, sq, logs, inv, bank, y_credits=0):
        self.const, self.y, self.sq, self.logs, self.inv, self.bank = const, y, sq, logs, inv, bank
        self.y_ready = t.count(f"{name}_y_ready", per, credits=y_credits)
        self.mean_ready = t.count(f"{name}_mean_ready", per)
        self.centred = t.count(f"{name}_centred", per)
        self.sq_ready = t.count(f"{name}_sq_ready", per)
        self.var_ready = t.count(f"{name}_var_ready", per)
        self.log_ready = t.count(f"{name}_log_ready", per, credits=1)
        self.inv_ready = t.count(f"{name}_inv_ready", per)

    def mean(self, nc, pe, i, n):
        pe.wait_ge(self.y_ready.sem, self.y_ready.after(i, n + 1))
        nc.tensor.matmul(self.bank[:, :], self.const["mean"][:, :], self.y[:, :], start=True, stop=True).then_inc(self.mean_ready.sem, 1)

    def variance(self, nc, pe, i, n):
        pe.wait_ge(self.sq_ready.sem, self.sq_ready.after(i, n + 1))
        nc.tensor.matmul(self.bank[:, :], self.const["mean"][:, :], self.sq[:, :], start=True, stop=True).then_inc(self.var_ready.sem, 1)

    def tensor(self, nc, pe, i, n):
        self.mean(nc, pe, i, n)
        self.variance(nc, pe, i, n)

    def square(self, nc, act, i, n):
        act.wait_ge(self.centred.sem, self.centred.after(i, n + 1))
        nc.scalar.activation(self.sq[:, :], self.y[:, :], ACT.Square).then_inc(self.sq_ready.sem, 1)

    def inverse(self, nc, act, i, n):
        act.wait_ge(self.var_ready.sem, self.var_ready.after(i, n + 1))
        nc.scalar.activation(self.logs[:, :], self.bank[:, :], ACT.Ln, bias=self.const["eps"][:, :]).then_inc(self.log_ready.sem, 1)
        act.wait_ge(self.log_ready.sem, self.log_ready.after(i, n + 1))
        nc.scalar.activation(self.inv[:, :], self.logs[:, :], ACT.Exp, scale=-0.5).then_inc(self.inv_ready.sem, 1)

    def scalar(self, nc, act, i, n):
        self.square(nc, act, i, n)
        self.inverse(nc, act, i, n)

    def centre(self, nc, dve, i, n):
        dve.wait_ge(self.mean_ready.sem, self.mean_ready.after(i, n + 1))
        nc.vector.tensor_tensor(self.y[:, :], self.y[:, :], self.bank[:, :], ALU.subtract).then_inc(self.centred.sem, 1)

    def divide(self, nc, dve, i, n, out, done):
        dve.wait_ge(self.inv_ready.sem, self.inv_ready.after(i, n + 1))
        nc.vector.tensor_tensor(out, self.y[:, :], self.inv[:, :], ALU.mult).then_inc(done.sem, 1)


def group_of(xT, i, u, U):
    return xT[:, bass.ds(i * (U * GROUP) + u * GROUP, GROUP)]


def load_transposed(nc, const, tag, pairs, bank):
    with ExitStack() as ctx:
        t = Tools(ctx, nc, tag)
        loads, fills, first = [], [], 0
        for dst, src in pairs:
            n = max(1, dst.shape[1] // P)
            rows, cols = (P, P) if n > 1 else src.shape
            loads.append((first, n, src))
            for k in range(0, n, 4):
                fills.append((dst, k, range(first + k, first + min(n, k + 4)), rows, cols, len(loads)))
            first += n
        raw = t.sb("raw", [P, first, P])
        loaded = [t.count(f"loaded{q}", weight=DMA) for q in range(len(loads))]
        turned = t.count("turned")
        kept = [t.count(f"kept{r}") for r in range(2)]
        with nc.Block() as block:

            def load(engine, which):
                for q in range(which, len(loads), 2):
                    at, n, src = loads[q]
                    if n == 1:
                        engine.dma_start(raw[0:src.shape[0], at, 0:src.shape[1]], src).then_inc(loaded[q].sem, DMA)
                    else:
                        tall = src.rearrange("(k p) d -> p k d", p=P) if src.shape[0] == n * P else src.rearrange("p (k d) -> p k d", d=P)
                        engine.dma_start(raw[:, at:at + n, :], tall).then_inc(loaded[q].sem, DMA)

            @block.sync
            def _(sp):
                load(sp, 0)

            @block.tensor
            def _(pe):
                for f, (_, _, blocks, a, b, q) in enumerate(fills):
                    pe.wait_ge(loaded[q - 1].sem, DMA)
                    if f >= 2:
                        pe.wait_ge(kept[f % 2].sem, f // 2)
                    for j, n in enumerate(blocks):
                        last = nc.tensor.transpose(bank[f % 2][0:b, j * P:j * P + a], raw[0:a, n, 0:b], const["ident"][0:a, 0:a])
                    last.then_inc(turned.sem, 1)

            def keep(engine, which, copy):
                for f in range(which, len(fills), 2):
                    dst, k, blocks, a, b, _ = fills[f]
                    engine.wait_ge(turned.sem, f + 1)
                    width = (len(blocks) - 1) * P + a
                    copy(dst[0:b, k * P:k * P + width], bank[f % 2][0:b, 0:width]).then_inc(kept[which].sem, 1)

            @block.scalar
            def _(act):
                load(act, 1)
                keep(act, 1, lambda out, in_: nc.scalar.activation(out, in_, ACT.Copy))

            @block.vector
            def _(dve):
                keep(dve, 0, nc.vector.tensor_copy)
        t.clear_counts()


MLP = 64
LOG_T_MIN, LOG_T_MAX = float(np.log(0.1)), float(np.log(10.0))


def cross_attention(nc, const, tag, xT, context, wq, bq, wk, bk, wv, bv, wo, bo, turn, temper=None):
    with ExitStack() as ctx:
        t = Tools(ctx, nc, tag)
        KS = GB * S
        UNITS = [(0, 6), (6, 6), (12, 4)]
        RING = 2 * GB
        w = {n: t.sb(f"w_{n}", [P, D]) for n in "qkvo"}
        bias = {n: t.sb(f"b_{n}", [P, 1]) for n in "qko"}
        bv_row = t.sb("bv_row", [S, D])
        heads = t.sb("heads", [P, H])
        ctx_in = t.sb("ctx_in", [S, GB, D])
        cT = t.sb("cT", [P, KS])
        kT = t.sb("kT", [P, KS])
        q = t.sb("q", [P, GROUP])
        vaug = t.sb("vaug", [S, B, H, DK + 1])
        kbd = [t.sb(f"kbd{r}", [P, H, S]) for r in range(2)]
        m = t.sb("m", [P, B, H])
        dist = t.sb("dist", [P, RING, H, S])
        probs = [t.sb(f"probs{r}", [P, H, S]) for r in range(2)]
        pt = [t.sb(f"pt{r}", [S, H * T]) for r in range(2)]
        rz = [t.sb(f"rz{r}", [P, H]) for r in range(2)]
        zmax = [t.sb(f"zmax{r}", [P, H]) for r in range(2)]
        o = t.sb("o", [P, GB, H, DK])
        oT = t.sb("oT", [P, GROUP])
        y = t.sb("y", [P, GROUP])
        sq = t.sb("sq", [P, GROUP])
        logs = t.sb("logs", [P, GROUP])
        inv = t.sb("inv", [P, GROUP])
        ps_s = t.ps("scores", [P, 3, 512])
        ps_x = t.ps("proj", [P, 512])
        ps_t = [t.ps(f"turned{r}", [P, 512]) for r in range(2)]
        ps_o = t.ps("out", [P, 512])
        ps_n = t.ps("norm", [P, 512])
        if temper:
            tw1, tb1, tw2, tb2, tw3, tb3 = temper
            w1raw = t.sb("w1raw", [P, MLP, 3])
            w1b = t.sb("w1b", [P, 3, P])
            w2T = t.sb("w2T", [P, P])
            w3raw = t.sb("w3raw", [P, 1])
            w3b = t.sb("w3b", [P, P])
            mb1, mb2, mb3 = t.sb("mb1", [P, 1]), t.sb("mb2", [P, 1]), t.sb("mb3", [P, 1])
            half = t.sb("half", [P, 1])
            e1 = [t.sb(f"e1_{r}", [P, H, S]) for r in range(2)]
            e1sq = [t.sb(f"e1sq_{r}", [P, H, S]) for r in range(2)]
            qs, ks, qk = (t.sb(n, [P, GB]) for n in ("qs", "ks", "qk"))
            mean_f, z1, s2, var_f = (t.sb(n, [P, GB, H]) for n in ("mean_f", "z1", "s2", "var_f"))
            g1, g2, lt, rt = (t.sb(n, [P, GB * H]) for n in ("g1", "g2", "lt", "rt"))

        loaded = t.count("loaded", weight=DMA)
        masked = t.count("masked")
        ctx_loaded = t.count("ctx_loaded", 1, DMA)
        ctx_turned = t.count("ctx_turned")
        ct_ready = t.count("ct_ready")
        k_mm = t.count("k_mm")
        k_ready = t.count("k_ready")
        v_mm = t.count("v_mm")
        v_ready = t.count("v_ready", credits=1)
        q_mm = t.count("q_mm")
        q_ready = t.count("q_ready")
        kbd_ready = t.count("kbd_ready", GB, credits=1)
        s_mm = [t.count(f"s_mm{k}", GB, credits=2) for k in range(3)]
        m_ready = [t.count(f"m_ready{k}", GB) for k in range(3)]
        d_ready = [t.count(f"d_ready{k}", GB, credits=1) for k in range(3)]
        p_ready = t.count("p_ready", GB, credits=RING)
        t_mm = [t.count(f"t_mm{r}", 2 * GB, credits=4) for r in range(2)]
        pt_ready = [t.count(f"pt_ready{r}", 2 * GB, credits=1) for r in range(2)]
        pv_mm = t.count("pv_mm", GB, credits=2)
        z_ready = t.count("z_ready", GB)
        rz_ready = t.count("rz_ready", GB)
        o_ready = t.count("o_ready", GB, credits=1)
        ot_mm = t.count("ot_mm", credits=1)
        ot_ready = t.count("ot_ready")
        wo_mm = t.count("wo_mm")
        xT_ready = t.count("xT_ready")
        norm = Norm(t, const, "ln", 1, y, sq, logs, inv, ps_n)
        given = [v_ready, kbd_ready, *s_mm, *d_ready, p_ready, *t_mm, *pt_ready, pv_mm, o_ready, ot_mm, norm.log_ready]
        if temper:
            e1_ready = t.count("e1_ready", GB)
            e1sq_ready = t.count("e1sq_ready", GB)
            s2_ready = t.count("s2_ready", GB, credits=2)
            small = t.count("small", 5)
            mean_ready = t.count("mean_ready", credits=1)
            feat_ready = t.count("feat_ready", credits=1)
            hid_mm = t.count("hid_mm", credits=1)
            g1_ready = t.count("g1_ready")
            h2_mm = t.count("h2_mm")
            g2_ready = t.count("g2_ready")
            logt_mm = t.count("logt_mm")
            lt_ready = t.count("lt_ready", 2, credits=2)
            rt_ready = t.count("rt_ready")
            pre_ready = t.count("pre_ready", GB, credits=RING)
            given += [s2_ready, mean_ready, feat_ready, hid_mm, lt_ready, pre_ready]

        SLOT0 = [("scale", 2, 1), ("x0", 2, 2), ("soft", 1, 3), ("s0", 0, 0), ("s1", 0, 0), ("x1", 2, 2), ("s2", 0, 0),
                 ("pre", 2, 3), ("kbd", 0, 1), ("exp", 2, 3), ("sums", 1, 3), ("feat", 1, 0), ("v0", 2, 2), ("v1", 2, 2)]
        SLOT1 = [("scale", 2, 2), ("x0", 2, 3), ("s0", 0, 1), ("t1", 1, 0), ("s1", 0, 1), ("x1", 2, 3), ("s2", 0, 1),
                 ("kbd", 0, 2), ("v0", 2, 3), ("t2", 1, 0), ("v1", 2, 3), ("t3", 1, 0), ("soft", 0, 0), ("sums", 0, 0), ("mean", 0, 0), ("pre", 1, 0)]
        SLOT2 = [("scale", 2, 3), ("soft", 0, 1), ("s0", 0, 2), ("s1", 0, 2), ("s2", 0, 2), ("collect", 2, 0), ("pre", 1, 1), ("kbd", 0, 3),
                 ("values", 0, 0), ("context", -1, 0), ("mix", 2, 0), ("exp", 1, 0), ("x0", 1, 0), ("mean0", 2, 0), ("x1", 1, 0),
                 ("keys", -1, 0), ("exp", 1, 1), ("sums", 0, 1), ("v0", 1, 0), ("v1", 1, 0)]
        SLOT3 = [("scale", 1, 0), ("x0", 1, 1), ("soft", 0, 2), ("s0", 0, 3), ("s1", 0, 3), ("x1", 1, 1), ("s2", 0, 3), ("queries", -1, 0),
                 ("pre", 1, 2), ("kbd", -1, 0), ("exp", 1, 2), ("sums", 0, 2), ("v0", 1, 1), ("var0", 2, 0), ("v1", 1, 1)]
        TEMPER_ONLY = ("soft", "sums", "feat", "mean", "t1", "t2", "t3", "pre")
        ORDER = [s for s in SLOT0 + SLOT1 + SLOT2 + SLOT3 if temper or s[0] not in TEMPER_ONLY]
        LOOP = (2, NG - 1)

        def run(engine, step):
            def peeled(g):
                for kind, lag, b in ORDER:
                    if 0 <= g - lag < NG:
                        step(kind, g - lag, b)
            for g in range(-1, LOOP[0]):
                peeled(g)
            with engine.Fori(*LOOP) as g:
                for kind, lag, b in ORDER:
                    step(kind, g - lag, b)
            for g in range(LOOP[1], NG + 2):
                peeled(g)

        if turn:
            load_transposed(nc, const, f"{tag}_w", [(w[n][:, :], a) for n, a in zip("qkvo", (wq, wk, wv, wo))], ps_t)
        NPRE = 5
        with nc.Block() as block:

            @block.sync
            def _(sp):
                loads = [(bias["q"][:, :], bq.rearrange("(p a) -> p a", a=1)), (bias["k"][:, :], bk.rearrange("(p a) -> p a", a=1)),
                         (bias["o"][:, :], bo.rearrange("(p a) -> p a", a=1)), (bv_row[:, :], bv.partition_broadcast(S))]
                if not turn:
                    loads += [(w[n][:, :], a) for n, a in zip("qkvo", (wq, wk, wv, wo))]
                for dst, src in loads:
                    sp.dma_start(dst, src).then_inc(loaded.sem, DMA)
                if temper:
                    sp.wait_ge(masked.sem, 2 + NPRE)
                    for dst, src in ((w1raw[:, :, :].rearrange("p a b -> p (a b)"), tw1.rearrange("a b -> (a b)").partition_broadcast(P)),
                                     (mb1[0:MLP, :], tb1.rearrange("(p a) -> p a", a=1)), (mb2[0:MLP, :], tb2.rearrange("(p a) -> p a", a=1)),
                                     (w3raw[0:MLP, :], tw3.rearrange("a p -> p a")), (mb3[:, :], tb3.partition_broadcast(P))):
                        sp.dma_start(dst, src, allow_slow_non_contiguous=True).then_inc(loaded.sem, DMA)
                sp.wait_ge(loaded.sem, (len(loads) + (5 if temper else 0)) * DMA)

            @block.gpsimd
            def _(pool):
                pool.memset(heads[:, :], 1.0).then_inc(masked.sem, 1)
                pool.wait_ge(masked.sem, 1)
                pool.affine_select(out=heads[:, :], in_=heads[:, :], compare_op=ALU.is_ge, fill=0.0, base=0,
                                   pattern=[[-DK, H]], channel_multiplier=1).then_inc(masked.sem, 1)
                if temper:
                    for z in (w1b[:, :, :], w2T[:, :], w3raw[:, :], mb1[:, :], mb2[:, :]):
                        pool.memset(z, 0.0).then_inc(masked.sem, 1)
                    pool.memset(half[:, :], float(np.log(0.5)))
                pool.wait_ge(masked.sem, 2)
                pool.affine_select(out=heads[:, :], in_=heads[:, :], compare_op=ALU.is_ge, fill=0.0, base=DK - 1,
                                   pattern=[[DK, H]], channel_multiplier=-1)

            @block.vector
            def _(dve):
                nc.vector.memset(vaug[:, :, :, DK:DK + 1], 1.0)
                if temper:
                    dve.wait_ge(loaded.sem, (4 + 5) * DMA)
                    root = float(np.sqrt(DK))
                    for f, s in enumerate((1.0 / (root * T * S), 1.0 / (root * T), 1.0 / T)):
                        nc.vector.tensor_scalar(w1b[:, f, 0:MLP], w1raw[:, :, f], s, None, ALU.mult)
                    nc.vector.tensor_scalar(w3b[:, :], const["ones"][:, :], w3raw[:, 0:1], None, ALU.mult)
        if temper:
            load_transposed(nc, const, f"{tag}_w2", [(w2T[:, :], tw2)], ps_t)

        def one(a, n, *rest):
            return a[(slice(None), bass.ds(n, 1)) + rest].rearrange("p a n -> p (a n)")

        def ring(j, b):
            return (j & 1) * GB + b

        with nc.Block() as block:

            @block.sync
            def _(sp):
                def load(first):
                    sp.dma_start(ctx_in[:, :, :], context[first].rearrange("b s d -> s b d")).then_inc(ctx_loaded.sem, DMA)
                load(slice(0, GB))
                with sp.Fori(0, NG - 1) as j:
                    sp.wait_ge(ctx_turned.sem, ctx_turned.after(j))
                    load(bass.ds((j + 1) * GB, GB))

            @block.tensor
            def _(pe):
                mm, turn_ = nc.tensor.matmul, nc.tensor.transpose
                ident = const["ident"]

                def step(kind, j, b):
                    if kind == "context":
                        pe.wait_ge(ctx_loaded.sem, ctx_loaded.after(j))
                        pe.wait_ge(v_ready.sem, v_ready.free(j))
                        for c in range(GB):
                            last = turn_(ps_x[:, c * S:(c + 1) * S], ctx_in[:, c, :], ident[0:S, 0:S])
                        last.then_inc(ctx_turned.sem, 1)
                    elif kind == "keys":
                        pe.wait_ge(ct_ready.sem, ct_ready.after(j))
                        mm(ps_x[:, 0:KS], w["k"][:, :], cT[:, :], start=True, stop=True).then_inc(k_mm.sem, 1)
                    elif kind == "queries":
                        pe.wait_ge(k_ready.sem, k_ready.after(j))
                        mm(ps_x[:, :], w["q"][:, :], group_of(xT, j, 0, 1), start=True, stop=True).then_inc(q_mm.sem, 1)
                    elif kind == "values":
                        pe.wait_ge(q_ready.sem, q_ready.after(j))
                        if temper:
                            pe.wait_ge(lt_ready.sem, lt_ready.free(j))
                        for c in range(GB):
                            last = mm(ps_x[0:S, c * D:(c + 1) * D], cT[:, c * S:(c + 1) * S], w["v"][:, :], start=True, stop=True)
                        last.then_inc(v_mm.sem, 1)
                    elif kind in ("s0", "s1", "s2"):
                        k = int(kind[1])
                        if k == 0:
                            pe.wait_ge(kbd_ready.sem, kbd_ready.after(j, b + 1))
                            if b == 0:
                                pe.wait_ge(q_ready.sem, q_ready.after(j))
                        pe.wait_ge(d_ready[k].sem, d_ready[k].free(j, b))
                        h0, nh = UNITS[k]
                        mm(ps_s[:, k, 0:nh * S], q[:, b * T:(b + 1) * T], kbd[b % 2][:, h0:h0 + nh, :].rearrange("p h s -> p (h s)"),
                           start=True, stop=True).then_inc(s_mm[k].sem, 1)
                    elif kind in ("x0", "x1"):
                        half_ = int(kind[1])
                        if half_ == 0:
                            pe.wait_ge(p_ready.sem, p_ready.after(j, b + 1))
                        for r in range(2):
                            pe.wait_ge(pt_ready[r].sem, pt_ready[r].free(j, 2 * b + half_))
                            for h in range(4):
                                last = turn_(ps_t[r][0:S, h * T:(h + 1) * T], probs[b % 2][:, 8 * half_ + 4 * r + h, :], ident[:, :])
                            last.then_inc(t_mm[r].sem, 1)
                    elif kind in ("v0", "v1"):
                        half_ = int(kind[1])
                        for r in range(2):
                            pe.wait_ge(pt_ready[r].sem, pt_ready[r].after(j, 2 * b + half_ + 1))
                        if half_ == 0:
                            pe.wait_ge(o_ready.sem, o_ready.free(j, b))
                            if b == 0:
                                pe.wait_ge(v_ready.sem, v_ready.after(j))
                        for h in range(8 * half_, 8 * half_ + 8):
                            last = mm(ps_o[:, h * (DK + 1):(h + 1) * (DK + 1)], pt[b % 2][:, h * T:(h + 1) * T],
                                      one(vaug, j * GB + b, h, slice(None)), start=True, stop=True)
                        if half_:
                            last.then_inc(pv_mm.sem, 1)
                    elif kind == "t1":
                        pe.wait_ge(feat_ready.sem, feat_ready.after(j))
                        if isinstance(j, int) and j == NG - 1:
                            pe.wait_ge(v_ready.sem, v_ready.after(j))
                        else:
                            pe.wait_ge(q_ready.sem, q_ready.after(j + 1))
                        for f, feat in enumerate((mean_f[:, :, :], m[:, bass.ds(j * GB, GB), :], var_f[:, :, :])):
                            last = mm(ps_x[:, 0:GB * H], w1b[:, f, :], feat.rearrange("p b h -> p (b h)"), start=(f == 0), stop=(f == 2))
                        last.then_inc(hid_mm.sem, 1)
                    elif kind == "t2":
                        pe.wait_ge(g1_ready.sem, g1_ready.after(j))
                        mm(ps_x[:, 0:GB * H], w2T[:, :], g1[:, :], start=True, stop=True).then_inc(h2_mm.sem, 1)
                    elif kind == "t3":
                        pe.wait_ge(g2_ready.sem, g2_ready.after(j))
                        mm(ps_x[:, 0:GB * H], w3b[:, :], g2[:, :], start=True, stop=True).then_inc(logt_mm.sem, 1)
                    elif kind == "collect":
                        pe.wait_ge(o_ready.sem, o_ready.after(j, GB))
                        pe.wait_ge(norm.log_ready.sem, norm.log_ready.free(j))
                        for c in range(GB):
                            last = turn_(ps_n[:, c * T:(c + 1) * T], o[:, c, :, :].rearrange("p h d -> p (h d)"), ident[:, :])
                        last.then_inc(ot_mm.sem, 1)
                    elif kind == "mix":
                        pe.wait_ge(ot_ready.sem, ot_ready.after(j))
                        mm(ps_n[:, :], w["o"][:, :], oT[:, :], start=True, stop=True).then_inc(wo_mm.sem, 1)
                    elif kind == "mean0":
                        norm.mean(nc, pe, j, 0)
                    elif kind == "var0":
                        norm.variance(nc, pe, j, 0)

                run(pe, step)

            @block.scalar
            def _(act):
                f = nc.scalar.activation
                nc.scalar.preload_act_table_set(LN_EXP)

                def step(kind, j, b):
                    if kind == "context":
                        act.wait_ge(ctx_turned.sem, ctx_turned.after(j))
                        f(cT[:, :], ps_x[:, 0:KS], ACT.Copy).then_inc(ct_ready.sem, 1)
                    elif kind == "keys":
                        act.wait_ge(kbd_ready.sem, kbd_ready.free(j))
                        if temper:
                            act.wait_ge(mean_ready.sem, mean_ready.free(j))
                        act.wait_ge(k_mm.sem, k_mm.after(j))
                        f(kT[:, :], ps_x[:, 0:KS], ACT.Identity, bias=bias["k"][:, :]).then_inc(k_ready.sem, 1)
                    elif kind == "queries":
                        act.wait_ge(q_mm.sem, q_mm.after(j))
                        f(q[:, :], ps_x[:, :], ACT.Identity, bias=bias["q"][:, :]).then_inc(q_ready.sem, 1)
                    elif kind == "soft":
                        act.wait_ge(s2_ready.sem, s2_ready.free(j, b))
                        act.wait_ge(d_ready[2].sem, d_ready[2].after(j, b + 1))
                        f(e1[b % 2][:, :, :], dist[:, bass.ds(ring(j, b), 1), :, :].rearrange("p a h s -> p (a h) s"), ACT.Exp,
                          scale=DK ** -0.5).then_inc(e1_ready.sem, 1)
                        act.wait_ge(e1_ready.sem, e1_ready.after(j, b + 1))
                        f(e1sq[b % 2][:, :, :], e1[b % 2][:, :, :], ACT.Square).then_inc(e1sq_ready.sem, 1)
                    elif kind == "t1":
                        act.wait_ge(hid_mm.sem, hid_mm.after(j))
                        f(g1[:, :], ps_x[:, 0:GB * H], ACT.Gelu, bias=mb1[:, :]).then_inc(g1_ready.sem, 1)
                    elif kind == "t2":
                        act.wait_ge(h2_mm.sem, h2_mm.after(j))
                        f(g2[:, :], ps_x[:, 0:GB * H], ACT.Gelu, bias=mb2[:, :]).then_inc(g2_ready.sem, 1)
                    elif kind == "t3":
                        nc.scalar.preload_act_table_set(LN_EXP)
                        act.wait_ge(pre_ready.sem, pre_ready.after(j, 0))
                        act.wait_ge(lt_ready.sem, lt_ready.after(j, 2))
                        f(rt[:, :], lt[:, :], ACT.Exp, bias=half[:, :], scale=-1.0).then_inc(rt_ready.sem, 1)
                    elif kind == "exp":
                        if temper:
                            act.wait_ge(pre_ready.sem, pre_ready.after(j, b + 1))
                            f(probs[b % 2][:, :, :], probs[b % 2][:, :, :], ACT.Exp).then_inc(p_ready.sem, 1)
                        else:
                            act.wait_ge(t_mm[1].sem, t_mm[1].free(j, 2 * b + 1))
                            act.wait_ge(d_ready[2].sem, d_ready[2].after(j, b + 1))
                            f(probs[b % 2][:, :, :], dist[:, bass.ds(ring(j, b), 1), :, :].rearrange("p a h s -> p (a h) s"), ACT.Exp,
                              scale=DK ** -0.5).then_inc(p_ready.sem, 1)
                    elif kind in ("x0", "x1"):
                        half_ = int(kind[1])
                        if half_ == 0:
                            act.wait_ge(pv_mm.sem, pv_mm.free(j, b))
                        for r in range(2):
                            act.wait_ge(t_mm[r].sem, t_mm[r].after(j, 2 * b + half_ + 1))
                            c = 2 * half_ + r
                            f(pt[b % 2][:, 4 * c * T:4 * (c + 1) * T], ps_t[r][0:S, :], ACT.Relu).then_inc(pt_ready[r].sem, 1)
                    elif kind == "collect":
                        act.wait_ge(ot_mm.sem, ot_mm.after(j))
                        f(oT[:, :], ps_n[:, :], ACT.Copy).then_inc(ot_ready.sem, 1)
                    elif kind == "mean0":
                        norm.square(nc, act, j, 0)
                    elif kind == "var0":
                        norm.inverse(nc, act, j, 0)

                run(act, step)

            @block.gpsimd
            def _(pool):
                def step(kind, j, b):
                    if kind == "kbd":
                        if b == 0:
                            pool.wait_ge(k_ready.sem, k_ready.after(j))
                        pool.wait_ge(s_mm[2].sem, s_mm[2].free(j, b))
                        keys = kT[:, b * S:(b + 1) * S].unsqueeze(1).broadcast_to([P, H, S])
                        pool.tensor_tensor(kbd[b % 2][:, :, :], keys, heads[:, :].unsqueeze(2).broadcast_to([P, H, S]), ALU.mult).then_inc(kbd_ready.sem, 1)
                    elif kind == "pre":
                        if b == 0:
                            pool.wait_ge(rt_ready.sem, rt_ready.after(j))
                        pool.wait_ge(t_mm[1].sem, t_mm[1].free(j, 2 * b + 1))
                        r = rt[:, b * H:(b + 1) * H].unsqueeze(2).broadcast_to([P, H, S])
                        pool.tensor_tensor(probs[b % 2][:, :, :], dist[:, bass.ds(ring(j, b), 1), :, :].rearrange("p a h s -> p (a h) s"), r,
                                           ALU.mult).then_inc(pre_ready.sem, 1)

                run(pool, step)

            @block.vector
            def _(dve):
                v = nc.vector
                for c in given:
                    c.give(dve)

                def scores(k):
                    h0, nh = UNITS[k]
                    return ps_s[:, k, 0:nh * S].rearrange("p (h s) -> p h s", s=S)

                def greatest(j, b, k):
                    h0, nh = UNITS[k]
                    dve.wait_ge(s_mm[k].sem, s_mm[k].after(j, b + 1))
                    v.tensor_reduce(one(m, j * GB + b, slice(h0, h0 + nh)), scores(k), AX.X, ALU.max).then_inc(m_ready[k].sem, 1)

                def subtract(j, b, k):
                    h0, nh = UNITS[k]
                    dve.wait_ge(m_ready[k].sem, m_ready[k].after(j, b + 1))
                    v.tensor_tensor(dist[:, bass.ds(ring(j, b), 1), h0:h0 + nh, :].rearrange("p a h s -> p (a h) s"), scores(k),
                                    one(m, j * GB + b, slice(h0, h0 + nh)).unsqueeze(2).broadcast_to([P, nh, S]),
                                    ALU.subtract).then_inc(d_ready[k].sem, 1)

                def step(kind, j, b):
                    if kind == "values":
                        dve.wait_ge(v_mm.sem, v_mm.after(j))
                        row = bv_row[:, :].unsqueeze(1).broadcast_to([S, GB, D]).rearrange("p b (h d) -> p b h d", d=DK)
                        v.tensor_tensor(vaug[:, bass.ds(j * GB, GB), :, 0:DK], ps_x[0:S, :].rearrange("p (b h d) -> p b h d", b=GB, d=DK),
                                        row, ALU.add).then_inc(v_ready.sem, 1)
                    elif kind == "mean":
                        dve.wait_ge(q_ready.sem, q_ready.after(j))
                        v.tensor_reduce(qs[:, :], q[:, :].rearrange("p (b t) -> p b t", b=GB), AX.X, ALU.add)
                        v.tensor_reduce(ks[:, :], kT[:, :].rearrange("p (b s) -> p b s", b=GB), AX.X, ALU.add).then_inc(small.sem, 1)
                        dve.wait_ge(small.sem, small.after(j, 1))
                        v.tensor_tensor(qk[:, :], qs[:, :], ks[:, :], ALU.mult).then_inc(small.sem, 1)
                        dve.wait_ge(small.sem, small.after(j, 2))
                        dve.wait_ge(hid_mm.sem, hid_mm.free(j))
                        v.tensor_tensor(mean_f[:, :, :], heads[:, :].unsqueeze(1).broadcast_to([P, GB, H]),
                                        qk[:, :].unsqueeze(2).broadcast_to([P, GB, H]), ALU.mult).then_inc(mean_ready.sem, 1)
                    elif kind == "s0":
                        used = pre_ready if temper else p_ready
                        dve.wait_ge(used.sem, used.free(j, b))
                        greatest(j, b, 0)
                    elif kind == "s1":
                        greatest(j, b, 1)
                        subtract(j, b, 0)
                    elif kind == "s2":
                        greatest(j, b, 2)
                        subtract(j, b, 1)
                        subtract(j, b, 2)
                    elif kind == "sums":
                        if b == 0:
                            dve.wait_ge(feat_ready.sem, feat_ready.free(j))
                        dve.wait_ge(e1_ready.sem, e1_ready.after(j, b + 1))
                        v.tensor_reduce(z1[:, b, :], e1[b % 2][:, :, :], AX.X, ALU.add)
                        dve.wait_ge(e1sq_ready.sem, e1sq_ready.after(j, b + 1))
                        v.tensor_reduce(s2[:, b, :], e1sq[b % 2][:, :, :], AX.X, ALU.add).then_inc(s2_ready.sem, 1)
                    elif kind == "feat":
                        dve.wait_ge(s2_ready.sem, s2_ready.after(j, GB))
                        v.reciprocal(z1[:, :, :], z1[:, :, :]).then_inc(small.sem, 1)
                        dve.wait_ge(small.sem, small.after(j, 3))
                        v.tensor_tensor(s2[:, :, :], s2[:, :, :], z1[:, :, :], ALU.mult).then_inc(small.sem, 1)
                        dve.wait_ge(small.sem, small.after(j, 4))
                        v.tensor_tensor(s2[:, :, :], s2[:, :, :], z1[:, :, :], ALU.mult).then_inc(small.sem, 1)
                        dve.wait_ge(small.sem, small.after(j, 5))
                        dve.wait_ge(hid_mm.sem, hid_mm.free(j))
                        v.tensor_scalar(var_f[:, :, :], s2[:, :, :], 1.0 / (S - 1), -1.0 / (S * (S - 1)), ALU.mult, ALU.add).then_inc(feat_ready.sem, 1)
                    elif kind == "t3":
                        dve.wait_ge(logt_mm.sem, logt_mm.after(j))
                        v.tensor_scalar(lt[:, :], ps_x[:, 0:GB * H], mb3[:, 0:1], LOG_T_MIN, ALU.add, ALU.max).then_inc(lt_ready.sem, 1)
                        dve.wait_ge(lt_ready.sem, lt_ready.after(j, 1))
                        v.tensor_scalar(lt[:, :], lt[:, :], LOG_T_MAX, None, ALU.min).then_inc(lt_ready.sem, 1)
                    elif kind == "scale":
                        dve.wait_ge(pv_mm.sem, pv_mm.after(j, b + 1))
                        heads_out = ps_o[:, 0:H * (DK + 1)].rearrange("p (h d) -> p h d", d=DK + 1)
                        v.tensor_scalar(zmax[b % 2][:, :], heads_out[:, :, DK:DK + 1].rearrange("p h a -> p (h a)"), 1e-30, None, ALU.max).then_inc(z_ready.sem, 1)
                        dve.wait_ge(z_ready.sem, z_ready.after(j, b + 1))
                        v.reciprocal(rz[b % 2][:, :], zmax[b % 2][:, :]).then_inc(rz_ready.sem, 1)
                        dve.wait_ge(rz_ready.sem, rz_ready.after(j, b + 1))
                        dve.wait_ge(ot_mm.sem, ot_mm.free(j))
                        v.tensor_tensor(o[:, b, :, :], heads_out[:, :, 0:DK], rz[b % 2][:, :].unsqueeze(2).broadcast_to([P, H, DK]),
                                        ALU.mult).then_inc(o_ready.sem, 1)
                    elif kind == "mix":
                        dve.wait_ge(wo_mm.sem, wo_mm.after(j))
                        v.scalar_tensor_tensor(y[:, :], ps_n[:, :], bias["o"][:, 0:1], group_of(xT, j, 0, 1), ALU.add, ALU.add).then_inc(norm.y_ready.sem, 1)
                    elif kind == "mean0":
                        norm.centre(nc, dve, j, 0)
                    elif kind == "var0":
                        norm.divide(nc, dve, j, 0, group_of(xT, j, 0, 1), xT_ready)

                run(dve, step)
        t.clear_counts()


class DoubleNorm:

    def __init__(self, t, const, name, per, y, sq, logs, inv, bank, gamma, beta, y_credits=0):
        self.own = Norm(t, const, f"{name}_own", per, y, sq, logs, inv, bank, y_credits)
        self.stream = Norm(t, const, f"{name}_str", per, y, sq, logs, inv, bank)
        self.gained = t.count(f"{name}_gained", per)
        self.gamma, self.beta = gamma, beta

    def give(self, engine):
        self.own.log_ready.give(engine)
        self.stream.log_ready.give(engine)

    def tensor(self, nc, pe, i, n):
        self.own.tensor(nc, pe, i, n)
        self.stream.tensor(nc, pe, i, n)

    def scalar(self, nc, act, i, n):
        self.own.scalar(nc, act, i, n)
        self.stream.scalar(nc, act, i, n)

    def gain(self, nc, dve, i, n, x):
        y = self.own.y[:, :]
        dve.wait_ge(self.own.inv_ready.sem, self.own.inv_ready.after(i, n + 1))
        nc.vector.scalar_tensor_tensor(y, y, self.gamma[:, 0:1], self.own.inv[:, :], ALU.mult, ALU.mult).then_inc(self.gained.sem, 1)
        dve.wait_ge(self.gained.sem, self.gained.after(i, n + 1))
        nc.vector.scalar_tensor_tensor(y, y, self.beta[:, 0:1], x, ALU.add, ALU.add).then_inc(self.stream.y_ready.sem, 1)

    def vector(self, nc, dve, i, n, x, out, done):
        self.own.centre(nc, dve, i, n)
        self.gain(nc, dve, i, n, x)
        self.stream.centre(nc, dve, i, n)
        self.stream.divide(nc, dve, i, n, out, done)


class Chain:

    def __init__(self, t, name, engine):
        self.done, self.engine, self.n = t.count(name), engine, 0

    def __call__(self, instruction):
        instruction.then_inc(self.done.sem, 1)
        self.n += 1
        self.engine.wait_ge(self.done.sem, self.n)


TILES, CLUSTERS, TPC = 64, 8, 8
COMP, GRID, KNOTS = 32, 16, 8


def first_max_one_hot(link, v, g, top, cand, iota, n):
    wide = lambda a: a.unsqueeze(2).broadcast_to([P, B, n])
    link(v.tensor_reduce(top, g, AX.X, ALU.max))
    link(v.tensor_tensor(cand, g, wide(top), ALU.is_equal))
    link(v.scalar_tensor_tensor(cand, cand, -float(n), iota, ALU.mult, ALU.add))
    link(v.tensor_reduce(top, cand, AX.X, ALU.min))
    link(v.tensor_tensor(cand, cand, wide(top), ALU.is_equal))


def tile_ffn(nc, const, xT, raw, knots, temp, cw1, cb1, cw2, cb2, sw1, sb1, sw2, sb2, dirs, gamma, beta, scale):
    with ExitStack() as ctx:
        t = Tools(ctx, nc, "ffn")
        U = 2
        ITER = NG // U
        NS = CLUSTERS + TILES
        TAB = 3 * GRID + GRID + 1
        rawT = t.sb("rawT", [P, TILES])
        sig = t.sb("sig", [P, NS])
        q = t.sb("q", [P, TILES])
        lt = t.sb("lt", [P, TILES])
        csum = t.sb("csum", [P, CLUSTERS])
        cneg = t.sb("cneg", [P, CLUSTERS])
        w1 = t.sb("w1", [P, COMP])
        b1 = t.sb("b1", [COMP, 1])
        w2 = t.sb("w2", [COMP, 2])
        b2 = t.sb("b2", [P, 2])
        table = t.sb("table", [TILES, TAB])
        dir_sb = t.sb("dirs", [TILES, D])
        knot = t.sb("knot", [P, KNOTS])
        slope = t.sb("slope", [P, KNOTS])
        nit = t.sb("nit", [P, 1])
        scale_c = t.sb("scale", [P, 1])
        gamma_c, beta_c = t.sb("gamma", [P, 1]), t.sb("beta", [P, 1])
        iota_i = t.sb("iota_i", [P, B, TPC], I32)
        iota = t.sb("iota", [P, B, TPC])
        scores = t.sb("scores", [P, B, NS])
        comp = t.sb("comp", [P, B, 2])
        xs = [t.sb(f"xs{u}", [P, GROUP]) for u in range(U)]
        hid = [t.sb(f"hid{u}", [COMP, GROUP]) for u in range(U)]
        e = t.sb("e", [P, B * 8])
        low = t.sb("low", [P, B * 8])
        frac = t.sb("frac", [P, B * 8])
        term = t.sb("term", [P, B * 8])
        inc = t.sb("inc", [P, B * 8])
        gates = t.sb("gates", [P, B * 8])
        top = t.sb("top", [P, B])
        cluster = t.sb("cluster", [P, B, CLUSTERS])
        local = t.sb("local", [P, B, TPC])
        picked = t.sb("picked", [P, B, CLUSTERS, TPC])
        mine = t.sb("mine", [P, B, TPC])
        oh = [t.sb(f"oh{u}", [P, GB, P]) for u in range(U)]
        ohm = [t.sb(f"ohm{u}", [P, GB, P]) for u in range(U)]
        ohT = [t.sb(f"ohT{u}", [TILES, GROUP]) for u in range(U)]
        ohmT = [t.sb(f"ohmT{u}", [TILES, GROUP]) for u in range(U)]
        ha = t.sb("ha", [P, GB, GRID])
        hb = t.sb("hb", [P, GB, GRID])
        mag = t.sb("mag", [P, GB])
        y, sq, logs, inv = ([t.sb(f"{name}{u}", [P, GROUP]) for u in range(U)] for name in ("y", "sq", "logs", "inv"))
        ps_a = [t.ps(f"bank_a{u}", [P, 512]) for u in range(U)]
        ps_b = [t.ps(f"bank_b{u}", [P, 512]) for u in range(U)]
        ps_c = [t.ps(f"bank_c{u}", [P, 512]) for u in range(U)]
        ps_n = [t.ps(f"norm{u}", [P, 512]) for u in range(U)]

        load_transposed(nc, const, "ffn_sig", [(rawT[:, :], raw)], ps_a)
        loaded = t.count("loaded", weight=DMA)
        N_LOADS = 15
        table_zeroed = t.count("table_zeroed")
        xs_ready = t.count("xs_ready", U)
        sc_mm = t.count("sc_mm", U)
        sc_kept = t.count("sc_kept", U, credits=U)
        hid_mm = t.count("hid_mm", U)
        hid_ready = t.count("hid_ready", U, credits=U)
        comp_mm = t.count("comp_mm", U)
        comp_kept = t.count("comp_kept", U, credits=U)
        sig_ready = t.count("sig_ready")
        iota_made = t.count("iota_made")
        with nc.Block() as block:

            @block.sync
            def _(sp):
                col = lambda a: a.rearrange("(p a) -> p a", a=1)
                loads = [(w1[:, :], cw1), (b1[:, :], col(cb1)), (w2[:, :], cw2), (b2[:, :], cb2.partition_broadcast(P)),
                         (knot[:, :], knots.partition_broadcast(P)), (nit[:, :], temp.partition_broadcast(P)),
                         (scale_c[:, :], scale.partition_broadcast(P)), (gamma_c[:, :], col(gamma)), (beta_c[:, :], col(beta)),
                         (dir_sb[:, :], dirs), (table[:, 0:2 * GRID], sw1.rearrange("n i g -> n (i g)")),
                         (table[:, 2 * GRID:3 * GRID], sb1), (table[:, 3 * GRID:4 * GRID], sw2.rearrange("n g a -> n (g a)")),
                         (table[:, 4 * GRID:], sb2)]
                for dst, src in loads:
                    sp.dma_start(dst, src).then_inc(loaded.sem, DMA)

            @block.gpsimd
            def _(pool):
                pool.iota(iota_i[:, :, :], pattern=[[0, B], [1, TPC]], base=0, channel_multiplier=0).then_inc(iota_made.sem, 1)

            @block.vector
            def _(dve):
                v = nc.vector
                for a in (*oh, *ohm):
                    v.memset(a[:, :, TILES:], 0.0)
                link = Chain(t, "setup", dve)
                for c in (sc_kept, hid_ready, comp_kept):
                    c.give(dve)
                signs = sig[:, CLUSTERS:]
                link(v.tensor_scalar(q[:, :], rawT[:, :], 0.3, None, ALU.is_gt))
                link(v.tensor_scalar(lt[:, :], rawT[:, :], -0.3, None, ALU.is_lt))
                link(v.tensor_tensor(q[:, :], q[:, :], lt[:, :], ALU.subtract))
                link(v.tensor_tensor(q[:, :], q[:, :], rawT[:, :], ALU.subtract))
                link(v.tensor_tensor(signs, rawT[:, :], q[:, :], ALU.add))
                link(v.tensor_reduce(csum[:, :], signs.rearrange("p (c t) -> p c t", t=TPC), AX.X, ALU.add))
                link(v.tensor_scalar(cneg[:, :], csum[:, :], 0.0, None, ALU.is_lt))
                link(v.tensor_scalar(csum[:, :], csum[:, :], 0.0, None, ALU.is_gt))
                link(v.tensor_tensor(sig[:, 0:CLUSTERS], csum[:, :], cneg[:, :], ALU.subtract))
                dve.wait_ge(loaded.sem, 14 * DMA)
                link(v.tensor_tensor(slope[:, 0:KNOTS - 1], knot[:, 1:KNOTS], knot[:, 0:KNOTS - 1], ALU.subtract))
                link(v.tensor_scalar(nit[:, :], nit[:, :], 1e-6, None, ALU.add))
                link(v.reciprocal(nit[:, :], nit[:, :]))
                link(v.tensor_scalar(nit[:, :], nit[:, :], -1.0, None, ALU.mult))
                dve.wait_ge(iota_made.sem, 1)
                link(v.tensor_copy(iota[:, :, :], iota_i[:, :, :]))

        with nc.Block() as block:

            @block.tensor
            def _(pe):
                mm = nc.tensor.matmul
                with pe.Fori(0, ITER) as i:
                    for u in range(U):
                        pe.wait_ge(xs_ready.sem, xs_ready.after(i, u + 1))
                        pe.wait_ge(sc_kept.sem, sc_kept.free(i, u))
                        for b in range(GB):
                            last = mm(ps_a[u][:, b * NS:(b + 1) * NS], xs[u][:, b * T:(b + 1) * T], sig[:, :], start=True, stop=True)
                        last.then_inc(sc_mm.sem, 1)
                        pe.wait_ge(hid_ready.sem, hid_ready.free(i, u))
                        mm(ps_b[u][0:COMP, :], w1[:, :], xs[u][:, :], start=True, stop=True).then_inc(hid_mm.sem, 1)
                    for u in range(U):
                        pe.wait_ge(hid_ready.sem, hid_ready.after(i, u + 1))
                        pe.wait_ge(comp_kept.sem, comp_kept.free(i, u))
                        for b in range(GB):
                            last = mm(ps_c[u][:, 2 * b:2 * b + 2], hid[u][:, b * T:(b + 1) * T], w2[:, :], start=True, stop=True)
                        last.then_inc(comp_mm.sem, 1)

            @block.scalar
            def _(act):
                f = nc.scalar.activation
                with act.Fori(0, ITER) as i:
                    for u in range(U):
                        act.wait_ge(hid_ready.sem, hid_ready.free(i, u))
                        f(xs[u][:, :], group_of(xT, i, u, U), ACT.Copy).then_inc(xs_ready.sem, 1)
                    for u in range(U):
                        act.wait_ge(hid_mm.sem, hid_mm.after(i, u + 1))
                        act.wait_ge(comp_kept.sem, comp_kept.free(i, u))
                        f(hid[u][:, :], ps_b[u][0:COMP, :], ACT.Gelu, bias=b1[:, :]).then_inc(hid_ready.sem, 1)

            @block.vector
            def _(dve):
                v = nc.vector
                with dve.Fori(0, ITER) as i:
                    for u in range(U):
                        first = i * (U * GB) + u * GB
                        dve.wait_ge(sc_mm.sem, sc_mm.after(i, u + 1))
                        v.tensor_copy(scores[:, bass.ds(first, GB), :], ps_a[u][:, 0:GB * NS].rearrange("p (b n) -> p b n", b=GB)).then_inc(sc_kept.sem, 1)
                    for u in range(U):
                        first = i * (U * GB) + u * GB
                        dve.wait_ge(comp_mm.sem, comp_mm.after(i, u + 1))
                        v.tensor_tensor(comp[:, bass.ds(first, GB), :], ps_c[u][:, 0:GB * 2].rearrange("p (b n) -> p b n", b=GB),
                                        b2[:, :].unsqueeze(1).broadcast_to([P, GB, 2]), ALU.add).then_inc(comp_kept.sem, 1)

        exp_asked = t.count("exp_asked")
        exp_ready = t.count("exp_ready")
        with nc.Block() as block:

            @block.scalar
            def _(act):
                f = nc.scalar.activation
                f(comp[:, :, :], comp[:, :, :], ACT.Tanh)
                e3 = e[:, :].rearrange("p (b n) -> p b n", n=8)
                f(e3, scores[:, :, 0:CLUSTERS], ACT.Exp, scale=nit[:, :]).then_inc(exp_ready.sem, 1)
                act.wait_ge(exp_asked.sem, 1)
                f(e3, mine[:, :, :], ACT.Exp, scale=nit[:, :]).then_inc(exp_ready.sem, 1)

            @block.vector
            def _(dve):
                v = nc.vector
                link = Chain(t, "route", dve)

                def calibrate(n):
                    dve.wait_ge(exp_ready.sem, n)
                    link(v.tensor_scalar(e[:, :], e[:, :], 1.0, None, ALU.add))
                    link(v.reciprocal(e[:, :], e[:, :]))
                    link(v.tensor_scalar(e[:, :], e[:, :], float(KNOTS - 1), None, ALU.mult))
                    link(v.tensor_scalar(low[:, :], e[:, :], 1.0, None, ALU.is_ge))
                    for k in range(2, KNOTS - 1):
                        link(v.scalar_tensor_tensor(low[:, :], e[:, :], float(k), low[:, :], ALU.is_ge, ALU.add))
                    v.tensor_tensor(frac[:, :], e[:, :], low[:, :], ALU.subtract)
                    v.tensor_scalar(gates[:, :], low[:, :], 0.0, knot[:, 0:1], ALU.is_equal, ALU.mult)
                    link(v.tensor_scalar(inc[:, :], low[:, :], 0.0, slope[:, 0:1], ALU.is_equal, ALU.mult))
                    for k in range(1, KNOTS - 1):
                        for acc, of in ((gates, knot), (inc, slope)):
                            link(v.tensor_scalar(term[:, :], low[:, :], float(k), of[:, k:k + 1], ALU.is_equal, ALU.mult))
                            link(v.tensor_tensor(acc[:, :], acc[:, :], term[:, :], ALU.add))
                    link(v.tensor_tensor(inc[:, :], inc[:, :], frac[:, :], ALU.mult))
                    link(v.tensor_tensor(gates[:, :], gates[:, :], inc[:, :], ALU.add))

                g3 = gates[:, :].rearrange("p (b n) -> p b n", n=8)
                calibrate(1)
                first_max_one_hot(link, v, g3, top[:, :], cluster[:, :, :], iota[:, :, :], CLUSTERS)
                link(v.tensor_tensor(picked[:, :, :, :], scores[:, :, CLUSTERS:].rearrange("p b (c j) -> p b c j", c=CLUSTERS),
                                     cluster[:, :, :].unsqueeze(3).broadcast_to([P, B, CLUSTERS, TPC]), ALU.mult))
                v.tensor_reduce(mine[:, :, :], picked[:, :, :, :].rearrange("p b c j -> p b j c"), AX.X, ALU.add).then_inc(exp_asked.sem, 1)
                calibrate(2)
                first_max_one_hot(link, v, g3, top[:, :], local[:, :, :], iota[:, :, :], TPC)

        oh_ready = t.count("oh_ready", U)
        ohT_mm = t.count("ohT_mm", U)
        ohT_ready = t.count("ohT_ready", U)
        row_mm = t.count("row_mm", U)
        mag_steps = 8
        hh = t.count("hh", mag_steps * U)
        ohm_ready = t.count("ohm_ready", U)
        ohmT_mm = t.count("ohmT_mm", U)
        ohmT_ready = t.count("ohmT_ready", U)
        dir_mm = t.count("dir_mm", U)
        xT_ready = [t.count(f"xT_ready{u}", credits=1) for u in range(U)]
        norm = [DoubleNorm(t, const, f"ln{u}", 1, y[u], sq[u], logs[u], inv[u], ps_n[u], gamma_c, beta_c, y_credits=1)
                for u in range(U)]

        ORDER = []
        for front, back in ((["one_hot"], []), (["turn"], ["own_mean"]), (["rows"], ["own_square", "own_variance"]),
                            (["weigh"], ["own_inverse", "gain"]), ([], ["mean"]),
                            (["turn_weighed"], ["square", "variance"]), (["directions"], ["inverse", "divide"]), (["sum"], [])):
            ORDER += [(kind, 1, u) for kind in back for u in range(U)] + [(kind, 0, u) for kind in front for u in range(U)]

        def run(engine, step):
            def peeled(i):
                for kind, lag, u in ORDER:
                    if 0 <= i - lag < ITER:
                        step(kind, i - lag, u)
            peeled(0)
            with engine.Fori(1, ITER) as i:
                for kind, lag, u in ORDER:
                    step(kind, i - lag, u)
            peeled(ITER)

        with nc.Block() as block:

            @block.tensor
            def _(pe):
                mm, turn = nc.tensor.matmul, nc.tensor.transpose

                def step(kind, i, u):
                    if kind == "turn":
                        pe.wait_ge(oh_ready.sem, oh_ready.after(i, u + 1))
                        pe.wait_ge(norm[u].own.y_ready.sem, norm[u].own.y_ready.free(i))
                        for b in range(GB):
                            last = turn(ps_a[u][:, b * T:(b + 1) * T], oh[u][:, b, :], const["ident"][:, :])
                        last.then_inc(ohT_mm.sem, 1)
                    elif kind == "rows":
                        pe.wait_ge(ohT_ready.sem, ohT_ready.after(i, u + 1))
                        for b in range(GB):
                            last = mm(ps_b[u][:, b * TAB:(b + 1) * TAB], ohT[u][:, b * T:(b + 1) * T], table[:, :], start=True, stop=True)
                        last.then_inc(row_mm.sem, 1)
                    elif kind == "turn_weighed":
                        pe.wait_ge(ohm_ready.sem, ohm_ready.after(i, u + 1))
                        for b in range(GB):
                            last = turn(ps_c[u][:, b * T:(b + 1) * T], ohm[u][:, b, :], const["ident"][:, :])
                        last.then_inc(ohmT_mm.sem, 1)
                    elif kind == "directions":
                        pe.wait_ge(ohmT_ready.sem, ohmT_ready.after(i, u + 1))
                        mm(ps_a[u][:, :], dir_sb[:, :], ohmT[u][:, :], start=True, stop=True).then_inc(dir_mm.sem, 1)
                    elif kind == "own_mean":
                        pe.wait_ge(norm[u].stream.log_ready.sem, norm[u].stream.log_ready.free(i))
                        norm[u].own.mean(nc, pe, i, 0)
                    elif kind == "own_variance":
                        norm[u].own.variance(nc, pe, i, 0)
                    elif kind == "mean":
                        norm[u].stream.mean(nc, pe, i, 0)
                    elif kind == "variance":
                        norm[u].stream.variance(nc, pe, i, 0)

                run(pe, step)

            @block.scalar
            def _(act):
                f = nc.scalar.activation
                nc.scalar.preload_act_table_set(LN_EXP)

                def step(kind, i, u):
                    if kind == "turn":
                        act.wait_ge(ohT_mm.sem, ohT_mm.after(i, u + 1))
                        f(ohT[u][:, :], ps_a[u][0:TILES, :], ACT.Copy).then_inc(ohT_ready.sem, 1)
                    elif kind == "turn_weighed":
                        act.wait_ge(ohmT_mm.sem, ohmT_mm.after(i, u + 1))
                        f(ohmT[u][:, :], ps_c[u][0:TILES, :], ACT.Copy).then_inc(ohmT_ready.sem, 1)
                    elif kind == "own_square":
                        norm[u].own.square(nc, act, i, 0)
                    elif kind == "own_inverse":
                        norm[u].own.inverse(nc, act, i, 0)
                    elif kind == "square":
                        norm[u].stream.square(nc, act, i, 0)
                    elif kind == "inverse":
                        norm[u].stream.inverse(nc, act, i, 0)

                run(act, step)

            @block.vector
            def _(dve):
                v = nc.vector
                for u in range(U):
                    norm[u].give(dve)
                    xT_ready[u].give(dve)
                    norm[u].own.y_ready.give(dve)

                def step(kind, i, u):
                    first = i * (U * GB) + u * GB
                    if kind == "one_hot":
                        shape = [P, GB, CLUSTERS, TPC]
                        v.tensor_tensor(oh[u][:, :, 0:TILES].rearrange("p b (c j) -> p b c j", c=CLUSTERS),
                                        cluster[:, bass.ds(first, GB), :].unsqueeze(3).broadcast_to(shape),
                                        local[:, bass.ds(first, GB), :].unsqueeze(2).broadcast_to(shape), ALU.mult).then_inc(oh_ready.sem, 1)
                    elif kind == "weigh":
                        rows = ps_b[u][:, 0:GB * TAB].rearrange("p (b n) -> p b n", b=GB)
                        dve.wait_ge(row_mm.sem, row_mm.after(i, u + 1))
                        done = [u * mag_steps]

                        def link(instruction):
                            instruction.then_inc(hh.sem, 1)
                            done[0] += 1
                            dve.wait_ge(hh.sem, hh.after(i, done[0]))

                        c = lambda n: comp[:, bass.ds(first, GB), n:n + 1].broadcast_to([P, GB, GRID])
                        v.tensor_tensor(ha[:, :, :], rows[:, :, 0:GRID], c(0), ALU.mult)
                        link(v.tensor_tensor(hb[:, :, :], rows[:, :, GRID:2 * GRID], c(1), ALU.mult))
                        link(v.tensor_tensor(ha[:, :, :], ha[:, :, :], hb[:, :, :], ALU.add))
                        link(v.tensor_tensor(ha[:, :, :], ha[:, :, :], rows[:, :, 2 * GRID:3 * GRID], ALU.add))
                        link(v.tensor_scalar(ha[:, :, :], ha[:, :, :], 0.0, None, ALU.max))
                        link(v.tensor_tensor(ha[:, :, :], ha[:, :, :], rows[:, :, 3 * GRID:4 * GRID], ALU.mult))
                        link(v.tensor_reduce(mag[:, :], ha[:, :, :], AX.X, ALU.add))
                        link(v.tensor_tensor(mag[:, :], mag[:, :], rows[:, :, 4 * GRID:TAB].rearrange("p b a -> p (b a)"), ALU.add))
                        link(v.tensor_scalar(mag[:, :], mag[:, :], scale_c[:, 0:1], None, ALU.mult))
                        v.tensor_tensor(ohm[u][:, :, 0:TILES], oh[u][:, :, 0:TILES], mag[:, :].unsqueeze(2).broadcast_to([P, GB, TILES]), ALU.mult).then_inc(ohm_ready.sem, 1)
                    elif kind == "sum":
                        dve.wait_ge(dir_mm.sem, dir_mm.after(i, u + 1))
                        dve.wait_ge(xT_ready[u].sem, xT_ready[u].free(i))
                        v.tensor_tensor(y[u][:, :], ps_a[u][:, :], group_of(xT, i, u, U), ALU.add).then_inc(norm[u].own.y_ready.sem, 1)
                    elif kind == "own_mean":
                        norm[u].own.centre(nc, dve, i, 0)
                    elif kind == "gain":
                        norm[u].gain(nc, dve, i, 0, group_of(xT, i, u, U))
                    elif kind == "mean":
                        norm[u].stream.centre(nc, dve, i, 0)
                    elif kind == "divide":
                        norm[u].stream.divide(nc, dve, i, 0, group_of(xT, i, u, U), xT_ready[u])

                run(dve, step)
        t.clear_counts()


HD = 64
INNER = H * HD
PAIRS = H // 2
HALF = 4


def self_attention(nc, const, xT, scale, wq, bq, wk, bk, wv, bv, wo, bo, gamma, beta):
    with ExitStack() as ctx:
        t = Tools(ctx, nc, "self")
        HALVES = GB * 2
        w = {n: t.sb(f"w_{n}", [P, INNER]) for n in "qkvo"}
        bq_c, bk_c, sc_c = t.sb("bq", [P, PAIRS]), t.sb("bk", [P, PAIRS]), t.sb("scale", [P, PAIRS])
        bo_c, gamma_c, beta_c = t.sb("bo", [P, 1]), t.sb("gamma", [P, 1]), t.sb("beta", [P, 1])
        bv_row = t.sb("bv_row", [P, INNER])
        xs = t.sb("xs", [P, GROUP])
        qT, kT = t.sb("qT", [P, PAIRS, GROUP]), t.sb("kT", [P, PAIRS, GROUP])
        vs = t.sb("v", [P, GB, INNER])
        neg = [t.sb(f"neg{r}", [P, 2, HALF]) for r in range(2)]
        probs = [t.sb(f"probs{r}", [P, 2, HALF, T]) for r in range(2)]
        z = [t.sb(f"z{r}", [P, 2, HALF]) for r in range(2)]
        rz = [t.sb(f"rz{r}", [P, 2, HALF]) for r in range(2)]
        pt = [t.sb(f"pt{r}", [P, 2, HALF, T]) for r in range(2)]
        o = [t.sb(f"o{r}", [P, HALF, 2, HD]) for r in range(2)]
        oT = t.sb("oT", [P, PAIRS, GROUP])
        y, sq = t.sb("y", [P, GROUP]), t.sb("sq", [P, GROUP])
        logs, inv = t.sb("logs", [P, GROUP]), t.sb("inv", [P, GROUP])
        ps_s = [t.ps(f"scores{r}", [P, 2, 512]) for r in range(2)]
        ps_t = [t.ps(f"turned{r}", [P, 512]) for r in range(2)]
        ps_o = t.ps("out", [P, 512])
        ps_n = t.ps("norm", [P, 512])

        load_transposed(nc, const, "self_w", [(w[n][:, :], a) for n, a in zip("qkvo", (wq, wk, wv, wo))], ps_t)
        loaded = t.count("loaded", weight=DMA)
        scaled = t.count("scaled")
        with nc.Block() as block:

            @block.sync
            def _(sp):
                cols = lambda a: a.rearrange("(n p) -> p n", p=P)
                loads = [(bq_c[:, :], cols(bq)), (bk_c[:, :], cols(bk)), (bo_c[:, :], cols(bo)), (gamma_c[:, :], cols(gamma)),
                         (beta_c[:, :], cols(beta)), (bv_row[:, :], bv.partition_broadcast(P)),
                         (sc_c[0:HD, :], scale.rearrange("(c a) -> a c", a=2)[0:1, :].broadcast_to([HD, PAIRS])),
                         (sc_c[HD:P, :], scale.rearrange("(c a) -> a c", a=2)[1:2, :].broadcast_to([HD, PAIRS]))]
                for dst, src in loads:
                    sp.dma_start(dst, src, allow_slow_non_contiguous=True).then_inc(loaded.sem, DMA)

            @block.vector
            def _(dve):
                dve.wait_ge(loaded.sem, 8 * DMA)
                nc.vector.tensor_scalar(sc_c[:, :], sc_c[:, :], HD ** -0.5, None, ALU.mult).then_inc(scaled.sem, 1)
                dve.wait_ge(scaled.sem, 1)
                nc.vector.tensor_tensor(bq_c[:, :], bq_c[:, :], sc_c[:, :], ALU.mult)

        xs_ready = t.count("xs_ready")
        qk_mm = [t.count(f"qk_mm{r}", PAIRS) for r in range(2)]
        qk_ready = [t.count(f"qk_ready{r}", PAIRS) for r in range(2)]
        turned = [t.count(f"turned{r}", HALVES, credits=2) for r in range(2)]
        pt_ready = [t.count(f"pt_ready{r}", HALVES) for r in range(2)]
        v_mm = t.count("v_mm", GB, credits=1)
        v_ready = t.count("v_ready", GB)
        s_mm = t.count("s_mm", HALVES, credits=1)
        max_ready = t.count("max_ready", HALVES)
        neg_ready = t.count("neg_ready", HALVES)
        p_ready = t.count("p_ready", HALVES, credits=2)
        pv_mm = t.count("pv_mm", HALVES, credits=2)
        rz_ready = t.count("rz_ready", HALVES, credits=2)
        o_ready = t.count("o_ready", HALVES)
        ot_mm = t.count("ot_mm", HALVES, credits=2)
        ot_ready = t.count("ot_ready", HALVES, credits=1)
        wo_mm = t.count("wo_mm")
        xT_ready = t.count("xT_ready")
        norm = DoubleNorm(t, const, "ln", 1, y, sq, logs, inv, ps_n, gamma_c, beta_c)

        def scored(lag, k):
            return [("scores_a", lag, k), ("scores_b", lag, k)]

        NORM_TENSOR = {0: [("own_mean", 1, 0)], 1: [("own_variance", 1, 0)], 3: [("mean", 1, 0)], 4: [("variance", 1, 0)]}
        NORM_SCALAR = {1: [("own_square", 1, 0)], 2: [("own_inverse", 1, 0)], 4: [("square", 1, 0)], 5: [("inverse", 1, 0)]}
        NORM_VECTOR = {0: [("own_centre", 1, 0)], 2: [("gain", 1, 0)], 3: [("centre", 1, 0)], 5: [("divide", 1, 0)]}
        ORDER = []
        for k in range(HALVES):
            ORDER.append(("turn", 0, k))
            ORDER += NORM_SCALAR.get(k, [])
            ahead = scored(0, k + 2) if k + 2 < HALVES else []
            ORDER += ahead[:1] + ([("collect", 0, k - 1)] if k else []) + ahead[1:]
            if k == 5:
                ORDER.append(("stream", -1, 0))
            if k >= 6:
                ORDER += [("project", -1, n) for n in range((k - 6) * PAIRS, (k - 5) * PAIRS)]
            ORDER += NORM_TENSOR.get(k, []) + [("attend", 0, k)] + NORM_VECTOR.get(k, [])
        ORDER += [("values", -1, 0), ("collect", 0, HALVES - 1)] + [("values", -1, c) for c in range(1, GB)]
        ORDER += scored(-1, 0) + [("mix", 0, 0)] + scored(-1, 1)
        LOOP = (1, NG - 1)

        def run(engine, step):
            def peeled(g):
                for kind, lag, k in ORDER:
                    if 0 <= g - lag < NG:
                        step(kind, g - lag, k)
            for g in range(-1, LOOP[0]):
                peeled(g)
            with engine.Fori(*LOOP) as g:
                for kind, lag, k in ORDER:
                    step(kind, g - lag, k)
            for g in range(LOOP[1], NG + 1):
                peeled(g)

        def proj_bank(k):
            return (*ps_t, ps_n)[k % 3]

        def at(i, where):
            return isinstance(i, int) and i == where

        with nc.Block() as block:

            @block.tensor
            def _(pe):
                mm, turn = nc.tensor.matmul, nc.tensor.transpose
                ident = const["ident"]

                def step(kind, i, k):
                    b, half = k // 2, k % 2
                    if kind == "project":
                        if k == 0:
                            pe.wait_ge(xs_ready.sem, xs_ready.after(i))
                        if k >= 3:
                            pe.wait_ge(qk_ready[(k - 3) % 2].sem, qk_ready[(k - 3) % 2].after(i, (k - 3) // 2 + 1))
                        if k in (0, 1) and not at(i, 0):
                            pe.wait_ge(pt_ready[k].sem, pt_ready[k].after(i - 1, HALVES - 1))
                        elif k == 2 and not at(i, 0):
                            pe.wait_ge(norm.stream.log_ready.sem, norm.stream.log_ready.after(i - 2))
                        elif k in (PAIRS + 1, PAIRS + 2) and not at(i, 0):
                            pe.wait_ge(pt_ready[k - PAIRS - 1].sem, pt_ready[k - PAIRS - 1].after(i - 1, HALVES))
                        wt = w["q" if k < PAIRS else "k"]
                        c = k % PAIRS
                        mm(proj_bank(k)[:, :], wt[:, c * P:(c + 1) * P], xs[:, :], start=True, stop=True).then_inc(qk_mm[k % 2].sem, 1)
                    elif kind == "values":
                        if k < 2:
                            pe.wait_ge(p_ready.sem, p_ready.free(i, k))
                        else:
                            pe.wait_ge(v_ready.sem, v_ready.after(i, k - 1))
                        for j in range(2):
                            last = mm(ps_s[k % 2][:, j, :], xs[:, k * T:(k + 1) * T], w["v"][:, j * 512:(j + 1) * 512], start=True, stop=True)
                        last.then_inc(v_mm.sem, 1)
                    elif kind in ("scores_a", "scores_b"):
                        part = kind == "scores_b"
                        if part == 0 and k < 2:
                            pe.wait_ge(v_ready.sem, v_ready.after(i, GB - 1 + k))
                            if k == 0:
                                for r in range(2):
                                    pe.wait_ge(qk_ready[r].sem, qk_ready[r].after(i, PAIRS))
                        elif part == 0:
                            pe.wait_ge(p_ready.sem, p_ready.free(i, k))
                        for j in range(part * 2, part * 2 + 2):
                            c = half * HALF + j
                            for e in range(2):
                                rows = slice(e * HD, (e + 1) * HD)
                                last = mm(ps_s[k % 2][:, e, j * T:(j + 1) * T], qT[rows, c, b * T:(b + 1) * T],
                                          kT[rows, c, b * T:(b + 1) * T], start=True, stop=True)
                        if part:
                            last.then_inc(s_mm.sem, 1)
                    elif kind == "turn":
                        pe.wait_ge(p_ready.sem, p_ready.after(i, k + 1))
                        for e in range(2):
                            if k:
                                pe.wait_ge(pt_ready[e].sem, pt_ready[e].after(i, k))
                            else:
                                pe.wait_ge(qk_ready[e].sem, qk_ready[e].after(i, PAIRS))
                            if k == HALVES - 1 and not at(i, NG - 1):
                                pe.wait_ge(qk_ready[e].sem, qk_ready[e].after(i + 1, PAIRS // 2))
                            for j in range(HALF):
                                last = turn(ps_t[e][:, j * T:(j + 1) * T], probs[k % 2][:, e, j, :], ident[:, :])
                            last.then_inc(turned[e].sem, 1)
                    elif kind == "attend":
                        for e in range(2):
                            pe.wait_ge(pt_ready[e].sem, pt_ready[e].after(i, k + 1))
                        pe.wait_ge(ot_ready.sem, ot_ready.free(i, k))
                        for j in range(HALF):
                            for e in range(2):
                                head = 2 * (half * HALF + j) + e
                                last = mm(ps_o[:, (2 * j + e) * HD:(2 * j + e + 1) * HD], pt[k % 2][:, e, j, :],
                                          vs[:, b, head * HD:(head + 1) * HD], start=True, stop=True)
                        last.then_inc(pv_mm.sem, 1)
                    elif kind == "collect":
                        pe.wait_ge(o_ready.sem, o_ready.after(i, k + 1))
                        for j in range(HALF):
                            last = turn(ps_o[:, j * T:(j + 1) * T], o[k % 2][:, j, :, :].rearrange("p e d -> p (e d)"), ident[:, :])
                        last.then_inc(ot_mm.sem, 1)
                    elif kind == "mix":
                        pe.wait_ge(ot_ready.sem, ot_ready.after(i, HALVES))
                        pe.wait_ge(norm.stream.log_ready.sem, norm.stream.log_ready.free(i))
                        for c in range(PAIRS):
                            last = mm(ps_n[:, :], w["o"][:, c * P:(c + 1) * P], oT[:, c, :], start=(c == 0), stop=(c == PAIRS - 1))
                        last.then_inc(wo_mm.sem, 1)
                    elif kind == "own_mean":
                        norm.own.mean(nc, pe, i, 0)
                    elif kind == "own_variance":
                        norm.own.variance(nc, pe, i, 0)
                    elif kind == "mean":
                        norm.stream.mean(nc, pe, i, 0)
                    elif kind == "variance":
                        norm.stream.variance(nc, pe, i, 0)

                run(pe, step)

            @block.scalar
            def _(act):
                f = nc.scalar.activation
                nc.scalar.preload_act_table_set(LN_EXP)

                def step(kind, i, k):
                    if kind == "stream":
                        act.wait_ge(v_mm.sem, v_mm.after(i, 0))
                        f(xs[:, :], group_of(xT, i, 0, 1), ACT.Copy).then_inc(xs_ready.sem, 1)
                    elif kind == "project" and k % 2 == 0:
                        c = k % PAIRS
                        if k == 0:
                            act.wait_ge(s_mm.sem, s_mm.after(i, 0))
                        act.wait_ge(qk_mm[0].sem, qk_mm[0].after(i, k // 2 + 1))
                        if k < PAIRS:
                            f(qT[:, c, :], proj_bank(k)[:, :], ACT.Identity, bias=bq_c[:, c:c + 1], scale=sc_c[:, c:c + 1]).then_inc(qk_ready[0].sem, 1)
                        else:
                            f(kT[:, c, :], proj_bank(k)[:, :], ACT.Identity, bias=bk_c[:, c:c + 1]).then_inc(qk_ready[0].sem, 1)
                    elif kind == "scores_b":
                        for e in range(2):
                            act.wait_ge(turned[e].sem, turned[e].after(i, k - 1))
                        act.wait_ge(rz_ready.sem, rz_ready.after(i, k - 1))
                        act.wait_ge(neg_ready.sem, neg_ready.after(i, k + 1))
                        for e in range(2):
                            for j in range(HALF):
                                last = f(probs[k % 2][:, e, j, :], ps_s[k % 2][:, e, j * T:(j + 1) * T], ACT.Exp,
                                         bias=neg[k % 2][:, e, j:j + 1], accum_out=z[k % 2][:, e, j:j + 1])
                        last.then_inc(p_ready.sem, 1)
                    elif kind == "own_square":
                        norm.own.square(nc, act, i, 0)
                    elif kind == "own_inverse":
                        norm.own.inverse(nc, act, i, 0)
                    elif kind == "square":
                        norm.stream.square(nc, act, i, 0)
                    elif kind == "inverse":
                        norm.stream.inverse(nc, act, i, 0)

                run(act, step)

            @block.vector
            def _(dve):
                v = nc.vector
                for c in (*turned, v_mm, s_mm, p_ready, pv_mm, rz_ready, ot_mm, ot_ready, norm):
                    c.give(dve)

                def step(kind, i, k):
                    b, half = k // 2, k % 2
                    if kind == "project" and k % 2:
                        c = k % PAIRS
                        if k == 1:
                            dve.wait_ge(s_mm.sem, s_mm.after(i, 0))
                        dve.wait_ge(qk_mm[1].sem, qk_mm[1].after(i, k // 2 + 1))
                        if k < PAIRS:
                            v.tensor_scalar(qT[:, c, :], proj_bank(k)[:, :], sc_c[:, c:c + 1], bq_c[:, c:c + 1], ALU.mult, ALU.add).then_inc(qk_ready[1].sem, 1)
                        else:
                            v.tensor_scalar(kT[:, c, :], proj_bank(k)[:, :], bk_c[:, c:c + 1], None, ALU.add).then_inc(qk_ready[1].sem, 1)
                    elif kind == "values":
                        if k == 0:
                            dve.wait_ge(pv_mm.sem, pv_mm.after(i, 0))
                        dve.wait_ge(v_mm.sem, v_mm.after(i, k + 1))
                        v.tensor_tensor(vs[:, k, :], ps_s[k % 2][:, :, :].rearrange("p j n -> p (j n)"), bv_row[:, :], ALU.add).then_inc(v_ready.sem, 1)
                    elif kind == "scores_b":
                        dve.wait_ge(s_mm.sem, s_mm.after(i, k + 1))
                        v.tensor_reduce(neg[k % 2][:, :, :], ps_s[k % 2][:, :, :].rearrange("p e (j t) -> p e j t", t=T), AX.X, ALU.max).then_inc(max_ready.sem, 1)
                        dve.wait_ge(max_ready.sem, max_ready.after(i, k + 1))
                        v.tensor_scalar(neg[k % 2][:, :, :], neg[k % 2][:, :, :], -1.0, None, ALU.mult).then_inc(neg_ready.sem, 1)
                    elif kind == "turn":
                        dve.wait_ge(p_ready.sem, p_ready.after(i, k + 1))
                        v.reciprocal(rz[k % 2][:, :, :], z[k % 2][:, :, :]).then_inc(rz_ready.sem, 1)
                        dve.wait_ge(pv_mm.sem, pv_mm.after(i, k - 1))
                        for e in range(2):
                            dve.wait_ge(turned[e].sem, turned[e].after(i, k + 1))
                            v.tensor_copy(pt[k % 2][:, e, :, :].rearrange("p j t -> p (j t)"), ps_t[e][:, :]).then_inc(pt_ready[e].sem, 1)
                    elif kind == "attend":
                        dve.wait_ge(rz_ready.sem, rz_ready.after(i, k + 1))
                        dve.wait_ge(pv_mm.sem, pv_mm.after(i, k + 1))
                        dve.wait_ge(ot_mm.sem, ot_mm.after(i, k - 1))
                        v.tensor_tensor(o[k % 2][:, :, :, :], ps_o[:, :].rearrange("p (j e d) -> p j e d", e=2, d=HD),
                                        rz[k % 2][:, :, :].rearrange("p e j -> p j e").unsqueeze(3).broadcast_to([P, HALF, 2, HD]),
                                        ALU.mult).then_inc(o_ready.sem, 1)
                    elif kind == "collect":
                        dve.wait_ge(ot_mm.sem, ot_mm.after(i, k + 1))
                        v.tensor_copy(oT[:, half * HALF:(half + 1) * HALF, b * T:(b + 1) * T],
                                      ps_o[:, :].rearrange("p (j t) -> p j t", t=T)).then_inc(ot_ready.sem, 1)
                    elif kind == "mix":
                        dve.wait_ge(wo_mm.sem, wo_mm.after(i))
                        v.scalar_tensor_tensor(y[:, :], ps_n[:, :], bo_c[:, 0:1], group_of(xT, i, 0, 1), ALU.add, ALU.add).then_inc(norm.own.y_ready.sem, 1)
                    elif kind == "own_centre":
                        norm.own.centre(nc, dve, i, 0)
                    elif kind == "gain":
                        norm.gain(nc, dve, i, 0, group_of(xT, i, 0, 1))
                    elif kind == "centre":
                        norm.stream.centre(nc, dve, i, 0)
                    elif kind == "divide":
                        norm.stream.divide(nc, dve, i, 0, group_of(xT, i, 0, 1), xT_ready)

                run(dve, step)
        t.clear_counts()


EXPERTS, CAPACITY = 8, 100


def moe_ffn(nc, const, xT, w_gate, w_expert, b_expert, out):
    with ExitStack() as ctx:
        t = Tools(ctx, nc, "moe")
        U = 2
        ITER = NG // U
        NE = B * EXPERTS
        wg = t.sb("wg", [P, EXPERTS])
        we = t.sb("we", [P, D])
        be_row = t.sb("be_row", [P, D])
        iota_i = t.sb("iota_i", [P, B, EXPERTS], I32)
        iota = t.sb("iota", [P, B, EXPERTS])
        upto = t.sb("upto", [P, P])
        carry = t.sb("carry", [P, EXPERTS, B])
        logits = t.sb("logits", [P, B, EXPERTS])
        expert = t.sb("expert", [P, B, D])
        xtok = t.sb("xtok", [P, B, D])
        xs = [t.sb(f"xs{u}", [P, GROUP]) for u in range(U)]
        top = t.sb("top", [P, B])
        gate = t.sb("gate", [P, B])
        probs = t.sb("probs", [P, B, EXPERTS])
        best = t.sb("best", [P, B, EXPERTS])
        total = t.sb("total", [P, EXPERTS, B])
        before = t.sb("before", [P, EXPERTS, B])
        place = t.sb("place", [P, B, EXPERTS])
        yt = [t.sb(f"yt{u}", [P, GB, D]) for u in range(U)]
        stats = [t.sb(f"stats{u}", [P, GB, 6]) for u in range(U)]
        pad = t.sb("pad", [P, 1])
        mv = [t.sb(f"mv{u}", [P, GB, 2]) for u in range(U)]
        logs = [t.sb(f"logs{u}", [P, GB]) for u in range(U)]
        inv = [t.sb(f"inv{u}", [P, GB]) for u in range(U)]
        res = [t.sb(f"res{u}", [P, GB, D]) for u in range(U)]
        ps_e = [t.ps(f"bank_e{u}", [P, 512]) for u in range(U)]
        ps_g = [t.ps(f"bank_g{u}", [P, 512]) for u in range(U)]
        ps_x = [t.ps(f"bank_x{u}", [P, 512]) for u in range(U)]
        ps_c = t.ps("cum", [P, NE])
        ps_t = t.ps("tot", [P, NE])

        loaded = t.count("loaded", weight=DMA)
        made = t.count("made")
        xs_ready = t.count("xs_ready", U)
        e_mm, e_kept = t.count("e_mm", U), t.count("e_kept", U, credits=U)
        g_mm, g_kept = t.count("g_mm", U), t.count("g_kept", U, credits=U)
        x_mm, x_kept = t.count("x_mm", U, credits=U), t.count("x_kept", U, credits=U)
        with nc.Block() as block:

            @block.sync
            def _(sp):
                for dst, src in ((wg[:, :], w_gate), (we[:, :], w_expert), (be_row[:, :], b_expert.partition_broadcast(P))):
                    sp.dma_start(dst, src).then_inc(loaded.sem, DMA)

            @block.gpsimd
            def _(pool):
                pool.iota(iota_i[:, :, :], pattern=[[0, B], [1, EXPERTS]], base=0, channel_multiplier=0).then_inc(made.sem, 1)
                pool.memset(upto[:, :], 1.0).then_inc(made.sem, 1)
                pool.memset(carry[:, :, :], 1.0).then_inc(made.sem, 1)
                pool.wait_ge(made.sem, 3)
                pool.affine_select(out=upto[:, :], in_=upto[:, :], compare_op=ALU.is_ge, fill=0.0, base=0,
                                   pattern=[[1, P]], channel_multiplier=-1)
                pool.memset(carry[:, :, 0:1], 0.0)

            @block.vector
            def _(dve):
                for c in (e_kept, g_kept, x_mm, x_kept):
                    c.give(dve)
                dve.wait_ge(made.sem, 1)
                nc.vector.tensor_copy(iota[:, :, :], iota_i[:, :, :])
                dve.wait_ge(loaded.sem, 3 * DMA)

        with nc.Block() as block:

            @block.tensor
            def _(pe):
                mm, turn = nc.tensor.matmul, nc.tensor.transpose
                with pe.Fori(0, ITER) as i:
                    for u in range(U):
                        tok = lambda b: xs[u][:, b * T:(b + 1) * T]
                        pe.wait_ge(xs_ready.sem, xs_ready.after(i, u + 1))
                        pe.wait_ge(g_kept.sem, g_kept.free(i, u))
                        for b in range(GB):
                            last = mm(ps_g[u][:, b * EXPERTS:(b + 1) * EXPERTS], tok(b), wg[:, :], start=True, stop=True)
                        last.then_inc(g_mm.sem, 1)
                        pe.wait_ge(e_kept.sem, e_kept.free(i, u))
                        for b in range(GB):
                            last = mm(ps_e[u][:, b * D:(b + 1) * D], tok(b), we[:, :], start=True, stop=True)
                        last.then_inc(e_mm.sem, 1)
                        pe.wait_ge(x_kept.sem, x_kept.free(i, u))
                        for b in range(GB):
                            last = turn(ps_x[u][:, b * D:(b + 1) * D], tok(b), const["ident"][:, :])
                        last.then_inc(x_mm.sem, 1)

            @block.scalar
            def _(act):
                f = nc.scalar.activation
                with act.Fori(0, ITER) as i:
                    for u in range(U):
                        act.wait_ge(x_mm.sem, x_mm.free(i, u))
                        f(xs[u][:, :], group_of(xT, i, u, U), ACT.Copy).then_inc(xs_ready.sem, 1)
                    for u in range(U):
                        first = i * (U * GB) + u * GB
                        act.wait_ge(x_mm.sem, x_mm.after(i, u + 1))
                        f(xtok[:, bass.ds(first, GB), :], ps_x[u][:, :].rearrange("p (b d) -> p b d", d=D), ACT.Copy).then_inc(x_kept.sem, 1)

            @block.vector
            def _(dve):
                v = nc.vector
                with dve.Fori(0, ITER) as i:
                    for u in range(U):
                        first = i * (U * GB) + u * GB
                        dve.wait_ge(g_mm.sem, g_mm.after(i, u + 1))
                        v.tensor_copy(logits[:, bass.ds(first, GB), :], ps_g[u][:, 0:GB * EXPERTS].rearrange("p (b n) -> p b n", b=GB)).then_inc(g_kept.sem, 1)
                        dve.wait_ge(e_mm.sem, e_mm.after(i, u + 1))
                        v.tensor_tensor(expert[:, bass.ds(first, GB), :], ps_e[u][:, :].rearrange("p (b d) -> p b d", d=D),
                                        be_row[:, :].unsqueeze(1).broadcast_to([P, GB, D]), ALU.add).then_inc(e_kept.sem, 1)

        dist_ready = t.count("dist_ready")
        exp_ready = t.count("exp_ready")
        best_ready = t.count("best_ready")
        places_mm = t.count("places_mm")
        with nc.Block() as block:

            @block.scalar
            def _(act):
                act.wait_ge(dist_ready.sem, 1)
                nc.scalar.activation(probs[:, :, :], probs[:, :, :], ACT.Exp).then_inc(exp_ready.sem, 1)

            @block.tensor
            def _(pe):
                pe.wait_ge(best_ready.sem, 1)
                flat = best[:, :, :].rearrange("p b e -> p (b e)")
                nc.tensor.matmul(ps_c[:, :], upto[:, :], flat, start=True, stop=True)
                nc.tensor.matmul(ps_t[:, :], const["ones"][:, :], flat, start=True, stop=True).then_inc(places_mm.sem, 1)

            @block.vector
            def _(dve):
                v = nc.vector
                link = Chain(t, "route", dve)
                wide = lambda a: a[:, :].unsqueeze(2).broadcast_to([P, B, EXPERTS])
                by_seq = lambda a: a[:, :, :].rearrange("p e b -> p b e")
                link(v.tensor_reduce(top[:, :], logits[:, :, :], AX.X, ALU.max))
                v.tensor_tensor(probs[:, :, :], logits[:, :, :], wide(top), ALU.subtract).then_inc(dist_ready.sem, 1)
                dve.wait_ge(exp_ready.sem, 1)
                link(v.tensor_reduce(top[:, :], probs[:, :, :], AX.X, ALU.add))
                link(v.reciprocal(top[:, :], top[:, :]))
                link(v.tensor_tensor(probs[:, :, :], probs[:, :, :], wide(top), ALU.mult))
                link(v.tensor_reduce(gate[:, :], probs[:, :, :], AX.X, ALU.max))
                first_max_one_hot(link, v, probs[:, :, :], top[:, :], best[:, :, :], iota[:, :, :], EXPERTS)
                dve.sem_inc(best_ready.sem, 1)
                dve.wait_ge(places_mm.sem, 1)
                link(v.tensor_copy(by_seq(total), ps_t[:, :].rearrange("p (b e) -> p b e", e=EXPERTS)))
                flat = lambda a: a[:, :, :].rearrange("p e b -> p (e b)")
                link(v.tensor_tensor_scan(flat(before), flat(carry), flat(total), 0.0, ALU.mult, ALU.add))
                link(v.tensor_tensor(before[:, :, :], before[:, :, :], total[:, :, :], ALU.subtract))
                link(v.tensor_tensor(place[:, :, :], ps_c[:, :].rearrange("p (b e) -> p b e", e=EXPERTS), by_seq(before), ALU.add))
                link(v.scalar_tensor_tensor(place[:, :, :], place[:, :, :], float(CAPACITY), best[:, :, :], ALU.is_le, ALU.mult))
                link(v.tensor_reduce(top[:, :], place[:, :, :], AX.X, ALU.add))
                link(v.tensor_tensor(gate[:, :], gate[:, :], top[:, :], ALU.mult))

        y_ready = t.count("y_ready", U)
        part = t.count("part", U)
        stats_ready = t.count("stats_ready", U)
        mv_ready = t.count("mv_ready", U)
        log_ready = t.count("log_ready", U)
        inv_ready = t.count("inv_ready", U)
        res_ready = t.count("res_ready", U, credits=U)
        stored = [t.count(f"stored{u}", 1, DMA, credits=1) for u in range(U)]
        with nc.Block() as block:

            @block.sync
            def _(sp):
                with sp.Fori(0, ITER) as i:
                    for u in range(U):
                        sp.wait_ge(res_ready.sem, res_ready.after(i, u + 1))
                        dst = out[bass.ds(i * (U * GB) + u * GB, GB)].rearrange("b t d -> t b d")
                        sp.dma_start(dst, res[u][:, :, :]).then_inc(stored[u].sem, DMA)
                for u in range(U):
                    sp.wait_ge(stored[u].sem, (ITER + 1) * DMA)

            @block.scalar
            def _(act):
                f = nc.scalar.activation
                with act.Fori(0, ITER) as i:
                    for u in range(U):
                        nc.scalar.preload_act_table_set("natural_log_exp_and_others")
                        act.wait_ge(mv_ready.sem, mv_ready.after(i, u + 1))
                        f(logs[u][:, :], mv[u][:, :, 1:2].rearrange("p b a -> p (b a)"), ACT.Ln, bias=const["eps"][:, :]).then_inc(log_ready.sem, 1)
                        act.wait_ge(log_ready.sem, log_ready.after(i, u + 1))
                        f(inv[u][:, :], logs[u][:, :], ACT.Exp, scale=-0.5).then_inc(inv_ready.sem, 1)

            @block.vector
            def _(dve):
                v = nc.vector
                for u in range(U):
                    stored[u].give(dve)
                res_ready.give(dve)
                with dve.Fori(0, ITER) as i:
                    for u in range(U):
                        first = i * (U * GB) + u * GB
                        dve.wait_ge(res_ready.sem, res_ready.free(i, u))
                        v.tensor_tensor(yt[u][:, :, :], expert[:, bass.ds(first, GB), :],
                                        gate[:, bass.ds(first, GB)].unsqueeze(2).broadcast_to([P, GB, D]), ALU.mult).then_inc(part.sem, 1)
                        dve.wait_ge(part.sem, part.after(i, u + 1))
                        v.tensor_tensor(yt[u][:, :, :], yt[u][:, :, :], xtok[:, bass.ds(first, GB), :], ALU.add).then_inc(y_ready.sem, 1)
                        dve.wait_ge(y_ready.sem, y_ready.after(i, u + 1))
                        for b in range(GB):
                            last = v.bn_stats(stats[u][:, b, :], yt[u][:, b, :])
                        last.then_inc(stats_ready.sem, 1)
                        dve.wait_ge(stats_ready.sem, stats_ready.after(i, u + 1))
                        v.memset(pad[:, :], 0.0)
                        for b in range(GB):
                            last = v.bn_aggr(mv[u][:, b, :], stats[u][:, b, :])
                        last.then_inc(mv_ready.sem, 1)
                    for u in range(U):
                        dve.wait_ge(inv_ready.sem, inv_ready.after(i, u + 1))
                        dve.wait_ge(stored[u].sem, stored[u].free(i))
                        for b in range(GB):
                            last = v.tensor_scalar(res[u][:, b, :], yt[u][:, b, :], mv[u][:, b, 0:1], inv[u][:, b:b + 1], ALU.subtract, ALU.mult)
                        last.then_inc(res_ready.sem, 1)
        t.clear_counts()


def program(nc, a, out):
    def of(prefix, *names):
        return [a[f"{prefix}_{n}"] for n in names]

    with ExitStack() as ctx:
        xT = ctx.enter_context(nc.sbuf_tensor("xT", [P, NT], F32))
        const = constants(nc, ctx)
        min_gru(nc, const, xT, a["x"], *of("L0_attn", "Wp", "bp", "g1", "Whg", "bhg", "Wo", "bo", "g2", "gf", "Wf", "bf"))
        cross_attention(nc, const, "x0", xT, a["ctx_1024"], *of("L0_xattn", "Wq", "bq", "Wk", "bk", "Wv", "bv", "Wo", "bo"), turn=True,
                        temper=of("L0_xattn", "w1", "b1", "w2", "b2", "w3", "b3"))
        tile_ffn(nc, const, xT, *of("L0_ffn", "signatures_raw", "knot_values", "temperature", "compress_w1", "compress_b1",
                                    "compress_w2", "compress_b2", "spline_w1", "spline_b1", "spline_w2", "spline_b2",
                                    "directions", "norm_gamma", "norm_beta", "output_scale"))
        self_attention(nc, const, xT, *of("L1_attn", "adaptive_scale", "Wq", "bq", "Wk", "bk", "Wv", "bv", "Wo", "bo", "gamma", "beta"))
        cross_attention(nc, const, "x1", xT, a["ctx_1024"], *of("L1_xattn", "W_Q", "b_Q", "W_K", "b_K", "W_V", "b_V", "W_O", "b_O"), turn=False)
        moe_ffn(nc, const, xT, *of("L1_ffn", "w_gate", "w_expert", "b_expert"), out)


def kernel(**inputs):
    import concourse.bacc as _bacc
    from concourse.bass_utils import run_bass_kernel_spmd as _run

    nc = _bacc.Bacc("TRN2", target_bir_lowering=False, num_devices=1)
    arrays, aps = {}, {}
    for name, value in inputs.items():
        value = np.ascontiguousarray(value)
        arrays[f"in_{name}"] = value
        aps[name] = nc.dram_tensor(f"in_{name}", value.shape, mybir.dt.from_np(value.dtype), kind="ExternalInput").ap()
    out = nc.dram_tensor("out", (B, T, D), F32, kind="ExternalOutput").ap()
    program(nc, aps, out)
    r = _run(nc, [arrays], core_ids=[0])
    return r.results[0]["out"]
```
